# Optimizing a Trainium2 kernel written in Bass

```python
import numpy as np
import jax
import jax.numpy as jnp

def _softmax(x, axis=-1):
    return jax.nn.softmax(x, axis=axis)

def _gelu(x):
    return jax.nn.gelu(x, approximate=True)

def _silu(x):
    return jax.nn.silu(x)

def _sigmoid(x):
    return jax.nn.sigmoid(x)

def _layernorm(x, axis=-1, eps=1e-05):
    m = jnp.mean(x, axis=axis, keepdims=True)
    v = jnp.var(x, axis=axis, keepdims=True)
    return (x - m) / jnp.sqrt(v + eps)

def _scatter_add(tgt, idx, src, axis=0):
    return tgt.at[idx].add(src)

def _segment_sum(src, seg, n):
    return jax.ops.segment_sum(src, seg, n)
kernel_name = 'mk_seq_preln_d1_jaxref_r8_5037b3'

def setup_inputs(seed: int=0):
    np.random.seed(seed)
    _w = jnp.asarray

    def _L0_attn_setup():
        import jax, jax.numpy as jnp
        import numpy as np
        import math
        D_MODEL = 128
        N_HEADS = 16
        HEAD_DIM = D_MODEL // N_HEADS
        FEAT = 16
        WINDOW = 64
        EPS_NORM = 1e-06
        EPS_LIN = 1e-06
        CHUNK = 128

        def rmsnorm(x, w):
            return x * jax.lax.rsqrt(jnp.mean(x * x, axis=-1, keepdims=True) + EPS_NORM) * w

        def taylor_feature_map(x):
            d = x.shape[-1]
            iu, ju = jnp.triu_indices(d)
            scale = jnp.where(iu == ju, 0.5, 1.0 / math.sqrt(2.0)).astype(x.dtype)
            quad = x[..., iu] * x[..., ju] * scale
            ones = jnp.ones(x.shape[:-1] + (1,), dtype=x.dtype)
            return jnp.concatenate([ones, x, quad], axis=-1)

        def linear_attention_causal(q_phi, k_phi, v):
            B, T, H, F = q_phi.shape
            D = v.shape[-1]
            Nc = T // CHUNK
            qc = q_phi.reshape(B, Nc, CHUNK, H, F).transpose(1, 0, 2, 3, 4)
            kc = k_phi.reshape(B, Nc, CHUNK, H, F).transpose(1, 0, 2, 3, 4)
            vc = v.reshape(B, Nc, CHUNK, H, D).transpose(1, 0, 2, 3, 4)
            causal = jnp.tril(jnp.ones((CHUNK, CHUNK), dtype=q_phi.dtype))

            def step(carry, inp):
                kv, ksum = carry
                qb, kb, vb = inp
                A = jnp.einsum('bchf,bshf->bhcs', qb, kb) * causal
                y = jnp.einsum('bhcs,bshd->bchd', A, vb) + jnp.einsum('bchf,bhfd->bchd', qb, kv)
                z = jnp.einsum('bhcs->bch', A) + jnp.einsum('bchf,bhf->bch', qb, ksum)
                kv = kv + jnp.einsum('bshf,bshd->bhfd', kb, vb)
                ksum = ksum + kb.sum(axis=1)
                return ((kv, ksum), y / (z[..., None] + EPS_LIN))
            kv0 = jnp.zeros((B, H, F, D), dtype=q_phi.dtype)
            ks0 = jnp.zeros((B, H, F), dtype=q_phi.dtype)
            _, ys = jax.lax.scan(step, (kv0, ks0), (qc, kc, vc))
            return ys.transpose(1, 0, 2, 3, 4).reshape(B, T, H, D)

        def sliding_window_attention(q, k, v):
            B, T, H, D = q.shape
            scale = 1.0 / math.sqrt(D)
            t = jnp.arange(T)
            allowed = (t[None, :] <= t[:, None]) & (t[None, :] >= t[:, None] - WINDOW)
            scores = jnp.einsum('bqhd,bkhd->bhqk', q, k) * scale
            scores = jnp.where(allowed[None, None], scores, -jnp.inf)
            attn = jax.nn.softmax(scores, axis=-1)
            out = jnp.einsum('bhqk,bkhd->bqhd', attn, v)
            return out.reshape(B, T, H * D)
        key = jax.random.key(seed)
        ks = jax.random.split(key, 7)
        B, T = (2, 256)
        s = 0.02
        return {'x': jax.random.normal(ks[0], (B, T, D_MODEL), jnp.float32), 'norm_w': jnp.ones((D_MODEL,), jnp.float32), 'Wq': jax.random.normal(ks[1], (D_MODEL, D_MODEL), jnp.float32) * s, 'Wk': jax.random.normal(ks[2], (D_MODEL, D_MODEL), jnp.float32) * s, 'Wv': jax.random.normal(ks[3], (D_MODEL, D_MODEL), jnp.float32) * s, 'Wqf': jax.random.normal(ks[4], (HEAD_DIM, FEAT), jnp.float32) * s, 'Wkf': jax.random.normal(ks[5], (HEAD_DIM, FEAT), jnp.float32) * s, 'Wout': jax.random.normal(ks[6], (2 * D_MODEL, D_MODEL), jnp.float32) * s}
    _L0_attn_in = _L0_attn_setup()

    def _L0_ffn_setup():
        import jax, jax.numpy as jnp
        import numpy as np
        NUM_EXPERTS = 8
        TOP_K = 2
        NUM_GRIDS = 8
        INV_DENOM = 0.5
        GRID = np.linspace(-1.2, 0.2, NUM_GRIDS).astype(np.float32)
        LN_EPS = 1e-05

        def _layernorm(x, g, b):
            mu = x.mean(-1, keepdims=True)
            var = x.var(-1, keepdims=True)
            return (x - mu) * jax.lax.rsqrt(var + LN_EPS) * g + b

        def _rswaf(x, grid):
            t = jnp.tanh((x[..., None] - grid) * INV_DENOM)
            return 1.0 - t * t
        key = jax.random.key(seed)
        ks = jax.random.split(key, 8)
        B, S, H, F = (1, 256, 128, 512)
        F2 = F // 2
        E2 = NUM_EXPERTS // 2
        G = NUM_GRIDS
        s = 0.02
        return {'hidden_states': jax.random.normal(ks[0], (B, S, H), jnp.float32), 'gate_W': jax.random.normal(ks[1], (H, NUM_EXPERTS), jnp.float32) * s, 'mlp_W1': jax.random.normal(ks[2], (E2, H, F), jnp.float32) * s, 'mlp_b1': jnp.zeros((E2, F), jnp.float32), 'mlp_W2': jax.random.normal(ks[3], (E2, F, H), jnp.float32) * s, 'mlp_b2': jnp.zeros((E2, H), jnp.float32), 'kan_ln_g0': jnp.ones((E2, H), jnp.float32), 'kan_ln_b0': jnp.zeros((E2, H), jnp.float32), 'kan_sl_W0': jax.random.normal(ks[4], (E2, H * G, F2), jnp.float32) * s, 'kan_sl_b0': jnp.zeros((E2, F2), jnp.float32), 'kan_ln_g1': jnp.ones((E2, F2), jnp.float32), 'kan_ln_b1': jnp.zeros((E2, F2), jnp.float32), 'kan_sl_W1': jax.random.normal(ks[5], (E2, F2 * G, H), jnp.float32) * s, 'kan_sl_b1': jnp.zeros((E2, H), jnp.float32)}
    _L0_ffn_in = _L0_ffn_setup()
    _d = {'L0_attn_x': _L0_attn_in['x'], 'L0_attn_norm_w': _L0_attn_in['norm_w'], 'L0_attn_Wq': _L0_attn_in['Wq'], 'L0_attn_Wk': _L0_attn_in['Wk'], 'L0_attn_Wv': _L0_attn_in['Wv'], 'L0_attn_Wqf': _L0_attn_in['Wqf'], 'L0_attn_Wkf': _L0_attn_in['Wkf'], 'L0_attn_Wout': _L0_attn_in['Wout'], 'L0_ffn_gate_W': _L0_ffn_in['gate_W'], 'L0_ffn_mlp_W1': _L0_ffn_in['mlp_W1'], 'L0_ffn_mlp_b1': _L0_ffn_in['mlp_b1'], 'L0_ffn_mlp_W2': _L0_ffn_in['mlp_W2'], 'L0_ffn_mlp_b2': _L0_ffn_in['mlp_b2'], 'L0_ffn_kan_ln_g0': _L0_ffn_in['kan_ln_g0'], 'L0_ffn_kan_ln_b0': _L0_ffn_in['kan_ln_b0'], 'L0_ffn_kan_sl_W0': _L0_ffn_in['kan_sl_W0'], 'L0_ffn_kan_sl_b0': _L0_ffn_in['kan_sl_b0'], 'L0_ffn_kan_ln_g1': _L0_ffn_in['kan_ln_g1'], 'L0_ffn_kan_ln_b1': _L0_ffn_in['kan_ln_b1'], 'L0_ffn_kan_sl_W1': _L0_ffn_in['kan_sl_W1'], 'L0_ffn_kan_sl_b1': _L0_ffn_in['kan_sl_b1']}
    _x0 = _d['L0_attn_x']
    _d['L0_attn_x'] = jax.random.normal(jax.random.fold_in(jax.random.key(seed), 1), (8, 512, 128), dtype=_x0.dtype)
    del _x0
    return _d

def reference(L0_attn_x, L0_attn_norm_w, L0_attn_Wq, L0_attn_Wk, L0_attn_Wv, L0_attn_Wqf, L0_attn_Wkf, L0_attn_Wout, L0_ffn_gate_W, L0_ffn_mlp_W1, L0_ffn_mlp_b1, L0_ffn_mlp_W2, L0_ffn_mlp_b2, L0_ffn_kan_ln_g0, L0_ffn_kan_ln_b0, L0_ffn_kan_sl_W0, L0_ffn_kan_sl_b0, L0_ffn_kan_ln_g1, L0_ffn_kan_ln_b1, L0_ffn_kan_sl_W1, L0_ffn_kan_sl_b1):

    def _L0_attn_ref(x, norm_w, Wq, Wk, Wv, Wqf, Wkf, Wout):
        import jax, jax.numpy as jnp
        import numpy as np
        import math
        D_MODEL = 128
        N_HEADS = 16
        HEAD_DIM = D_MODEL // N_HEADS
        FEAT = 16
        WINDOW = 64
        EPS_NORM = 1e-06
        EPS_LIN = 1e-06
        CHUNK = 128

        def rmsnorm(x, w):
            return x * jax.lax.rsqrt(jnp.mean(x * x, axis=-1, keepdims=True) + EPS_NORM) * w

        def taylor_feature_map(x):
            d = x.shape[-1]
            iu, ju = jnp.triu_indices(d)
            scale = jnp.where(iu == ju, 0.5, 1.0 / math.sqrt(2.0)).astype(x.dtype)
            quad = x[..., iu] * x[..., ju] * scale
            ones = jnp.ones(x.shape[:-1] + (1,), dtype=x.dtype)
            return jnp.concatenate([ones, x, quad], axis=-1)

        def linear_attention_causal(q_phi, k_phi, v):
            B, T, H, F = q_phi.shape
            D = v.shape[-1]
            Nc = T // CHUNK
            qc = q_phi.reshape(B, Nc, CHUNK, H, F).transpose(1, 0, 2, 3, 4)
            kc = k_phi.reshape(B, Nc, CHUNK, H, F).transpose(1, 0, 2, 3, 4)
            vc = v.reshape(B, Nc, CHUNK, H, D).transpose(1, 0, 2, 3, 4)
            causal = jnp.tril(jnp.ones((CHUNK, CHUNK), dtype=q_phi.dtype))

            def step(carry, inp):
                kv, ksum = carry
                qb, kb, vb = inp
                A = jnp.einsum('bchf,bshf->bhcs', qb, kb) * causal
                y = jnp.einsum('bhcs,bshd->bchd', A, vb) + jnp.einsum('bchf,bhfd->bchd', qb, kv)
                z = jnp.einsum('bhcs->bch', A) + jnp.einsum('bchf,bhf->bch', qb, ksum)
                kv = kv + jnp.einsum('bshf,bshd->bhfd', kb, vb)
                ksum = ksum + kb.sum(axis=1)
                return ((kv, ksum), y / (z[..., None] + EPS_LIN))
            kv0 = jnp.zeros((B, H, F, D), dtype=q_phi.dtype)
            ks0 = jnp.zeros((B, H, F), dtype=q_phi.dtype)
            _, ys = jax.lax.scan(step, (kv0, ks0), (qc, kc, vc))
            return ys.transpose(1, 0, 2, 3, 4).reshape(B, T, H, D)

        def sliding_window_attention(q, k, v):
            B, T, H, D = q.shape
            scale = 1.0 / math.sqrt(D)
            t = jnp.arange(T)
            allowed = (t[None, :] <= t[:, None]) & (t[None, :] >= t[:, None] - WINDOW)
            scores = jnp.einsum('bqhd,bkhd->bhqk', q, k) * scale
            scores = jnp.where(allowed[None, None], scores, -jnp.inf)
            attn = jax.nn.softmax(scores, axis=-1)
            out = jnp.einsum('bhqk,bkhd->bqhd', attn, v)
            return out.reshape(B, T, H * D)
        B, T, _ = x.shape
        h = rmsnorm(x, norm_w)
        q = (h @ Wq).reshape(B, T, N_HEADS, HEAD_DIM)
        k = (h @ Wk).reshape(B, T, N_HEADS, HEAD_DIM)
        v = (h @ Wv).reshape(B, T, N_HEADS, HEAD_DIM)
        q_phi = taylor_feature_map(q @ Wqf)
        k_phi = taylor_feature_map(k @ Wkf)
        lin = linear_attention_causal(q_phi, k_phi, v).reshape(B, T, D_MODEL)
        win = sliding_window_attention(q, k, v)
        out = jnp.concatenate([lin, win], axis=-1) @ Wout
        return x + out

    def _L0_ffn_ref(hidden_states, gate_W, mlp_W1, mlp_b1, mlp_W2, mlp_b2, kan_ln_g0, kan_ln_b0, kan_sl_W0, kan_sl_b0, kan_ln_g1, kan_ln_b1, kan_sl_W1, kan_sl_b1):
        import jax, jax.numpy as jnp
        import numpy as np
        NUM_EXPERTS = 8
        TOP_K = 2
        NUM_GRIDS = 8
        INV_DENOM = 0.5
        GRID = np.linspace(-1.2, 0.2, NUM_GRIDS).astype(np.float32)
        LN_EPS = 1e-05

        def _layernorm(x, g, b):
            mu = x.mean(-1, keepdims=True)
            var = x.var(-1, keepdims=True)
            return (x - mu) * jax.lax.rsqrt(var + LN_EPS) * g + b

        def _rswaf(x, grid):
            t = jnp.tanh((x[..., None] - grid) * INV_DENOM)
            return 1.0 - t * t
        B, S, H = hidden_states.shape
        E2, _, F2 = (kan_sl_W0.shape[0], kan_sl_W0.shape[1], kan_sl_W0.shape[2])
        G = NUM_GRIDS
        x = hidden_states.reshape(-1, H)
        T = x.shape[0]
        logits = x @ gate_W
        probs = jax.nn.softmax(logits.astype(jnp.float32), axis=-1)
        rw, sel = jax.lax.top_k(probs, TOP_K)
        rw = rw / rw.sum(axis=-1, keepdims=True)
        w_full = jnp.sum(jax.nn.one_hot(sel, NUM_EXPERTS, dtype=rw.dtype) * rw[..., None], axis=1)
        w_full = w_full.astype(x.dtype)
        h = jnp.einsum('th,ehf->etf', x, mlp_W1) + mlp_b1[:, None, :]
        h = jax.nn.gelu(h, approximate=False)
        mlp_out = jnp.einsum('etf,efh->eth', h, mlp_W2) + mlp_b2[:, None, :]
        grid = jnp.asarray(GRID)
        h0 = _layernorm(x[None], kan_ln_g0[:, None, :], kan_ln_b0[:, None, :])
        basis0 = _rswaf(h0, grid).reshape(E2, T, H * G)
        z = jnp.einsum('eti,eio->eto', basis0, kan_sl_W0) + kan_sl_b0[:, None, :]
        h1 = _layernorm(z, kan_ln_g1[:, None, :], kan_ln_b1[:, None, :])
        basis1 = _rswaf(h1, grid).reshape(E2, T, F2 * G)
        kan_out = jnp.einsum('eti,eio->eto', basis1, kan_sl_W1) + kan_sl_b1[:, None, :]
        expert_out = jnp.concatenate([mlp_out, kan_out], axis=0)
        out = jnp.einsum('eth,te->th', expert_out, w_full)
        return out.reshape(B, S, H)
    x = L0_attn_x
    x = x + _L0_attn_ref(_layernorm(x, axis=-1), L0_attn_norm_w, L0_attn_Wq, L0_attn_Wk, L0_attn_Wv, L0_attn_Wqf, L0_attn_Wkf, L0_attn_Wout)
    x = x + _L0_ffn_ref(_layernorm(x, axis=-1), L0_ffn_gate_W, L0_ffn_mlp_W1, L0_ffn_mlp_b1, L0_ffn_mlp_W2, L0_ffn_mlp_b2, L0_ffn_kan_ln_g0, L0_ffn_kan_ln_b0, L0_ffn_kan_sl_W0, L0_ffn_kan_sl_b0, L0_ffn_kan_ln_g1, L0_ffn_kan_ln_b1, L0_ffn_kan_sl_W1, L0_ffn_kan_sl_b1)
    return x

_drawn_inputs = setup_inputs


def setup_inputs(seed=0):
    import zlib

    import numpy as np

    out = dict(_drawn_inputs(seed))
    spreads = {'L0_attn_norm_w': (1.0, 0.6),
     'L0_ffn_mlp_b1': (0.0, 0.8),
     'L0_ffn_mlp_b2': (0.0, 0.306),
     'L0_ffn_kan_ln_g0': (1.0, 0.6),
     'L0_ffn_kan_ln_b0': (0.0, 0.8),
     'L0_ffn_kan_sl_b0': (0.0, 0.617),
     'L0_ffn_kan_ln_g1': (1.0, 0.6),
     'L0_ffn_kan_ln_b1': (0.0, 0.8),
     'L0_ffn_kan_sl_b1': (0.0, 0.342)}
    factors = {'L0_attn_Wq': 8.0,
     'L0_attn_Wk': 8.0,
     'L0_attn_Wv': 4.728,
     'L0_attn_Wqf': 8.0,
     'L0_attn_Wkf': 8.0,
     'L0_attn_Wout': 4.883,
     'L0_ffn_mlp_W1': 4.208,
     'L0_ffn_mlp_W2': 3.801}
    for name, (base, spread) in spreads.items():
        noise = np.random.default_rng([zlib.crc32(name.encode()), seed]).standard_normal(out[name].shape)
        drawn = base * np.exp(spread * noise) if base else spread * noise
        out[name] = jnp.asarray(drawn.astype(out[name].dtype))
    for name, factor in factors.items():
        out[name] = (out[name] * factor).astype(out[name].dtype)
    return out
```

```python
from contextlib import ExitStack

import concourse.bass as bass
from concourse import mybir

ALU = mybir.AluOpType
ACT = mybir.ActivationFunctionType
AX = mybir.AxisListType
F32 = mybir.dt.float32
F16 = mybir.dt.float16
BF16 = mybir.dt.bfloat16
I32 = mybir.dt.int32

P = 128
B, T, D = 8, 512, 128
H, DH, FEAT = 16, 8, 16
NT = T // P
WIN = 64
WQ = P + WIN
HG = 4
NHG = H // HG
LN_EPS, RMS_EPS, LIN_EPS = 1e-5, 1e-6, 1e-6
NEG = -1e30

E, E2 = 8, 4
F, F2, G = 512, 256, 8
TS = 512
Q4 = TS // P
SIGS = 4
STEPS = (G, 2 * G)
RECS = 4
TOK = B * T
TILES = 20
GRID_LO, GRID_HI = -1.2, 0.2

KR = 3 * DH
SHIFT_ROW = KR

FRONT = ["hT", "q", "k", "u", "v"]


def main_jobs():
    seg = [("max", hg, NT) for hg in range(NHG)]
    seg += [("lin", 0, 6), ("mT", 0, 1)]
    for n in range(1, NHG):
        seg += [("lin", n, 6), ("pv", n - 1, 0)]
        if n == 3:
            seg += [("ytr", 0, 1)]
        seg += [(f, 0, 1) for f in (["hT"], ["q", "k"], ["u"])[n - 1]]
    for n in range(NHG, 2 * NHG):
        seg += [("win", n, NT), ("pv", n - 1, 0)]
        if n == 4:
            seg += [("v", 0, 1)]
        if n in (5, 7):
            seg += [("ytr", (n - 3) // 2, 1)]
    seg += [("pv", 7, 0)]
    return seg


TAIL = [("ytr", 3, 1), ("ycT", 0, 1), ("out", 0, 1), ("h2T", 0, 1), ("logit", 0, 1), ("rank", 0, 1), ("total", 0, 1)]


def schedule():
    first = [(s, n, k, 0) for s, n, k in main_jobs()]
    second = [(s, n, k, 1) for s, n, k in main_jobs()]
    tail0 = [(s, n, k, 0) for s, n, k in TAIL]
    tail1 = [(s, n, k, 1) for s, n, k in TAIL]
    merged = [tail0[0]] + second[:2] + [tail0[1]] + second[2:4] + [tail0[2]] + second[4:6]
    merged += [tail0[3]] + second[6:8] + [tail0[4]] + second[8:10] + tail0[5:] + second[10:]
    return first + merged + tail1


SCHED = schedule()
SLOTS = 3
SPLIT = ["q", "k", "u"]
JOB0 = len(FRONT)
JOBS = {}
_n = JOB0
for _s, _m, _k, _u in SCHED:
    for _j in range(_k):
        JOBS[(_s, _m, _j, _u)] = _n
        _n += 1
PER_TURN = _n - JOB0
assert PER_TURN % SLOTS == 0
USES = PER_TURN // SLOTS


def transformer_kernel(nc, x, norm_w, Wq, Wk, Wv, Wqf, Wkf, Wout, gate_W, mW1, mb1, mW2, mb2,
                       g0, b0, kW0, kb0, g1, b1, kW1, kb1, grid, out):
    with ExitStack() as ctx:
        def sb(name, shape, dt=F32):
            return ctx.enter_context(nc.sbuf_tensor(name, shape, dt))

        def sem(name):
            return ctx.enter_context(nc.semaphore(name))

        identf = sb("identf", [P, P])
        identb = sb("identb", [P, P], BF16)
        mask_max = sb("mask_max", [P, 2, WQ], BF16)
        mask_win = sb("mask_win", [P, 2, WQ], BF16)
        mask_lin = sb("mask_lin", [P, P])
        block = sb("block", [P, P])
        consts = sb("consts", [P, 5, NT])
        w_raw = sb("w_raw", [P, 3, D])
        w_n = sb("w_n", [P, 4, D])
        w_T = sb("w_T", [P, D])
        w_u = sb("w_u", [P, D])
        qf_rep = sb("qf_rep", [FEAT, H, DH])
        kf_rep = sb("kf_rep", [FEAT, H, DH])
        qf_in = sb("qf_in", [FEAT, DH])
        kf_in = sb("kf_in", [FEAT, DH])
        m_blk = sb("m_blk", [P, P])
        nw = sb("nw", [P, 1])
        wout = sb("wout", [P, 2, D])
        gate = sb("gate", [P, 8])
        ones16 = sb("ones16", [H, T], F16)
        zeros16 = sb("zeros16", [H, T], F16)
        xb = sb("xb", [P, NT, D])
        res = sb("res", [P, 2, NT, D])
        stack = [[sb(f"stack{s}{u}", [P, H * T], F16) for s in range(3)] for u in range(2)]
        vaug = sb("vaug", [P, 2, NT, H, 16])
        stats = sb("stats", [P, NT, 6])
        stats2 = sb("stats2", [P, NT, 6])
        stats2c = sb("stats2c", [P, 1])
        mv = sb("mv", [P, NT, 2])
        mv2 = sb("mv2", [P, NT, 2])
        c1 = sb("c1", [P, 9, NT])
        c2 = sb("c2", [P, 9, NT])
        hn = sb("hn", [P, NT, D])
        hT = sb("hT", [P, T])
        hi = sb("hi", [P, 3, T], F16)
        lo = sb("lo", [P, 3, T], F16)
        negm = sb("negm", [P, NT, H])
        mT16 = sb("mT16", [H, T], F16)
        Pb = sb("Pb", [P, 2, 5120])
        y_sb = sb("y_sb", [P, 2, 2, T])
        rz4 = sb("rz", [P, 4, 32])
        ycat = sb("ycat", [P, NT, 2, D])
        ycT = sb("ycT", [P, 2, T])
        h2 = sb("h2", [P, NT, D])
        n2 = sb("n2", [P, NT, D])
        h2T = sb("h2T", [P, T])
        upper = sb("upper", [P, P], BF16)
        ones_bf = sb("ones_bf", [P, P], BF16)
        prefer = sb("prefer", [P, NT, E])
        first_slot = sb("first_slot", [P, E])
        lg = sb("lg", [P, 8, NT, E])
        sc = sb("sc", [P, 12, NT])
        sel = sb("sel", [P, NT, E], BF16)
        carry = sb("carry", [P, E])
        pos = sb("pos", [P, NT, 2], I32)
        ids_f = sb("ids_f", [P, NT])
        rec = sb("rec", [P, NT, 2, 2], I32)
        tab_f = sb("tab_f", [1, 8, 2, TILES])
        tab_e = sb("tab_e", [1, 8, E])
        tab_i = sb("tab_i", [1, 2, 2, TILES], I32)
        cnt_i = sb("cnt_i", [1, E], I32)
        n_i = sb("n_i", [1, 2], I32)
        kp_raw = sb("kp_raw", [P, E2, 6])
        kp_all = sb("kp_all", [P, E2, 27])
        grid_sb = sb("grid_sb", [P, G])
        pad_rec = Pb[:, 0, 0:2 * E * TOK // P].bitcast(I32)
        zero_rows = Pb[:, 0, 512:512 + TS * D // P]
        kb_raw = Pb[0:1, 0, 1024:1024 + E2 * (F2 + D)].rearrange("p (e n) -> p e n", e=E2)
        ones1 = sb("ones1", [1, P])
        kprm = sb("kprm", [P, RECS, 27])
        mprm = sb("mprm", [P, RECS, F // P])
        mbias = sb("mbias", [1, 2, D])
        trec = sb("trec", [P, 2, RECS, Q4, 2], I32)
        zst = sb("zst", [P, Q4, 6])
        zmv = sb("zmv", [P, Q4, 2])
        zc = sb("zc", [P, 6, Q4])
        kconst = sb("kconst", [P, 3, Q4])
        space = [stack[u][m][:].bitcast(F32) for u in range(2) for m in range(3)]
        space += [Pb[:, 0, 0:4096], Pb[:, 1, 0:4096]]
        kbias = [Pb[0:1, r // 2, 4096 + (F2 + D) * (r % 2):4096 + (F2 + D) * (r % 2 + 1)] for r in range(RECS)]
        kw = [space[0], space[1]]
        basis = [space[2 + z].rearrange("p (r n) -> p r n", r=G) for z in range(2)]
        sig = [space[4][:, 2048 * z:2048 * (z + 1)].rearrange("p (r n) -> p r n", r=SIGS) for z in range(2)]
        k_rows, m_rows = (space[5][:, 2048 * z:2048 * z + 1024].rearrange("p (a q d) -> p a q d", a=2, q=Q4)
                          for z in range(2))
        k_res, m_res = (space[5][:, 2048 * z + 1024:2048 * (z + 1)].rearrange("p (a q d) -> p a q d", a=2, q=Q4)
                        for z in range(2))
        zn = space[6][:, 0:Q4 * F2].rearrange("p (q f) -> p q f", q=Q4)
        mw = [space[6][:, 1024 * (1 + z):1024 * (2 + z)] for z in range(2)]
        mxs = space[6][:, 3072:3072 + TS]
        gelu = space[7].rearrange("p (r n) -> p r n", r=2 * (F // P))

        ring = ctx.enter_context(nc.psum_tensor("ring", [P, SLOTS, 2, 512], F32))
        pv = ctx.enter_context(nc.psum_tensor("pv", [P, 2, 512], F32))

        hl_d = nc.dram_tensor("hl_d", [2, P, 3, T], F16, kind="Internal").ap()
        h2_d = nc.dram_tensor("h2_d", [TOK + TS, D], F32, kind="Internal").ap()
        n2_d = nc.dram_tensor("n2_d", [TOK + TS, D], F32, kind="Internal").ap()
        acc_d = nc.dram_tensor("acc_d", [TOK + TS, D], F32, kind="Internal").ap()
        slot_d = nc.dram_tensor("slot_d", [E * TOK, 2], I32, kind="Internal").ap()
        kp_d = nc.dram_tensor("kp_d", [E2, P, 27], F32, kind="Internal").ap()
        kb_d = nc.dram_tensor("kb_d", [E2, F2 + D], F32, kind="Internal").ap()

        filled = [sem(f"filled{s}") for s in range(SLOTS)]
        freed = [sem(f"freed{s}") for s in range(SLOTS)]
        w_loaded = sem("w_loaded")
        x_loaded = sem("x_loaded")
        const_ready = sem("const_ready")
        act_prep = sem("act_prep")
        prep_mm = sem("prep_mm")
        prep_dve = sem("prep_dve")
        pool_chain = sem("pool_chain")
        dve_chain = sem("dve_chain")
        stats_ready = sem("stats_ready")
        coef_ready = sem("coef_ready")
        hn_ready = sem("hn_ready")
        xres_ready = sem("xres_ready")
        hT_ready = sem("hT_ready")
        hi_ready = sem("hi_ready")
        lo_ready = sem("lo_ready")
        v_ready = sem("v_ready")
        hl_stored = sem("hl_stored")
        stack_loaded = [sem(f"stack_loaded{u}") for u in range(2)]
        ones_loaded = sem("ones_loaded")
        negm_ready = sem("negm_ready")
        mT_ready = sem("mT_ready")
        mrow_loaded = sem("mrow_loaded")
        dm_ready = sem("dm_ready")
        pd_ready = sem("pd_ready")
        po_ready = sem("po_ready")
        pw_ready = sem("pw_ready")
        pv_done = sem("pv_done")
        y_out = [sem("y_out_dve"), sem("y_out_act")]
        ycat_ready = sem("ycat_ready")
        ycT_ready = sem("ycT_ready")
        x1_ready = sem("x1_ready")
        stats2_ready = sem("stats2_ready")
        coef2_ready = sem("coef2_ready")
        h2_ready = sem("h2_ready")
        n2_ready = sem("n2_ready")
        rows_stored = sem("rows_stored")
        h2T_ready = sem("h2T_ready")
        sel_ready = sem("sel_ready")
        gap_ready = sem("gap_ready")
        exp_ready = sem("exp_ready")
        route_chain = sem("route_chain")
        rec_ready = sem("rec_ready")
        slots_stored = sem("slots_stored")
        slots_done = sem("slots_done")
        pads_ready = sem("pads_ready")
        pads_stored = sem("pads_stored")
        kp_loaded = sem("kp_loaded")
        kp_ready = sem("kp_ready")
        table_ready = sem("table_ready")
        k_w0, k_w1, k_x, m_w1, m_w2, m_x = ([sem(f"{name}_{u}") for u in range(2)] for name in (
            "k_w0", "k_w1", "k_x", "m_w1", "m_w2", "m_x"))
        k_rec, m_rec = ([sem(f"{name}_{u}") for u in range(RECS)] for name in ("k_rec", "m_rec"))
        k_xT, k_hT, k_st2, k_st, k_cf, k_zn, k_y, k_add, k_added = (
            sem(name) for name in ("k_xT", "k_hT", "k_st2", "k_st", "k_cf", "k_zn", "k_y", "k_add", "k_added"))
        k_sig, k_bas, k_mm = ([sem(f"{name}{z}") for z in range(2)] for name in ("k_sig", "k_bas", "k_mm"))
        m_xT, m_xs, m_h, m_g, m_mm, m_y, m_add, m_added = (
            sem(name) for name in ("m_xT", "m_xs", "m_h", "m_g", "m_mm", "m_y", "m_add", "m_added"))
        pool_at = sem("pool_at")
        mlps_done = sem("mlps_done")
        all_added = sem("all_added")
        copied = sem("copied")

        x_rows = x.rearrange("b (t p) d -> b p t d", p=P)
        out_rows, h2_rows, n2_rows = (a[0:TOK].rearrange("(b t p) d -> b p t d", b=B, p=P)
                                      for a in (acc_d, h2_d, n2_d))

        def slot(job):
            return ring[:, job % SLOTS]

        def fill_no(job, i):
            return i * USES + (job // SLOTS + 1)

        def wait_filled(eng, job, i):
            eng.wait_ge(filled[job % SLOTS], fill_no(job, i))

        def wait_freed(eng, job, i):
            if job >= SLOTS or not isinstance(i, int):
                eng.wait_ge(freed[job % SLOTS], i * USES + job // SLOTS)

        def job_of(s, n, j, u, i):
            if i == "prologue":
                return FRONT.index(s), 0
            return JOBS[(s, n, j, u)], i

        def batch_no(i, u, per, off):
            return i * (2 * per) + (u * per + off)

        def load_counts(eng):
            eng.wait_ge(table_ready, 1)
            return [eng.value_load(n_i[0:1, kind:kind + 1], min_val=0, max_val=TILES) for kind in range(2)]

        LEAD, LEAD_DMA = 1, 16

        TILE_LEAD = 4

        def tile_no(k, per=1, part=None, back=0):
            return k * per + ((TILE_LEAD - back) * per + (per if part is None else part))

        def tile_lead(eng, *sems):
            for s_, per in sems:
                eng.sem_inc(s_, TILE_LEAD * per)

        def use_no(buffers, i, u, per):
            return i * (RECS // buffers * per) + (u // buffers + 1) * per

        W_DMAS = 10
        PAD_DMAS = 16 * 6
        blk = ctx.enter_context(nc.Block())

        @blk.sync
        def _(sp):
            sp.sem_inc(mrow_loaded, LEAD_DMA)
            sp.sem_inc(rows_stored, LEAD_DMA)
            sp.dma_start(xb[:], x_rows[0]).then_inc(x_loaded, 16)
            for k, w in enumerate((Wq, Wk, Wv)):
                sp.dma_start(w_raw[:, k, :], w).then_inc(w_loaded, 16)
            sp.dma_start(nw[:], norm_w.rearrange("(d a) -> d a", a=1)).then_inc(w_loaded, 16)
            with nc.allow_non_contiguous_dma(reason="two 8x16 matrices, transposed"):
                sp.dma_start(qf_in[:], Wqf.rearrange("d f -> f d")).then_inc(w_loaded, 16)
                sp.dma_start(kf_in[:], Wkf.rearrange("d f -> f d")).then_inc(w_loaded, 16)
            sp.dma_start(wout[:], Wout.rearrange("(k p) n -> p k n", p=P)).then_inc(w_loaded, 32)
            sp.dma_start(gate[:], gate_W).then_inc(w_loaded, 32)
            with nc.allow_non_contiguous_dma(reason="a few hundred words"):
                for k, w in enumerate((g0, b0)):
                    sp.dma_start(kp_raw[:, :, k], w.rearrange("e p -> p e")).then_inc(kp_loaded, 16)
                for k, w in enumerate((g1, b1)):
                    for f in range(2):
                        sp.dma_start(kp_raw[:, :, 2 + 2 * k + f], w[:, P * f:P * (f + 1)].rearrange("e p -> p e")
                                     ).then_inc(kp_loaded, 16)
            sp.dma_start(kb_raw[:, :, 0:F2], kb0.unsqueeze(0)).then_inc(kp_loaded, 16)
            sp.dma_start(kb_raw[:, :, F2:], kb1.unsqueeze(0)).then_inc(kp_loaded, 16)
            sp.dma_start(grid_sb[:], grid.unsqueeze(0).to_broadcast([P, G])).then_inc(kp_loaded, 16)
            sp.wait_ge(const_ready, 3)
            for u in range(2):
                sp.dma_start(stack[u][1][SHIFT_ROW:SHIFT_ROW + 1, :].rearrange("a (h t) -> a h t", h=H),
                             ones16[:]).then_inc(ones_loaded, 16)

            def load_stacks(bf, u, nth):
                sp.wait_ge(lo_ready, bf * 3 + 3)
                sp.dma_start(hl_d[0], hi[:]).then_inc(hl_stored, 16)
                sp.dma_start(hl_d[1], lo[:]).then_inc(hl_stored, 16)
                sp.wait_ge(hl_stored, bf * 32 + 32)
                for s, parts in enumerate(((0, 1, 0), (0, 0, 1), (0, 1, 0))):
                    for g, part in enumerate(parts):
                        sp.dma_start(stack[u][s][DH * g:DH * (g + 1), :].rearrange("d (h t) -> d h t", h=H),
                                     hl_d[part, :, s, :].rearrange("(h d) t -> d h t", d=DH)
                                     ).then_inc(stack_loaded[u], 16)
                sp.dma_start(stack[u][0][SHIFT_ROW:SHIFT_ROW + 1, :].rearrange("a (h t) -> a h t", h=H),
                             zeros16[:]).then_inc(stack_loaded[u], 16)

            sp.wait_ge(pads_ready, 2)
            sp.dma_start(slot_d.rearrange("(p s) w -> p (s w)", p=P), pad_rec).then_inc(pads_stored, 16)
            for rows in (h2_d, n2_d, acc_d):
                sp.dma_start(rows[TOK:].rearrange("(p t) d -> p (t d)", p=P), zero_rows).then_inc(pads_stored, 16)
            sp.wait_ge(kp_ready, 2)
            sp.dma_start(kp_d.rearrange("e p c -> p e c"), kp_all[:]).then_inc(pads_stored, 16)
            sp.dma_start(kb_d.unsqueeze(0), kb_raw).then_inc(pads_stored, 16)
            sp.wait_ge(xres_ready, 1)
            sp.dma_start(xb[:], x_rows[1]).then_inc(x_loaded, 16)
            load_stacks(0, 0, 0)
            with sp.Fori(0, B // 2) as i:
                for s, n, k, u in SCHED:
                    b = i * 2 + u
                    if s == "win" and n == 6:
                        sp.wait_ge(xres_ready, batch_no(i, u, 1, 2))
                        sp.dma_start(xb[:], x_rows[bass.ds((b + 2) % B, 1)].rearrange(
                            "a p t d -> (a p) t d")).then_inc(x_loaded, 16)
                    if s == "mT":
                        sp.wait_ge(mT_ready, batch_no(i, u, 1, 1))
                        sp.dma_start(stack[u][0][SHIFT_ROW:SHIFT_ROW + 1, :].rearrange("a (h t) -> a h t", h=H),
                                     mT16[:]).then_inc(mrow_loaded, 16)
                    if s == "win" and n == 5:
                        sp.wait_ge(pw_ready, batch_no(i, u, 16, LEAD))
                        load_stacks(b + 1, 1 - u, 0)
                    if s == "logit":
                        rows = bass.ds(b, 1)
                        sp.wait_ge(x1_ready, batch_no(i, u, 1, 1))
                        sp.dma_start(out_rows[rows].rearrange("a p t d -> (a p) t d"), res[:, u]
                                     ).then_inc(rows_stored, 16)
                        sp.wait_ge(h2_ready, batch_no(i, u, 1, 1))
                        sp.dma_start(h2_rows[rows].rearrange("a p t d -> (a p) t d"), h2[:]
                                     ).then_inc(rows_stored, 16)
                        sp.wait_ge(n2_ready, batch_no(i, u, 1, 1))
                        sp.dma_start(n2_rows[rows].rearrange("a p t d -> (a p) t d"), n2[:]
                                     ).then_inc(rows_stored, 16)
            sp.wait_ge(rows_stored, LEAD_DMA + 48 * B)
            sp.wait_ge(stack_loaded[0], 160 * (B // 2 + 1))
            sp.wait_ge(x_loaded, 16 * (B + 2))

            n_kind = load_counts(sp)

            def tile_slots(kind, k):
                per = E2 * TOK // TS
                at = sp.value_load(tab_i[0:1, kind, 0, bass.ds(k, 1)], min_val=kind * per, max_val=kind * per + per - 1)
                e = sp.value_load(tab_i[0:1, kind, 1, bass.ds(k, 1)], min_val=kind * E2, max_val=kind * E2 + E2 - 1)
                return bass.ds(e - kind * E2, 1), slot_d.rearrange("(n p q) w -> n p q w", p=P, q=Q4)[bass.ds(at, 1)].rearrange(
                    "a p q w -> (a p) q w")

            with sp.Fori(0, TILES // RECS) as i:
                for u in range(RECS):
                    k = i * RECS + u
                    w = mw[u % 2]
                    with sp.If(k < n_kind[0]):
                        e, rows = tile_slots(0, k)
                        sp.wait_ge(m_added, tile_no(k, back=RECS))
                        sp.dma_start(trec[:, 0, u], rows).then_inc(m_rec[u], 16)
                        sp.wait_ge(m_g, tile_no(k, F // P, back=2))
                        sp.dma_start(w[:, 0:F], mW1[e].rearrange("a p n -> (a p) n")).then_inc(m_w1[u % 2], 16)
                        with nc.allow_non_contiguous_dma(reason="512 words"):
                            sp.dma_start(mprm[:, u], mb1[e].rearrange("a (f p) -> (a p) f", p=P)
                                         ).then_inc(m_w1[u % 2], 16)
                        sp.wait_ge(m_y, tile_no(k, back=2))
                        sp.dma_start(w[:, F:2 * F].rearrange("p (f n) -> p f n", f=F // P),
                                     mW2[e].rearrange("a (f p) n -> (a p) f n", p=P)).then_inc(m_w2[u % 2], 16)
                        sp.dma_start(mbias[:, u % 2], mb2[e]).then_inc(m_w2[u % 2], 16)
            with sp.Fori(0, TILES // RECS) as i:
                for u in range(RECS):
                    k = i * RECS + u
                    w = kw[u % 2]
                    with sp.If(k < n_kind[1]):
                        e, rows = tile_slots(1, k)
                        sp.wait_ge(k_added, tile_no(k, back=RECS))
                        sp.dma_start(trec[:, 1, u], rows).then_inc(k_rec[u], 16)
                        sp.wait_ge(k_zn, tile_no(k, back=2))
                        sp.dma_start(w[:, 0:2048].rearrange("p (g n) -> p g n", g=G),
                                     kW0[e].rearrange("a (p g) n -> (a p) g n", g=G)).then_inc(k_w0[u % 2], 16)
                        sp.dma_start(kprm[:, u], kp_d[e].rearrange("a p c -> (a p) c")).then_inc(k_w0[u % 2], 16)
                        sp.dma_start(kbias[u], kb_d[e]).then_inc(k_w0[u % 2], 16)
                        sp.wait_ge(k_y, tile_no(k, back=2))
                        sp.dma_start(w[:, 2048:4096].rearrange("p (f x) -> p f x", f=2),
                                     kW1[e].rearrange("a (f p g) n -> (a p) f (g n)", f=2, g=G)
                                     ).then_inc(k_w1[u % 2], 16)
            sp.wait_ge(all_added, 1)
            sp.dma_start(out.rearrange("b t d -> (b t) d"), acc_d[0:TOK]).then_inc(copied, 16)
            sp.wait_ge(copied, 16)

        @blk.gpsimd
        def _(pool):
            count = [0]

            def link(ins, i=0, per=0):
                count[0] += 1
                ins.then_inc(pool_chain, 1)
                pool.wait_ge(pool_chain, i * per + count[0])

            pool.sem_inc(slots_done, LEAD)
            pool.memset(ones16[:], 1.0)
            pool.memset(zeros16[:], 0.0).then_inc(const_ready, 1)
            for k, value in enumerate((-0.5, LN_EPS, RMS_EPS, -1.0, 1.0)):
                pool.memset(consts[:, k, :], value)
            link(pool.memset(identf[:], 0.0))
            link(pool.affine_select(identf[:], identf[:], [[-1, P]], ALU.not_equal, 1.0, base=0,
                                    channel_multiplier=1))
            pool.tensor_copy(identb[:], identf[:])
            link(pool.memset(mask_max[:], 0.0))
            link(pool.affine_select(mask_max[:], mask_max[:], [[0, 2], [1, WQ]], ALU.is_ge, NEG, base=0,
                                    channel_multiplier=-1))
            link(pool.affine_select(mask_max[:], mask_max[:], [[0, 2], [-1, WQ]], ALU.is_ge, NEG, base=WIN,
                                    channel_multiplier=1))
            link(pool.memset(mask_win[:], 0.0))
            link(pool.affine_select(mask_win[:], mask_win[:], [[0, 2], [1, WQ]], ALU.is_ge, NEG, base=0,
                                    channel_multiplier=-1))
            link(pool.affine_select(mask_win[:], mask_win[:], [[0, 2], [-1, WQ]], ALU.is_ge, NEG, base=WIN,
                                    channel_multiplier=1))
            link(pool.memset(mask_lin[:], 1.0))
            link(pool.affine_select(mask_lin[:], mask_lin[:], [[1, P]], ALU.is_ge, 0.0, base=0,
                                    channel_multiplier=-1))
            link(pool.memset(block[:], 0.5))
            link(pool.affine_select(block[:], block[:], [[-DH, H], [0, DH]], ALU.is_ge, 0.0, base=0,
                                    channel_multiplier=1))
            pool.affine_select(block[:], block[:], [[DH, H], [0, DH]], ALU.is_ge, 0.0, base=DH - 1,
                               channel_multiplier=-1).then_inc(const_ready, 1)

            half, ln_eps, rms_eps, minus, one = (consts[:, k, :] for k in range(5))

            def coefficients(mvt, c, eps2, i, per):
                m, v = mvt[:, :, 0], mvt[:, :, 1]
                link(pool.tensor_tensor(c[:, 4, :], v, ln_eps, ALU.add), i, per)
                link(pool.tensor_tensor(c[:, 0, :], c[:, 4, :], half, ALU.pow), i, per)
                pool.tensor_tensor(c[:, 8, :], c[:, 0, :], one, ALU.add)
                link(pool.tensor_tensor(c[:, 5, :], v, c[:, 0, :], ALU.mult), i, per)
                link(pool.tensor_tensor(c[:, 6, :], c[:, 5, :], c[:, 0, :], ALU.mult), i, per)
                link(pool.tensor_tensor(c[:, 7, :], c[:, 6, :], eps2, ALU.add), i, per)
                link(pool.tensor_tensor(c[:, 4, :], c[:, 7, :], half, ALU.pow), i, per)
                link(pool.tensor_tensor(c[:, 2, :], c[:, 4, :], c[:, 0, :], ALU.mult), i, per)
                link(pool.tensor_tensor(c[:, 5, :], m, c[:, 0, :], ALU.mult), i, per)
                link(pool.tensor_tensor(c[:, 1, :], c[:, 5, :], minus, ALU.mult), i, per)
                return pool.tensor_tensor(c[:, 3, :], c[:, 1, :], c[:, 4, :], ALU.mult)

            def front_coefficients(bf, i, per):
                pool.wait_ge(stats_ready, bf + 1)
                coefficients(mv, c1, rms_eps, i, per).then_inc(coef_ready, 1)

            pool.memset(zero_rows, 0.0)
            pool.memset(ones1[:], 1.0)
            pool.memset(ones_bf[:], 1.0)
            for k, value in enumerate((16.0, -4.0, LN_EPS)):
                pool.memset(kconst[:, k, :], value)
            pool.iota(pad_rec.rearrange("p (s w) -> p s w", w=2)[:, :, 0], [[1, E * TOK // P]], base=0,
                      channel_multiplier=E * TOK // P)
            pool.iota(rec[:, :, 0, 0], [[P, NT]], base=0, channel_multiplier=1)
            pool.iota(cnt_i[:], [[-1, E]], base=E, channel_multiplier=0)
            pool.iota(tab_i[:, :, 0], [[0, 2], [1, TILES]], base=0, channel_multiplier=0)
            link(pool.memset(upper[:], 1.0))
            pool.affine_select(upper[:], upper[:], [[1, P]], ALU.is_gt, 0.0, base=0, channel_multiplier=-1)
            for e in range(E):
                pool.memset(prefer[:, :, e:e + 1], float(E - e))
                pool.memset(first_slot[:, e:e + 1], float(e * TOK))
            last = pool.memset(carry[:, 0:1], 0.0)
            last.then_inc(pads_ready, 1)
            front_coefficients(0, 0, 0)
            POOL_PER = 36
            start = count[0]
            with pool.Fori(0, B // 2) as i:
                for s, n, k, u in SCHED:
                    b = i * 2 + u
                    if s == "lin":
                        for cp in range(2):
                            pool.wait_ge(dm_ready, batch_no(i, u, 8, 2 * n + cp + 1))
                            pd = Pb[:, n % 2, 1024 * cp:1024 * (cp + 1)]
                            pool.tensor_tensor(pd, pd, pd, ALU.mult).then_inc(pd_ready, 1)
                        if n == 0:
                            front_coefficients(b + 1, i, POOL_PER)
                    if s == "out":
                        pool.wait_ge(stats2_ready, batch_no(i, u, 1, 1))
                        coefficients(mv2, c2, ln_eps, i, POOL_PER).then_inc(coef2_ready, 1)
                    if s == "total":
                        pool.wait_ge(rec_ready, batch_no(i, u, 1, 1))
                        pool.sem_inc(pool_at, 1)
                        for t in range(NT):
                            for c in range(2):
                                pool.indirect_dma_start(
                                    slot_d, bass.IndirectOffsetOnAxis(ap=pos[:, t, c:c + 1], axis=0),
                                    rec[:, t, c, :], None).then_inc(slots_stored, 16)
                        pool.wait_ge(slots_stored, batch_no(i, u, 128, 128))
                        pool.sem_inc(slots_done, 1)
            assert count[0] - start == POOL_PER, count[0] - start

            n_kind = load_counts(pool)
            pool.wait_ge(rows_stored, LEAD_DMA + 48 * B)
            pool.wait_ge(pads_stored, PAD_DMAS)
            tile_lead(pool, (m_added, 1), (k_added, 1), (k_cf, 6))

            def gather(kind, i, u):
                source, rec_sem, xT_sem, x_sem, dst = ((h2_d, m_rec, m_xT, m_x, m_rows),
                                                       (n2_d, k_rec, k_xT, k_x, k_rows))[kind]
                pool.wait_ge(rec_sem[u % RECS], use_no(RECS, i, u, 16))
                pool.wait_ge(xT_sem, tile_no(i * RECS + u, back=2))
                pool.sem_inc(pool_at, 1)
                for q in range(Q4):
                    pool.indirect_dma_start(dst[:, u % 2, q, :], None, source, bass.IndirectOffsetOnAxis(
                        ap=trec[:, kind, u % RECS, q, 0:1], axis=0)).then_inc(x_sem[u % 2], 16)

            def scatter_add(kind, i, u):
                y_sem, add_sem, added, src = ((m_y, m_add, m_added, m_res), (k_y, k_add, k_added, k_res))[kind]
                k = i * RECS + u
                pool.wait_ge(y_sem, tile_no(k))
                pool.sem_inc(pool_at, 1)
                for q in range(Q4):
                    pool.indirect_dma_start(acc_d, bass.IndirectOffsetOnAxis(ap=trec[:, kind, u, q, 0:1], axis=0),
                                            src[:, u % 2, q, :], None, compute_op=ALU.add).then_inc(add_sem, 16)
                pool.wait_ge(add_sem, k * 64 + 64)
                pool.sem_inc(added, 1)

            def hidden_coefficients(i, u):
                k = i * RECS + u
                pool.wait_ge(k_st, tile_no(k))
                for c, (a, b_, op) in enumerate((
                        (zmv[:, :, 1], kconst[:, 0, :], ALU.mult), (zc[:, 0, :], kconst[:, 2, :], ALU.add),
                        (zc[:, 1, :], half, ALU.pow), (zc[:, 2, :], kconst[:, 1, :], ALU.mult),
                        (zmv[:, :, 0], zc[:, 3, :], ALU.mult), (zc[:, 4, :], minus, ALU.mult))):
                    pool.tensor_tensor(zc[:, c, :], a, b_, op).then_inc(k_cf, 1)
                    if c < 5:
                        pool.wait_ge(k_cf, tile_no(k, 6, c + 1))

            for u in range(2):
                with pool.If(n_kind[0] > u):
                    gather(0, 0, u)
            with pool.Fori(0, TILES // RECS) as i:
                for u in range(RECS):
                    k = i * RECS + u
                    with pool.If(k + 2 < n_kind[0]):
                        gather(0, i, u + 2)
                    with pool.If(k < n_kind[0]):
                        scatter_add(0, i, u)
            for u in range(2):
                with pool.If(n_kind[1] > u):
                    gather(1, 0, u)
            with pool.If(n_kind[1] > 0):
                hidden_coefficients(0, 0)
            with pool.If(n_kind[1] > 2):
                gather(1, 0, 2)
            with pool.Fori(0, TILES // RECS) as i:
                for u in range(RECS):
                    k = i * RECS + u
                    with pool.If(k + 1 < n_kind[1]):
                        hidden_coefficients(i, u + 1)
                    with pool.If(k + 3 < n_kind[1]):
                        gather(1, i, u + 3)
                    with pool.If(k < n_kind[1]):
                        scatter_add(1, i, u)
            pool.sem_inc(all_added, 1)

        @blk.scalar
        def _(act):
            act.sem_inc(pw_ready, LEAD)
            act.sem_inc(y_out[1], LEAD)
            act.wait_ge(prep_mm, 1)
            act.activation(w_T[:], slot(0)[:, 0, 0:D], ACT.Copy).then_inc(act_prep, 1)
            act.wait_ge(prep_mm, 2)
            act.activation(w_u[:], slot(1)[:, 0, 0:D], ACT.Copy).then_inc(act_prep, 1)

            def front(s, bf, u, job, i):
                wait_filled(act, job, i)
                src = slot(job)
                if s == "hT":
                    act.activation(hT[:], src[:, 0, :], ACT.Copy).then_inc(freed[job % SLOTS], 1)
                if s in SPLIT:
                    if s == "q" and not isinstance(bf, int):
                        act.wait_ge(hl_stored, bf * 32)
                    act.activation(hi[:, SPLIT.index(s), :], src[:, 0, :], ACT.Copy).then_inc(hi_ready, 1)
                if s == "v":
                    act.activation(vaug[:, u, :, :, 0:DH], src[:, 0, :].rearrange(
                        "p (t h d) -> p t h d", t=NT, h=H), ACT.Copy).then_inc(freed[job % SLOTS], 1)

            for s in FRONT:
                front(s, 0, 0, FRONT.index(s), 0)
            act.wait_ge(pads_stored, PAD_DMAS)
            with act.Fori(0, B // 2) as i:
                for s, n, k, u in SCHED:
                    b = i * 2 + u
                    if s in FRONT:
                        front(s, b + 1, 1 - u, JOBS[(s, n, 0, u)], i)
                    if s == "mT":
                        job = JOBS[(s, n, 0, u)]
                        wait_filled(act, job, i)
                        act.wait_ge(mrow_loaded, batch_no(i, u, 16, LEAD_DMA))
                        act.activation(mT16[:], slot(job)[0:H, 0, :], ACT.Copy).then_inc(mT_ready, 1)
                        act.wait_ge(mT_ready, batch_no(i, u, 1, 1))
                        act.sem_inc(freed[job % SLOTS], 1)
                    if s == "lin":
                        for j in range(HG):
                            job = JOBS[(s, n, 2 + j, u)]
                            wait_filled(act, job, i)
                            if j == 0 and n >= 2:
                                act.wait_ge(pv_done, batch_no(i, u, 8, LEAD + n - 1))
                            act.activation(Pb[:, n % 2, 2048 + 768 * j:2048 + 768 * (j + 1)].rearrange(
                                "p (k q) -> p k q", k=2), slot(job)[:, :, 0:384], ACT.Square,
                                bias=1.0).then_inc(freed[job % SLOTS], 1)
                    if s == "win":
                        for c in range(NT):
                            job = JOBS[(s, n, c, u)]
                            wq = WQ if c < NT - 1 else P
                            wait_filled(act, job, i)
                            if c == 0:
                                act.wait_ge(pv_done, batch_no(i, u, 8, LEAD + n - 1))
                            act.activation(
                                Pb[:, n % 2, 768 * c:768 * (c + 1)].rearrange(
                                    "p (k j q) -> p k j q", k=2, j=2)[:, :, :, 0:wq],
                                slot(job)[:, :, 0:384].rearrange("p k (j q) -> p k j q", j=2)[:, :, :, 0:wq],
                                ACT.Exp).then_inc(pw_ready, 1)
                            act.wait_ge(pw_ready, batch_no(i, u, 16, LEAD + 4 * (n - 4) + c + 1))
                            act.sem_inc(freed[job % SLOTS], 1)
                    if s == "pv" and n % 2 == 1:
                        act.wait_ge(pv_done, batch_no(i, u, 8, LEAD + n + 1))
                        act.activation(y_sb[:, (n // 2) % 2, 1, :], pv[:, 1, :], ACT.Copy
                                       ).then_inc(y_out[1], 1)
                    if s in ("ycT", "h2T"):
                        job = JOBS[(s, n, 0, u)]
                        wait_filled(act, job, i)
                        if s == "ycT":
                            act.activation(ycT[:], slot(job)[:], ACT.Copy).then_inc(freed[job % SLOTS], 1)
                        else:
                            act.activation(h2T[:], slot(job)[:, 0, :], ACT.Copy).then_inc(freed[job % SLOTS], 1)
                    if s == "rank":
                        act.wait_ge(gap_ready, batch_no(i, u, 1, 1))
                        act.activation(sc[:, 7, :], sc[:, 6, :], ACT.Exp).then_inc(exp_ready, 1)

            n_kind = load_counts(act)
            tile_lead(act, (m_xs, 1), (m_g, F // P), (k_sig[0], G), (k_sig[1], 2 * G))

            def copy_rows(i, u):
                k = i * RECS + u
                act.wait_ge(m_xT, tile_no(k))
                act.wait_ge(m_h, tile_no(k, F // P, back=1))
                act.activation(mxs, pv[:, 0, :], ACT.Copy).then_inc(m_xs, 1)

            def hidden(i, u):
                k = i * RECS + u
                act.wait_ge(m_w1[u % 2], use_no(2, i, u, 32))
                act.wait_ge(m_mm, tile_no(k, back=2))
                for f in range(F // P):
                    act.wait_ge(m_h, tile_no(k, F // P, f + 1))
                    act.activation(gelu[:, 4 * (u % 2) + f, :], ring[:, f // 2, f % 2, :], ACT.Gelu,
                                   bias=mprm[:, u % RECS, f:f + 1]).then_inc(m_g, 1)

            with act.If(n_kind[0] > 0):
                copy_rows(0, 0)
                hidden(0, 0)
            with act.If(n_kind[0] > 1):
                copy_rows(0, 1)
            with act.Fori(0, TILES // RECS) as i:
                for u in range(RECS):
                    k = i * RECS + u
                    with act.If(k + 1 < n_kind[0]):
                        hidden(i, u + 1)
                    with act.If(k + 2 < n_kind[0]):
                        copy_rows(i, u + 2)

            def sigmoids(z, i, u):
                k = i * RECS + u
                if z == 0:
                    act.wait_ge(k_w0[u % 2], use_no(2, i, u, 48))
                    act.wait_ge(k_xT, tile_no(k))
                else:
                    act.wait_ge(k_hT, tile_no(k))
                for g in range(STEPS[z]):
                    f = g // G
                    act.wait_ge(k_bas[z], tile_no(k, STEPS[z], g + 1 - SIGS))
                    prm = kprm[:, u % RECS]
                    if z == 0:
                        src, scale, bias = pv[:, 0, :], prm[:, 0:1], prm[:, 1 + g:2 + g]
                    else:
                        src, scale, bias = ring[:, 1, f, :], prm[:, 9 + f:10 + f], prm[:, 11 + g:12 + g]
                    act.activation(sig[z][:, g % SIGS, :], src, ACT.Sigmoid, bias=bias, scale=scale
                                   ).then_inc(k_sig[z], 1)

            for u in range(2):
                with act.If(n_kind[1] > u):
                    sigmoids(0, 0, u)
            with act.Fori(0, TILES // RECS) as i:
                for u in range(RECS):
                    k = i * RECS + u
                    with act.If(k < n_kind[1]):
                        sigmoids(1, i, u)
                    with act.If(k + 2 < n_kind[1]):
                        sigmoids(0, i, u + 2)

        @blk.vector
        def _(dve):
            count = [0]

            def link(ins, i=0, per=0):
                count[0] += 1
                ins.then_inc(dve_chain, 1)
                dve.wait_ge(dve_chain, i * per + count[0])

            dve.sem_inc(y_out[0], LEAD)
            for u in range(2):
                for s in range(3):
                    dve.memset(stack[u][s][:].bitcast(F32), 0.0)
            link(dve.memset(vaug[:], 0.0))
            dve.memset(vaug[:, :, :, :, DH:DH + 1], 1.0)
            dve.memset(pv[:], 0.0).then_inc(const_ready, 1)

            dve.wait_ge(w_loaded, 16 * W_DMAS)
            dve.wait_ge(const_ready, 3)
            dve.tensor_copy(qf_rep[:], qf_in[:].unsqueeze(1).to_broadcast([FEAT, H, DH]))
            dve.tensor_copy(kf_rep[:], kf_in[:].unsqueeze(1).to_broadcast([FEAT, H, DH]))
            dve.tensor_scalar(w_n[:, 0, :], w_raw[:, 0, :], nw[:], DH ** -0.5, ALU.mult, ALU.mult)
            dve.tensor_scalar(w_n[:, 1, :], w_raw[:, 1, :], nw[:], None, ALU.mult)
            dve.tensor_scalar(w_n[:, 2, :], w_raw[:, 2, :], nw[:], None, ALU.mult)
            dve.tensor_scalar(w_n[:, 3, :], w_raw[:, 0, :], nw[:], None, ALU.mult).then_inc(prep_dve, 1)
            dve.wait_ge(prep_mm, 1)
            dve.tensor_tensor(m_blk[:], slot(0)[:, 1, 0:P], block[:], ALU.mult).then_inc(prep_dve, 1)

            def norm_stats(bf, u):
                dve.wait_ge(x_loaded, bf * 16 + 16)
                return [dve.bn_stats(stats[:, t, :], xb[:, t, :]) for t in range(NT)][-1]

            def aggregate(st, m):
                return [dve.bn_aggr(m[:, t, :], st[:, t, :]) for t in range(NT)][-1]

            def front(s, bf, u, job, i):
                wait_filled(dve, job, i)
                m = SPLIT.index(s)
                dve.wait_ge(hi_ready, bf * 3 + m + 1)
                dve.tensor_tensor(lo[:, m, :], slot(job)[:, 0, :], hi[:, m, :], ALU.subtract
                                  ).then_inc(lo_ready, 1)
                dve.wait_ge(lo_ready, bf * 3 + m + 1)
                dve.sem_inc(freed[job % SLOTS], 1)

            def normed(bf, u):
                dve.wait_ge(coef_ready, bf + 1)
                for t in range(NT):
                    last = dve.tensor_scalar(hn[:, t, :], xb[:, t, :], c1[:, 2, t:t + 1],
                                             c1[:, 3, t:t + 1], ALU.mult, ALU.add)
                last.then_inc(hn_ready, 1)

            def residual(bf, u):
                for t in range(NT):
                    last = dve.tensor_scalar(res[:, u, t, :], xb[:, t, :], c1[:, 8, t:t + 1],
                                             c1[:, 1, t:t + 1], ALU.mult, ALU.add)
                last.then_inc(xres_ready, 1)

            dve.wait_ge(pads_ready, 1)
            pads = pad_rec.rearrange("p (s w) -> p s w", w=2)
            link(dve.tensor_scalar(pads[:, :, 0], pads[:, :, 0], TS - 1, None, ALU.bitwise_and))
            dve.tensor_scalar(pads[:, :, 1], pads[:, :, 0], 0.0, None, ALU.mult)
            dve.tensor_copy(ids_f[:], rec[:, :, 0, 0])
            dve.tensor_copy(carry[:], first_slot[:])
            link(dve.tensor_copy(tab_f[:, 0], tab_i[:, :, 0]))
            dve.tensor_scalar(pads[:, :, 0], pads[:, :, 0], float(TOK), None, ALU.add).then_inc(pads_ready, 1)
            dve.wait_ge(kp_loaded, 16 * 9)
            for e in range(E2):
                dve.tensor_copy(kp_all[:, e, 0:1], kp_raw[:, e, 0:1])
                dve.tensor_copy(kp_all[:, e, 9:11], kp_raw[:, e, 2:4])
                for dst, src in ((1, 1), (11, 4), (19, 5)):
                    last = dve.scalar_tensor_tensor(kp_all[:, e, dst:dst + G], grid_sb[:], -1.0,
                                                    kp_raw[:, e, src:src + 1].to_broadcast([P, G]),
                                                    ALU.mult, ALU.add)
            last.then_inc(kp_ready, 1)
            dve.tensor_scalar(kb_raw, kb_raw, -0.25, None, ALU.mult).then_inc(kp_ready, 1)
            link(norm_stats(0, 0))
            aggregate(stats, mv).then_inc(stats_ready, 1)
            normed(0, 0)
            residual(0, 0)
            for s in FRONT:
                if s in SPLIT:
                    front(s, 0, 0, FRONT.index(s), 0)
            dve.wait_ge(pads_stored, PAD_DMAS)
            DVE_PER = 16
            ROUTE = 20
            start = count[0]
            with dve.Fori(0, B // 2) as i:
                for s, n, k, u in SCHED:
                    b = i * 2 + u
                    if s in SPLIT:
                        front(s, b + 1, 1 - u, JOBS[(s, n, 0, u)], i)
                    if s == "max":
                        for c in range(NT):
                            job = JOBS[(s, n, c, u)]
                            wait_filled(dve, job, i)
                            k0 = WIN if c == 0 else 0
                            red = dve.tensor_reduce(
                                negm[:, c, HG * n:HG * (n + 1)].rearrange("p (k j) -> p k j", k=2),
                                slot(job)[:, :, 0:384].rearrange("p k (j q) -> p k j q", j=2)[:, :, :, k0:WQ],
                                AX.X, ALU.max, negate=True)
                            red.then_inc(freed[job % SLOTS], 1)
                            if n == 1 and c == 0:
                                aggregate(stats, mv).then_inc(stats_ready, 1)
                        if n == 0:
                            link(norm_stats(b + 1, 1 - u), i, DVE_PER)
                    if s == "lin":
                        for cp in range(2):
                            job = JOBS[(s, n, cp, u)]
                            wait_filled(dve, job, i)
                            if cp == 0 and n < 2:
                                dve.wait_ge(pv_done, batch_no(i, u, 8, LEAD))
                            if cp == 0 and n >= 2:
                                dve.wait_ge(pv_done, batch_no(i, u, 8, LEAD + n - 1))
                            dve.scalar_tensor_tensor(
                                Pb[:, n % 2, 1024 * cp:1024 * (cp + 1)].rearrange("p (a q) -> p a q", q=P),
                                slot(job)[:].rearrange("p k (j q) -> p (k j) q", q=P), 1.0,
                                mask_lin[:].unsqueeze(1).to_broadcast([P, 8, P]), ALU.add, ALU.mult
                            ).then_inc(dm_ready, 1)
                            dve.wait_ge(dm_ready, batch_no(i, u, 8, 2 * n + cp + 1))
                            dve.sem_inc(freed[job % SLOTS], 1)
                        if n == 0:
                            normed(b + 1, 1 - u)
                    if s == "win" and n == 4:
                        dve.wait_ge(rows_stored, batch_no(i, u, 48, LEAD_DMA))
                        residual(b + 1, 1 - u)
                    if s == "pv" and n % 2 == 0:
                        dve.wait_ge(pv_done, batch_no(i, u, 8, LEAD + n + 1))
                        dve.tensor_copy(y_sb[:, (n // 2) % 2, 0, :], pv[:, 0, :]).then_inc(y_out[0], 1)
                    if s == "ytr":
                        job = JOBS[(s, n, 0, u)]
                        wait_filled(dve, job, i)
                        z = slot(job)[:].rearrange("p k (a c) -> p (k a) c", c=32)[:, :, DH]
                        kind, rz = n // 2, rz4[:, n]
                        if kind == 0:
                            link(dve.tensor_scalar(rz, z, LIN_EPS, None, ALU.add), i, DVE_PER)
                            link(dve.reciprocal(rz, rz), i, DVE_PER)
                        else:
                            link(dve.reciprocal(rz, z), i, DVE_PER)
                        for bk in range(2):
                            hg = (2 * n + bk) % 4
                            last = dve.tensor_tensor(
                                ycat[:, :, kind, 32 * hg:32 * (hg + 1)].rearrange("p t (j d) -> p t j d", j=HG),
                                slot(job)[:, bk, :].rearrange("p (t j c) -> p t j c", t=NT, j=HG)[:, :, :, 0:DH],
                                rz[:, 16 * bk:16 * (bk + 1)].rearrange("p (t j) -> p t j", t=NT).unsqueeze(3)
                                .to_broadcast([P, NT, HG, DH]), ALU.mult)
                        last.then_inc(freed[job % SLOTS], 1)
                    if s == "out":
                        job = JOBS[(s, n, 0, u)]
                        wait_filled(dve, job, i)
                        dve.wait_ge(xres_ready, batch_no(i, u, 1, 1))
                        dve.tensor_tensor(res[:, u].rearrange("p t d -> p (t d)"), slot(job)[:, 0, :],
                                          res[:, u].rearrange("p t d -> p (t d)"), ALU.add).then_inc(x1_ready, 1)
                        dve.wait_ge(x1_ready, batch_no(i, u, 1, 1))
                        dve.sem_inc(freed[job % SLOTS], 1)
                        link([dve.bn_stats(stats2[:, t, :], res[:, u, t, :]) for t in range(NT)][-1], i, DVE_PER)
                        dve.tensor_copy(stats2c[:], stats2[:, 0, 0:1])
                        aggregate(stats2, mv2).then_inc(stats2_ready, 1)
                    if s == "h2T":
                        dve.wait_ge(coef2_ready, batch_no(i, u, 1, 1))
                        dve.wait_ge(rows_stored, batch_no(i, u, 48, LEAD_DMA))
                        for t in range(NT):
                            last = dve.tensor_scalar(h2[:, t, :], res[:, u, t, :], c2[:, 0, t:t + 1],
                                                     c2[:, 1, t:t + 1], ALU.mult, ALU.add)
                        last.then_inc(h2_ready, 1)
                        for t in range(NT):
                            last = dve.tensor_scalar(n2[:, t, :], res[:, u, t, :], c2[:, 2, t:t + 1],
                                                     c2[:, 3, t:t + 1], ALU.mult, ALU.add)
                        last.then_inc(n2_ready, 1)
                    if s == "logit":
                        job = JOBS[(s, n, 0, u)]
                        wait_filled(dve, job, i)
                        step = [0]

                        def chain(ins, wait=True):
                            step[0] += 1
                            ins.then_inc(route_chain, 1)
                            if wait:
                                dve.wait_ge(route_chain, batch_no(i, u, ROUTE, step[0]))

                        logit = slot(job)[:, 0, 0:NT * E].rearrange("p (t e) -> p t e", e=E)
                        dve.wait_ge(slots_done, batch_no(i, u, 1, LEAD))
                        dve.tensor_copy(lg[:, 0], logit).then_inc(freed[job % SLOTS], 1)
                        dve.wait_ge(freed[job % SLOTS], fill_no(job, i))

                        def over_e(row):
                            return sc[:, row, :].unsqueeze(2).to_broadcast([P, NT, E])

                        for c in range(2):
                            chain(dve.tensor_reduce(sc[:, c, :], lg[:, c], AX.X, ALU.max))
                            chain(dve.tensor_tensor(lg[:, 2], lg[:, c], over_e(c), ALU.is_equal))
                            chain(dve.tensor_tensor(lg[:, 5], lg[:, 2], prefer[:], ALU.mult))
                            chain(dve.tensor_reduce(sc[:, 2 + c, :], lg[:, 5], AX.X, ALU.max))
                            chain(dve.tensor_tensor(lg[:, 3 + c], prefer[:], over_e(2 + c), ALU.is_equal))
                            if c == 0:
                                chain(dve.scalar_tensor_tensor(lg[:, 1], lg[:, 3], NEG, lg[:, 0], ALU.mult, ALU.add))
                        dve.tensor_tensor(sel[:], lg[:, 3], lg[:, 4], ALU.add).then_inc(sel_ready, 1)
                        dve.tensor_tensor(sc[:, 6, :], sc[:, 1, :], sc[:, 0, :], ALU.subtract).then_inc(gap_ready, 1)
                    if s == "rank":
                        dve.wait_ge(exp_ready, batch_no(i, u, 1, 1))
                        w = rec[:].bitcast(F32)
                        chain(dve.tensor_scalar(sc[:, 8, :], sc[:, 7, :], 1.0, None, ALU.add))
                        chain(dve.reciprocal(w[:, :, 0, 1], sc[:, 8, :]))
                        chain(dve.tensor_tensor(w[:, :, 1, 1], w[:, :, 0, 1], sc[:, 7, :], ALU.mult), False)
                        for c in range(2):
                            dve.tensor_copy(rec[:, :, c, 0], ids_f[:])
                        chain(dve.tensor_scalar(sc[:, 9, :], ids_f[:], float(T), None, ALU.add))
                        chain(dve.tensor_copy(ids_f[:], sc[:, 9, :]), False)
                        job = JOBS[(s, n, 0, u)]
                        wait_filled(dve, job, i)
                        dve.tensor_tensor(lg[:, 6], slot(job)[:, 0, 0:NT * E].rearrange("p (t e) -> p t e", e=E),
                                          carry[:].unsqueeze(1).to_broadcast([P, NT, E]), ALU.add
                                          ).then_inc(freed[job % SLOTS], 1)
                        dve.wait_ge(freed[job % SLOTS], fill_no(job, i))
                        for c in range(2):
                            chain(dve.tensor_tensor(lg[:, 5 + 2 * c], lg[:, 6], lg[:, 3 + c], ALU.mult))
                            chain(dve.tensor_reduce(sc[:, 10 + c, :], lg[:, 5 + 2 * c], AX.X, ALU.add))
                        dve.tensor_copy(pos[:].rearrange("p t c -> p c t"), sc[:, 10:12, :]).then_inc(rec_ready, 1)
                        assert step[0] == ROUTE, step[0]
                    if s == "total":
                        job = JOBS[(s, n, 0, u)]
                        wait_filled(dve, job, i)
                        dve.tensor_tensor(carry[:], slot(job)[:, 0, 0:E], carry[:], ALU.add
                                          ).then_inc(freed[job % SLOTS], 1)
            assert count[0] - start == DVE_PER, count[0] - start

            total_job = JOBS[("total", 0, 0, 1)]
            dve.wait_ge(freed[total_job % SLOTS], fill_no(total_job, B // 2 - 1))
            last_count = (B // 2 - 1) * DVE_PER

            def link2(ins):
                link(ins, 1, last_count + start)

            count[0] = DVE_PER
            link2(dve.tensor_tensor(tab_e[:, 0], carry[0:1, :], first_slot[0:1, :], ALU.subtract))
            link2(dve.tensor_scalar(tab_e[:, 1], tab_e[:, 0], float(TS - 1), None, ALU.add))
            link2(dve.tensor_copy(cnt_i[:], tab_e[:, 1]))
            link2(dve.tensor_scalar(cnt_i[:], cnt_i[:], 9, None, ALU.logical_shift_right))
            link2(dve.tensor_copy(tab_e[:, 2], cnt_i[:]))
            link2(dve.tensor_scalar(tab_e[:, 3], tab_e[:, 2], -1.0, float(TOK // TS), ALU.mult, ALU.add))
            for kind in range(2):
                link2(dve.tensor_copy(tab_e[:, 4, E2 * kind:E2 * kind + 1], tab_e[:, 2, E2 * kind:E2 * kind + 1]))
                for e in range(E2 * kind + 1, E2 * kind + E2):
                    link2(dve.tensor_tensor(tab_e[:, 4, e:e + 1], tab_e[:, 4, e - 1:e], tab_e[:, 2, e:e + 1], ALU.add))
                link2(dve.tensor_scalar(tab_f[:, 1, kind], tab_f[:, 0, kind], float(E2 * kind * (TOK // TS)), None,
                                        ALU.add))
                for j in range(E2 - 1):
                    e = E2 * kind + j
                    link2(dve.tensor_scalar(tab_f[:, 5, kind], tab_f[:, 0, kind], tab_e[:, 4, e:e + 1],
                                            tab_e[:, 3, e:e + 1], ALU.is_ge, ALU.mult))
                    link2(dve.tensor_tensor(tab_f[:, 2 + j, kind], tab_f[:, 1 + j, kind], tab_f[:, 5, kind], ALU.add))
                link2(dve.tensor_scalar(tab_f[:, 6, kind], tab_f[:, 4, kind], float((kind + 1) * E2 * TOK // TS - 1),
                                        None, ALU.min))
                link2(dve.tensor_copy(tab_i[:, kind, 0], tab_f[:, 6, kind]))
                link2(dve.tensor_scalar(tab_i[:, kind, 1], tab_i[:, kind, 0], (TOK // TS).bit_length() - 1, None,
                                        ALU.logical_shift_right))
                link2(dve.tensor_copy(n_i[:, kind:kind + 1], tab_e[:, 4, E2 * kind + 3:E2 * kind + 4]))
            dve.wait_ge(slots_done, LEAD + B)
            dve.sem_inc(table_ready, 1)

            n_kind = load_counts(dve)
            tile_lead(dve, (m_y, 1), (k_y, 1), (k_st2, 1), (k_st, 1), (k_zn, 1), (k_bas[0], G), (k_bas[1], 2 * G))
            weight = trec[:].bitcast(F32)

            def weighted(kind, i, u):
                k = i * RECS + u
                rec_sem, added, mm_sem, per, dst, y_sem = (
                    (m_rec, m_added, m_mm, 1, m_res, m_y), (k_rec, k_added, k_mm[1], 2 * G, k_res, k_y))[kind]
                dve.wait_ge(rec_sem[u], use_no(RECS, i, u, 16))
                dve.wait_ge(added, tile_no(k, back=2))
                dve.wait_ge(mm_sem, tile_no(k, per))
                for q in range(Q4):
                    last = dve.tensor_scalar(dst[:, u % 2, q, :], pv[:, 1, P * q:P * (q + 1)],
                                             weight[:, kind, u, q, 1:2], (1.0, -4.0)[kind], ALU.mult, ALU.mult)
                last.then_inc(y_sem, 1)

            def basis_functions(z, i, u, steps):
                k = i * RECS + u
                for g in steps:
                    dve.wait_ge(k_sig[z], tile_no(k, STEPS[z], g + 1))
                    dve.wait_ge(k_mm[z], tile_no(k, STEPS[z], g + 1 - G))
                    s_ = sig[z][:, g % SIGS, :]
                    dve.scalar_tensor_tensor(basis[z][:, g % G, :], s_, -1.0, s_, ALU.add, ALU.mult
                                             ).then_inc(k_bas[z], 1)

            def z_rows(q):
                return ring[:, 0, q // 2, F2 * (q % 2):F2 * (q % 2 + 1)]

            def hidden_stats(i, u):
                k = i * RECS + u
                dve.wait_ge(k_mm[0], tile_no(k, G))
                for q in range(Q4):
                    last = dve.bn_stats(zst[:, q, :], z_rows(q))
                last.then_inc(k_st2, 1)
                dve.wait_ge(k_st2, tile_no(k))
                dve.tensor_copy(stats2c[:], zst[:, 0, 0:1])
                for q in range(Q4):
                    last = dve.bn_aggr(zmv[:, q, :], zst[:, q, :])
                last.then_inc(k_st, 1)

            def hidden_norm(i, u):
                k = i * RECS + u
                dve.wait_ge(k_cf, tile_no(k, 6))
                dve.wait_ge(k_hT, tile_no(k, back=1))
                for q in range(Q4):
                    last = dve.tensor_scalar(zn[:, q, :], z_rows(q), zc[:, 3, q:q + 1], zc[:, 5, q:q + 1],
                                             ALU.mult, ALU.add)
                last.then_inc(k_zn, 1)

            with dve.Fori(0, TILES // RECS) as i:
                for u in range(RECS):
                    k = i * RECS + u
                    with dve.If(k < n_kind[0]):
                        weighted(0, i, u)
            with dve.If(n_kind[1] > 0):
                basis_functions(0, 0, 0, range(G))
                hidden_stats(0, 0)
                hidden_norm(0, 0)
            with dve.If(n_kind[1] > 1):
                basis_functions(0, 0, 1, range(G))
            with dve.Fori(0, TILES // RECS) as i:
                for u in range(RECS):
                    k = i * RECS + u
                    with dve.If(k < n_kind[1]):
                        basis_functions(1, i, u, range(0, G))
                    with dve.If(k + 1 < n_kind[1]):
                        hidden_stats(i, u + 1)
                    with dve.If(k < n_kind[1]):
                        basis_functions(1, i, u, range(G, G + 2))
                    with dve.If(k + 1 < n_kind[1]):
                        hidden_norm(i, u + 1)
                    with dve.If(k < n_kind[1]):
                        basis_functions(1, i, u, range(G + 2, 2 * G))
                    with dve.If(k + 2 < n_kind[1]):
                        basis_functions(0, i, u + 2, range(G))
                    with dve.If(k < n_kind[1]):
                        weighted(1, i, u)

        @blk.tensor
        def _(pe):
            pe.sem_inc(pv_done, LEAD)
            pe.wait_ge(const_ready, 3)
            pe.wait_ge(prep_dve, 1)
            pe.transpose(slot(0)[:, 0, 0:P], w_n[:, 3, :], identf[:])
            pe.matmul(slot(0)[:, 1, 0:P], qf_rep[:].rearrange("f h d -> f (h d)"),
                      kf_rep[:].rearrange("f h d -> f (h d)"), start=True, stop=True).then_inc(prep_mm, 1)
            pe.wait_ge(act_prep, 1)
            pe.wait_ge(prep_dve, 2)
            pe.matmul(slot(1)[:, 0, 0:D], w_T[:], m_blk[:], start=True, stop=True).then_inc(prep_mm, 1)
            pe.wait_ge(act_prep, 2)

            def front(s, bf, u, job, i, first):
                if s == "hT":
                    pe.wait_ge(hn_ready, bf + 1)
                if s == "q":
                    hT_job = FRONT.index("hT") if first else JOBS[("hT", 0, 0, 1 - u)]
                    pe.wait_ge(freed[hT_job % SLOTS], fill_no(hT_job, i))
                wait_freed(pe, job, i)
                dst = slot(job)
                if s == "hT":
                    for t in range(NT):
                        mm = pe.transpose(dst[:, 0, P * t:P * (t + 1)], hn[:, t, :], identf[:])
                if s in SPLIT:
                    w = {"q": w_n[:, 0, :], "k": w_n[:, 1, :], "u": w_u[:]}[s]
                    mm = pe.matmul(dst[:, 0, :], w, hT[:], start=True, stop=True)
                if s == "v":
                    for t in range(NT):
                        mm = pe.matmul(dst[:, 0, P * t:P * (t + 1)], hT[:, P * t:P * (t + 1)], w_n[:, 2, :],
                                       start=True, stop=True)
                mm.then_inc(filled[job % SLOTS], 1)

            for s in FRONT:
                front(s, 0, 0, FRONT.index(s), 0, True)
            pe.wait_ge(ones_loaded, 32)
            with pe.Fori(0, B // 2) as i:
                for s, n, k, u in SCHED:
                    b = i * 2 + u
                    sq, sk, su = (stack[u][m][:].rearrange("r (h t) -> r h t", h=H) for m in range(3))
                    if s in FRONT:
                        front(s, b + 1, 1 - u, JOBS[(s, n, 0, u)], i, False)
                    if s == "max":
                        if n == 0:
                            pe.wait_ge(stack_loaded[u], i * 160 + 160)
                        for c in range(NT):
                            job = JOBS[(s, n, c, u)]
                            wait_freed(pe, job, i)
                            k0 = WIN if c == 0 else 0
                            for bk in range(2):
                                pe.matmul(slot(job)[:, bk, 0:2 * WQ], identb[:],
                                          mask_max[:].rearrange("p a q -> p (a q)"), start=True, stop=True)
                                for jj in range(2):
                                    h = HG * n + 2 * bk + jj
                                    mm = pe.matmul(slot(job)[:, bk, WQ * jj + k0:WQ * (jj + 1)],
                                                   sq[:, h, P * c:P * (c + 1)],
                                                   sk[:, h, P * c - WIN + k0:P * (c + 1)],
                                                   start=False, stop=True, skip_group_check=True)
                            mm.then_inc(filled[job % SLOTS], 1)
                    if s == "mT":
                        job = JOBS[(s, n, 0, u)]
                        wait_freed(pe, job, i)
                        last_max = JOBS[("max", NHG - 1, NT - 1, u)]
                        pe.wait_ge(freed[last_max % SLOTS], fill_no(last_max, i))
                        for c in range(NT):
                            mm = pe.transpose(slot(job)[0:H, 0, P * c:P * (c + 1)], negm[:, c, :], identf[:])
                        mm.then_inc(filled[job % SLOTS], 1)
                    if s == "lin":
                        for cp in range(2):
                            job = JOBS[(s, n, cp, u)]
                            wait_freed(pe, job, i)
                            for bk in range(2):
                                c = 2 * cp + bk
                                for j in range(HG):
                                    mm = pe.matmul(slot(job)[:, bk, P * j:P * (j + 1)],
                                                   sk[:, HG * n + j, P * c:P * (c + 1)],
                                                   su[:, HG * n + j, P * c:P * (c + 1)], start=True, stop=True)
                            mm.then_inc(filled[job % SLOTS], 1)
                        for j in range(HG):
                            job = JOBS[(s, n, 2 + j, u)]
                            wait_freed(pe, job, i)
                            for bk, o, c in ((0, 0, 0), (1, 0, 1), (1, 256, 2)):
                                w = T - P * (c + 1)
                                mm = pe.matmul(slot(job)[:, bk, o:o + w],
                                               sk[:, HG * n + j, P * c:P * (c + 1)],
                                               su[:, HG * n + j, P * (c + 1):T], start=True, stop=True)
                            mm.then_inc(filled[job % SLOTS], 1)
                    if s == "win":
                        if n == NHG:
                            pe.wait_ge(mrow_loaded, batch_no(i, u, 16, LEAD_DMA + 16))
                        for c in range(NT):
                            job = JOBS[(s, n, c, u)]
                            wq = WQ if c < NT - 1 else P
                            wait_freed(pe, job, i)
                            for bk in range(2):
                                pe.matmul(slot(job)[:, bk, 0:2 * WQ], identb[:],
                                          mask_win[:].rearrange("p a q -> p (a q)"), start=True, stop=True)
                                for jj in range(2):
                                    h = HG * (n - NHG) + 2 * bk + jj
                                    mm = pe.matmul(slot(job)[:, bk, WQ * jj:WQ * jj + wq],
                                                   sk[:, h, P * c:P * (c + 1)],
                                                   sq[:, h, P * c:P * c + wq],
                                                   start=False, stop=True, skip_group_check=True)
                            mm.then_inc(filled[job % SLOTS], 1)
                    if s == "pv":
                        if n == 0:
                            v_job = JOBS[("v", 0, 0, 1)] if u == 0 else JOBS[("v", 0, 0, 0)]
                        if n < NHG:
                            pe.wait_ge(pd_ready, batch_no(i, u, 8, 2 * n + 2))
                            po_job = JOBS[("lin", n, 5, u)]
                            pe.wait_ge(freed[po_job % SLOTS], fill_no(po_job, i))
                        else:
                            pe.wait_ge(pw_ready, batch_no(i, u, 16, LEAD + 4 * (n - NHG) + 4))
                        pe.wait_ge(y_out[n % 2], batch_no(i, u, 4, LEAD + n // 2))
                        for c in range(NT):
                            parts = []
                            if n < NHG:
                                pd = Pb[:, n % 2, 512 * c:512 * (c + 1)].rearrange("p (j q) -> p j q", j=HG)
                                po = Pb[:, n % 2, 2048:5120].rearrange("p (j q) -> p j q", j=HG)
                                parts.append((P * c, P, pd))
                                if c < NT - 1:
                                    o = (0, 384, 640)[c]
                                    w = T - P * (c + 1)
                                    parts.append((P * (c + 1), w, po[:, :, o:o + w]))
                            else:
                                wq = WQ if c < NT - 1 else P
                                pw = Pb[:, n % 2, 768 * c:768 * (c + 1)].rearrange("p (j q) -> p j q", j=HG)
                                parts.append((P * c, wq, pw[:, :, 0:wq]))
                            for x_, (q0, w, src) in enumerate(parts):
                                for j in range(HG):
                                    mm = pe.matmul(pv[32 * j:32 * j + 16, n % 2, q0:q0 + w],
                                                   vaug[:, u, c, HG * (n % NHG) + j, :], src[:, j, :],
                                                   start=(c == 0 and x_ == 0), stop=(c == NT - 1),
                                                   skip_group_check=True)
                        mm.then_inc(pv_done, 1)
                    if s == "ytr":
                        job = JOBS[(s, n, 0, u)]
                        wait_freed(pe, job, i)
                        for bk in range(2):
                            pe.wait_ge(y_out[bk], batch_no(i, u, 4, LEAD + n + 1))
                            for t in range(NT):
                                mm = pe.transpose(slot(job)[:, bk, P * t:P * (t + 1)],
                                                  y_sb[:, n % 2, bk, P * t:P * (t + 1)], identf[:])
                        mm.then_inc(filled[job % SLOTS], 1)
                    if s == "ycT":
                        job = JOBS[(s, n, 0, u)]
                        wait_freed(pe, job, i)
                        y_job = JOBS[("ytr", 3, 0, u)]
                        pe.wait_ge(freed[y_job % SLOTS], fill_no(y_job, i))
                        for kind in range(2):
                            for t in range(NT):
                                mm = pe.transpose(slot(job)[:, kind, P * t:P * (t + 1)], ycat[:, t, kind, :],
                                                  identf[:])
                        mm.then_inc(filled[job % SLOTS], 1)
                    if s == "out":
                        job = JOBS[(s, n, 0, u)]
                        wait_freed(pe, job, i)
                        c_job = JOBS[("ycT", 0, 0, u)]
                        pe.wait_ge(freed[c_job % SLOTS], fill_no(c_job, i))
                        for t in range(NT):
                            for kind in range(2):
                                mm = pe.matmul(slot(job)[:, 0, P * t:P * (t + 1)], ycT[:, kind, P * t:P * (t + 1)],
                                               wout[:, kind, :], start=(kind == 0), stop=(kind == 1))
                        mm.then_inc(filled[job % SLOTS], 1)
                    if s == "h2T":
                        job = JOBS[(s, n, 0, u)]
                        wait_freed(pe, job, i)
                        pe.wait_ge(h2_ready, batch_no(i, u, 1, 1))
                        for t in range(NT):
                            mm = pe.transpose(slot(job)[:, 0, P * t:P * (t + 1)], h2[:, t, :], identf[:])
                        mm.then_inc(filled[job % SLOTS], 1)
                    if s == "logit":
                        job = JOBS[(s, n, 0, u)]
                        wait_freed(pe, job, i)
                        t_job = JOBS[("h2T", 0, 0, u)]
                        pe.wait_ge(freed[t_job % SLOTS], fill_no(t_job, i))
                        for t in range(NT):
                            mm = pe.matmul(slot(job)[:, 0, 8 * t:8 * (t + 1)], h2T[:, P * t:P * (t + 1)], gate[:],
                                           start=True, stop=True)
                        mm.then_inc(filled[job % SLOTS], 1)
                    if s == "rank":
                        job = JOBS[(s, n, 0, u)]
                        wait_freed(pe, job, i)
                        pe.wait_ge(sel_ready, batch_no(i, u, 1, 1))
                        for t in range(NT):
                            for t2 in range(t + 1):
                                mm = pe.matmul(slot(job)[:, 0, E * t:E * (t + 1)], upper[:] if t2 == t else ones_bf[:],
                                               sel[:, t2, :], start=(t2 == 0), stop=(t2 == t))
                        mm.then_inc(filled[job % SLOTS], 1)
                    if s == "total":
                        job = JOBS[(s, n, 0, u)]
                        wait_freed(pe, job, i)
                        for t in range(NT):
                            mm = pe.matmul(slot(job)[:, 0, 0:E], ones_bf[:], sel[:, t, :], start=(t == 0),
                                           stop=(t == NT - 1))
                        mm.then_inc(filled[job % SLOTS], 1)

            n_kind = load_counts(pe)
            tile_lead(pe, (m_xT, 1), (m_h, F // P), (m_mm, 1), (k_xT, 1), (k_hT, 1), (k_mm[0], G), (k_mm[1], 2 * G))

            def rows_transposed(kind, i, u):
                k = i * RECS + u
                x_sem, rows, xT_sem = ((m_x, m_rows, m_xT), (k_x, k_rows, k_xT))[kind]
                pe.wait_ge(x_sem[u % 2], use_no(2, i, u, 64))
                pe.wait_ge(*((m_xs, tile_no(k, back=1)) if kind == 0 else (k_sig[0], tile_no(k, G, back=1))))
                for q in range(Q4):
                    mm = pe.transpose(pv[:, 0, P * q:P * (q + 1)], rows[:, u % 2, q, :], identf[:])
                mm.then_inc(xT_sem, 1)

            def bias_row(dst, copies, row, n):
                pe.matmul(dst.rearrange("p (q d) -> p q d", q=copies), ones1[:],
                          row.unsqueeze(1).to_broadcast([1, copies, n]), start=True, stop=True)

            def mlp_first(i, u):
                k = i * RECS + u
                pe.wait_ge(m_w1[u % 2], use_no(2, i, u, 32))
                pe.wait_ge(m_xs, tile_no(k))
                pe.wait_ge(m_g, tile_no(k, F // P, back=1))
                for f in range(F // P):
                    pe.matmul(ring[:, f // 2, f % 2, :], mw[u % 2][:, P * f:P * (f + 1)], mxs,
                              start=True, stop=True).then_inc(m_h, 1)

            def mlp_second(i, u):
                k = i * RECS + u
                pe.wait_ge(m_w2[u % 2], use_no(2, i, u, 32))
                pe.wait_ge(m_y, tile_no(k, back=1))
                bias_row(pv[:, 1, :], Q4, mbias[:, u % 2], D)
                for f in range(F // P):
                    pe.wait_ge(m_g, tile_no(k, F // P, f + 1))
                    for q in range(Q4):
                        mm = pe.matmul(pv[:, 1, P * q:P * (q + 1)], gelu[:, 4 * (u % 2) + f, P * q:P * (q + 1)],
                                       mw[u % 2][:, F + D * f:F + D * (f + 1)], start=False, stop=True,
                                       skip_group_check=True)
                mm.then_inc(m_mm, 1)

            with pe.If(n_kind[0] > 0):
                rows_transposed(0, 0, 0)
                mlp_first(0, 0)
            with pe.If(n_kind[0] > 1):
                rows_transposed(0, 0, 1)
            with pe.Fori(0, TILES // RECS) as i:
                for u in range(RECS):
                    k = i * RECS + u
                    with pe.If(k + 1 < n_kind[0]):
                        mlp_first(i, u + 1)
                    with pe.If(k + 2 < n_kind[0]):
                        rows_transposed(0, i, u + 2)
                    with pe.If(k < n_kind[0]):
                        mlp_second(i, u)
            pe.wait_ge(m_y, n_kind[0] + TILE_LEAD)
            pe.sem_inc(mlps_done, 1)

            def kan_first(i, u):
                k = i * RECS + u
                pe.wait_ge(k_w0[u % 2], use_no(2, i, u, 48))
                pe.wait_ge(k_zn, tile_no(k, back=1))
                for bk in range(2):
                    bias_row(ring[:, 0, bk, :], 2, kbias[u % RECS][:, 0:F2], F2)
                for g in range(G):
                    pe.wait_ge(k_bas[0], tile_no(k, G, g + 1))
                    for q in range(Q4):
                        mm = pe.matmul(ring[:, 0, q // 2, F2 * (q % 2):F2 * (q % 2 + 1)],
                                       basis[0][:, g, P * q:P * (q + 1)], kw[u % 2][:, F2 * g:F2 * (g + 1)],
                                       start=False, stop=True, skip_group_check=True)
                    mm.then_inc(k_mm[0], 1)

            def hidden_transposed(i, u):
                k = i * RECS + u
                pe.wait_ge(k_zn, tile_no(k))
                pe.wait_ge(k_sig[1], tile_no(k, 2 * G, back=1))
                for f in range(2):
                    for q in range(Q4):
                        mm = pe.transpose(ring[:, 1, f, P * q:P * (q + 1)], zn[:, q, P * f:P * (f + 1)], identf[:])
                mm.then_inc(k_hT, 1)

            def kan_second(i, u):
                k = i * RECS + u
                pe.wait_ge(k_w1[u % 2], use_no(2, i, u, 16))
                pe.wait_ge(k_y, tile_no(k, back=1))
                bias_row(pv[:, 1, :], Q4, kbias[u % RECS][:, F2:], D)
                for g in range(2 * G):
                    pe.wait_ge(k_bas[1], tile_no(k, 2 * G, g + 1))
                    for q in range(Q4):
                        mm = pe.matmul(pv[:, 1, P * q:P * (q + 1)], basis[1][:, g % G, P * q:P * (q + 1)],
                                       kw[u % 2][:, 2048 + D * g:2048 + D * (g + 1)], start=False, stop=True,
                                       skip_group_check=True)
                    mm.then_inc(k_mm[1], 1)

            with pe.If(n_kind[1] > 0):
                rows_transposed(1, 0, 0)
                kan_first(0, 0)
            with pe.If(n_kind[1] > 1):
                rows_transposed(1, 0, 1)
            with pe.Fori(0, TILES // RECS) as i:
                for u in range(RECS):
                    k = i * RECS + u
                    with pe.If(k < n_kind[1]):
                        hidden_transposed(i, u)
                    with pe.If(k + 1 < n_kind[1]):
                        kan_first(i, u + 1)
                    with pe.If(k + 2 < n_kind[1]):
                        rows_transposed(1, i, u + 2)
                    with pe.If(k < n_kind[1]):
                        kan_second(i, u)


def kernel(**inputs):
    import numpy as np
    import concourse.bacc as bacc
    from concourse.bass_utils import run_bass_kernel_spmd as run

    nc = bacc.Bacc("TRN2", target_bir_lowering=False, num_devices=1)
    names = ["L0_attn_x", "L0_attn_norm_w", "L0_attn_Wq", "L0_attn_Wk", "L0_attn_Wv", "L0_attn_Wqf",
             "L0_attn_Wkf", "L0_attn_Wout", "L0_ffn_gate_W", "L0_ffn_mlp_W1", "L0_ffn_mlp_b1", "L0_ffn_mlp_W2",
             "L0_ffn_mlp_b2", "L0_ffn_kan_ln_g0", "L0_ffn_kan_ln_b0", "L0_ffn_kan_sl_W0", "L0_ffn_kan_sl_b0",
             "L0_ffn_kan_ln_g1", "L0_ffn_kan_ln_b1", "L0_ffn_kan_sl_W1", "L0_ffn_kan_sl_b1"]
    arrays, args = {}, []
    for name in names:
        a = np.ascontiguousarray(inputs[name])
        arrays[name] = a
        args.append(nc.dram_tensor(name, a.shape, mybir.dt.from_np(a.dtype), kind="ExternalInput").ap())
    arrays["grid"] = np.linspace(GRID_LO, GRID_HI, G).astype(np.float32)
    args.append(nc.dram_tensor("grid", (G,), F32, kind="ExternalInput").ap())
    args.append(nc.dram_tensor("result", (B, T, D), F32, kind="ExternalOutput").ap())
    transformer_kernel(nc, *args)
    return run(nc, [arrays], core_ids=[0]).results[0]["result"]
```

```python
from contextlib import ExitStack

import concourse.bass as bass
from concourse import mybir

ALU = mybir.AluOpType
ACT = mybir.ActivationFunctionType
AX = mybir.AxisListType
F32 = mybir.dt.float32
F16 = mybir.dt.float16
BF16 = mybir.dt.bfloat16
I32 = mybir.dt.int32

P = 128
B, T, D = 8, 512, 128
H, DH, FEAT = 16, 8, 16
NT = T // P
WIN = 64
WQ = P + WIN
HG = 4
NHG = H // HG
LN_EPS, RMS_EPS, LIN_EPS = 1e-5, 1e-6, 1e-6
NEG = -1e30

E, E2 = 8, 4
F, F2, G = 512, 256, 8
TS = 512
Q4 = TS // P
SIGS = 4
STEPS = (G, 2 * G)
RECS = 4
TOK = B * T
TILES = 20
ENTRIES = TILES + 3
GRID_LO, GRID_HI = -1.2, 0.2

KR = 3 * DH
SHIFT_ROW = KR

FRONT = ["hT", "q", "k", "u", "v"]
RING_STEPS = FRONT + ["max", "lin", "win", "mT", "ytr", "ycT", "out", "h2T", "logit", "rank", "total"]
SPLIT = ["q", "k", "u"]
SLOTS = 3


def batch_steps(u, tail, front):
    steps = [("begin", 0, 0, u)]
    maxima = [("max", hg, c, u) for hg in range(NHG) for c in range(NT)]

    def put(n, share, extra):
        for j in range(6):
            steps.append(("lin", n, j, u))
            if share > j:
                steps.append(maxima.pop(0))
            steps.extend(extra.get(j, []))

    def t(*names):
        return [(x.rstrip("3"), 3 if x == "ytr3" else 0, 0, u - 1) for x in names] if tail else []

    def f(*names):
        return [(x, 0, 0, u) for x in names] if front else []

    put(0, 6, {1: t("ytr3"), 4: t("ycT")})
    put(1, 5, {0: t("out"), 1: f("stats"), 2: t("coef2"), 3: f("aggr"), 4: t("h2norm"), 5: [("pv", 0, 0, u)] + f("coef")})
    put(2, 5, {0: t("h2T"), 3: f("normed"), 4: t("logit"), 5: [("pv", 1, 0, u)] + f("hT")})
    steps.append(("mT", 0, 0, u))
    put(3, 0, {0: f("q"), 2: t("gapexp") + f("k"), 3: t("rank") + f("u"), 4: t("total"),
               5: [("pv", 2, 0, u)] + f("v") + [("ytr", 0, 0, u)] + f("stacks")})
    for n in range(NHG, 2 * NHG):
        steps.extend(("win", n, c, u) for c in range(NT))
        steps.append(("pv", n - 1, 0, u))
        if n == 4:
            steps.extend(t("scatter") + f("residual"))
        if n in (4, 6):
            steps.append(("ytr", n // 2 - 1, 0, u))
        if n == 6:
            steps.extend(f("xload"))
    steps.append(("pv", 7, 0, u))
    assert not maxima
    return steps


TAIL = [("ytr", 3), ("ycT", 0), ("out", 0), ("coef2", 0), ("h2norm", 0), ("h2T", 0), ("logit", 0), ("gapexp", 0),
        ("rank", 0), ("total", 0), ("scatter", 0)]
FIRST = batch_steps(0, False, True)
TURN = batch_steps(1, True, True) + batch_steps(2, True, True)
LAST = batch_steps(1, True, False) + [(step, n, 0, 1) for step, n in TAIL]
TURNS = B // 2 - 1


def numbered(steps, job):
    jobs = {}
    for entry in steps:
        if entry[0] in RING_STEPS:
            jobs[entry] = job
            job += 1
    return jobs, job


JOBS_FIRST, LOOP_JOB = numbered(FIRST, len(FRONT))
JOBS_TURN, _end = numbered(TURN, LOOP_JOB)
JOBS_LAST, _ = numbered(LAST, LOOP_JOB)
PER_TURN = _end - LOOP_JOB
assert PER_TURN % SLOTS == 0
USES = PER_TURN // SLOTS


def transformer_kernel(nc, x, norm_w, Wq, Wk, Wv, Wqf, Wkf, Wout, gate_W, mW1, mb1, mW2, mb2,
                       g0, b0, kW0, kb0, g1, b1, kW1, kb1, grid, out):
    with ExitStack() as ctx:
        def sb(name, shape, dt=F32):
            return ctx.enter_context(nc.sbuf_tensor(name, shape, dt))

        def sem(name):
            return ctx.enter_context(nc.semaphore(name))

        identf = sb("identf", [P, P])
        identb = sb("identb", [P, P], BF16)
        mask_max = sb("mask_max", [P, 2, WQ], BF16)
        mask_win = sb("mask_win", [P, 2, WQ], BF16)
        mask_lin = sb("mask_lin", [P, P])
        block = sb("block", [P, P])
        consts = sb("consts", [P, 5, NT])
        w_raw = sb("w_raw", [P, 3, D])
        w_n = sb("w_n", [P, 4, D])
        w_T = sb("w_T", [P, D])
        w_u = sb("w_u", [P, D])
        qf_rep = sb("qf_rep", [FEAT, H, DH])
        kf_rep = sb("kf_rep", [FEAT, H, DH])
        qf_in = sb("qf_in", [FEAT, DH])
        kf_in = sb("kf_in", [FEAT, DH])
        m_blk = sb("m_blk", [P, P])
        nw = sb("nw", [P, 1])
        wout = sb("wout", [P, 2, D])
        gate = sb("gate", [P, 8])
        ones16 = sb("ones16", [H, T], F16)
        zeros16 = sb("zeros16", [H, T], F16)
        xb = sb("xb", [P, NT, D])
        res = sb("res", [P, 2, NT, D])
        stack = [[sb(f"stack{s}{u}", [P, H * T], F16) for s in range(3)] for u in range(2)]
        vaug = sb("vaug", [P, 2, NT, H, 16])
        stats = sb("stats", [P, NT, 6])
        stats2 = sb("stats2", [P, NT, 6])
        stats2c = sb("stats2c", [P, 1])
        mv = sb("mv", [P, NT, 2])
        mv2 = sb("mv2", [P, NT, 2])
        c1 = sb("c1", [P, 9, NT])
        c2 = sb("c2", [P, 9, NT])
        hn = sb("hn", [P, NT, D])
        hT = sb("hT", [P, T])
        hi = sb("hi", [P, 3, T], F16)
        lo = sb("lo", [P, 3, T], F16)
        negm = sb("negm", [P, NT, H])
        mT16 = sb("mT16", [H, T], F16)
        Pb = sb("Pb", [P, 2, 5120])
        y_sb = sb("y_sb", [P, 2, 2, T])
        rz4 = sb("rz", [P, 4, 32])
        ycat = sb("ycat", [P, NT, 2, D])
        ycT = sb("ycT", [P, 2, T])
        h2 = sb("h2", [P, NT, D])
        n2 = sb("n2", [P, NT, D])
        h2T = sb("h2T", [P, T])
        upper = sb("upper", [P, P], BF16)
        ones_bf = sb("ones_bf", [P, P], BF16)
        prefer = sb("prefer", [P, NT, E])
        first_slot = sb("first_slot", [P, E])
        lg = sb("lg", [P, 8, NT, E])
        sc = sb("sc", [P, 12, NT])
        sel = sb("sel", [P, NT, E], BF16)
        carry = sb("carry", [P, E])
        pos = sb("pos", [P, NT, 2], I32)
        ids_f = sb("ids_f", [P, NT])
        rec = sb("rec", [P, NT, 2, 2], I32)
        tile_idx = sb("tile_idx", [1, 2, 2, ENTRIES])
        tile_idx4 = sb("tile_idx4", [1, 2, ENTRIES])
        tab_e = sb("tab_e", [1, 8, 2, E2])
        tab_i = sb("tab_i", [1, 3, 2, ENTRIES], I32)
        cnt_i = sb("cnt_i", [1, 2, 2, E2], I32)
        n_i = sb("n_i", [1, 2], I32)
        kp_raw = sb("kp_raw", [P, E2, 6])
        kp_all = sb("kp_all", [P, E2, 27])
        grid_sb = sb("grid_sb", [P, G])
        pad_rec = Pb[:, 0, 0:2 * E * TOK // P].bitcast(I32)
        zero_rows = Pb[:, 0, 512:512 + TS * D // P]
        KB, BIASES = E2 * (F2 + D) // P, E2 * (F2 + 2 * D) // P
        bias_in = Pb[:, 0, 1024:1024 + BIASES]
        bias_rest = Pb[:, 0, 1088:1088 + 2 * BIASES].rearrange("p (r n) -> p r n", r=2)
        bias3 = Pb[:, 0, 1152:1152 + 3 * BIASES // 2].bitcast(BF16).rearrange("p (c n) -> p c n", c=3)
        kprm = sb("kprm", [P, RECS, 27])
        mprm = sb("mprm", [P, RECS, F // P])
        mbias = sb("mbias", [3, 2, D], BF16)
        grec = sb("grec", [P, 2, RECS, Q4, 2], I32)
        srec = sb("srec", [P, 2, RECS, Q4, 2], I32)
        zst = sb("zst", [P, Q4, 6])
        zmv = sb("zmv", [P, Q4, 2])
        zc = sb("zc", [P, 6, Q4])
        kconst = sb("kconst", [P, 3, Q4])
        space = [stack[u][m][:].bitcast(F32) for u in range(2) for m in range(3)]
        space += [Pb[:, 0, 0:4096], Pb[:, 1, 0:4096]]
        kbias = [Pb[0:3, 0, 4096 + (F2 + D) // 2 * r:4096 + (F2 + D) // 2 * (r + 1)].bitcast(BF16) for r in range(RECS)]
        kw = [space[0], space[1]]
        basis = [space[2 + z].rearrange("p (r n) -> p r n", r=G) for z in range(2)]
        sig = [space[4][:, 2048 * z:2048 * (z + 1)].rearrange("p (r n) -> p r n", r=SIGS) for z in range(2)]
        k_rows, m_rows = (space[5][:, 2048 * z:2048 * z + 1024].rearrange("p (a q d) -> p a q d", a=2, q=Q4)
                          for z in range(2))
        k_res, m_res = (space[5][:, 2048 * z + 1024:2048 * (z + 1)].rearrange("p (a q d) -> p a q d", a=2, q=Q4)
                        for z in range(2))
        zn = space[6][:, 0:Q4 * F2].rearrange("p (q f) -> p q f", q=Q4)
        mw = [space[6][:, 1024 * (1 + z):1024 * (2 + z)] for z in range(2)]
        mxs = space[6][:, 3072:3072 + TS]
        gelu = space[7].rearrange("p (r n) -> p r n", r=2 * (F // P))

        ring = ctx.enter_context(nc.psum_tensor("ring", [P, SLOTS, 2, 512], F32))
        pv = ctx.enter_context(nc.psum_tensor("pv", [P, 2, 512], F32))

        hl_d = nc.dram_tensor("hl_d", [2, P, 3, T], F16, kind="Internal").ap()
        h2_d = nc.dram_tensor("h2_d", [TOK + TS, D], F32, kind="Internal").ap()
        n2_d = nc.dram_tensor("n2_d", [TOK + TS, D], F32, kind="Internal").ap()
        acc_d = nc.dram_tensor("acc_d", [TOK + TS, D], F32, kind="Internal").ap()
        slot_d = nc.dram_tensor("slot_d", [E * TOK, 2], I32, kind="Internal").ap()
        kp_d = nc.dram_tensor("kp_d", [E2, P, 27], F32, kind="Internal").ap()
        kb0_d = nc.dram_tensor("kb0_d", [3, E2 * F2], BF16, kind="Internal").ap()
        kb1_d = nc.dram_tensor("kb1_d", [3, E2 * D], BF16, kind="Internal").ap()
        mb_d = nc.dram_tensor("mb_d", [3, E2 * D], BF16, kind="Internal").ap()

        filled = [sem(f"filled{s}") for s in range(SLOTS)]
        freed = [sem(f"freed{s}") for s in range(SLOTS)]
        w_loaded = sem("w_loaded")
        x_loaded = sem("x_loaded")
        const_ready = sem("const_ready")
        wout_loaded = sem("wout_loaded")
        zeroed = sem("zeroed")
        stacks_zeroed = sem("stacks_zeroed")
        ones_column = sem("ones_column")
        pv_zeroed = sem("pv_zeroed")
        act_prep = sem("act_prep")
        prep_mm = sem("prep_mm")
        prep_dve = sem("prep_dve")
        pool_chain = sem("pool_chain")
        dve_chain = sem("dve_chain")
        stats_ready = sem("stats_ready")
        coef_ready = sem("coef_ready")
        hn_ready = sem("hn_ready")
        xres_ready = sem("xres_ready")
        hT_ready = sem("hT_ready")
        hi_ready = sem("hi_ready")
        lo_ready = sem("lo_ready")
        v_ready = sem("v_ready")
        hl_stored = sem("hl_stored")
        stack_loaded = [sem(f"stack_loaded{u}") for u in range(2)]
        ones_loaded = sem("ones_loaded")
        negm_ready = sem("negm_ready")
        mT_ready = sem("mT_ready")
        mrow_loaded = sem("mrow_loaded")
        dm_ready = sem("dm_ready")
        pd_ready = sem("pd_ready")
        po_ready = sem("po_ready")
        pw_ready = sem("pw_ready")
        pv_done = sem("pv_done")
        y_out = [sem("y_out_dve"), sem("y_out_act")]
        ycat_ready = sem("ycat_ready")
        ycT_ready = sem("ycT_ready")
        x1_ready = sem("x1_ready")
        stats2_ready = sem("stats2_ready")
        coef2_ready = sem("coef2_ready")
        h2_ready = sem("h2_ready")
        n2_ready = sem("n2_ready")
        rows_stored = sem("rows_stored")
        h2T_ready = sem("h2T_ready")
        sel_ready = sem("sel_ready")
        gap_ready = sem("gap_ready")
        exp_ready = sem("exp_ready")
        route_chain = sem("route_chain")
        rec_ready = sem("rec_ready")
        slots_stored = sem("slots_stored")
        slots_done = sem("slots_done")
        pads_ready = sem("pads_ready")
        pads_stored = sem("pads_stored")
        kp_loaded = sem("kp_loaded")
        kp_ready = sem("kp_ready")
        table_ready = sem("table_ready")
        k_w0, k_w1, k_x, m_w1, m_w2, m_x = ([sem(f"{name}_{u}") for u in range(2)] for name in (
            "k_w0", "k_w1", "k_x", "m_w1", "m_w2", "m_x"))
        k_grec, k_srec, m_grec, m_srec = ([sem(f"{name}_{u}") for u in range(RECS)] for name in (
            "k_grec", "k_srec", "m_grec", "m_srec"))
        k_xT, k_hT, k_st2, k_st, k_cf, k_zn, k_y, k_add, k_added = (
            sem(name) for name in ("k_xT", "k_hT", "k_st2", "k_st", "k_cf", "k_zn", "k_y", "k_add", "k_added"))
        k_sig, k_bas, k_mm = ([sem(f"{name}{z}") for z in range(2)] for name in ("k_sig", "k_bas", "k_mm"))
        m_xT, m_xs, m_h, m_g, m_mm, m_y, m_add, m_added = (
            sem(name) for name in ("m_xT", "m_xs", "m_h", "m_g", "m_mm", "m_y", "m_add", "m_added"))
        pool_at = sem("pool_at")
        mlps_done = sem("mlps_done")
        all_added = sem("all_added")
        copied = sem("copied")

        x_rows = x.rearrange("b (t p) d -> b p t d", p=P)
        out_rows, h2_rows, n2_rows = (a[0:TOK].rearrange("(b t p) d -> b p t d", b=B, p=P)
                                      for a in (acc_d, h2_d, n2_d))

        def slot(job):
            return ring[:, job % SLOTS]

        def fill_no(job, i):
            return i * USES + (job // SLOTS + 1)

        def wait_filled(eng, job, i):
            eng.wait_ge(filled[job % SLOTS], fill_no(job, i))

        def wait_freed(eng, job, i):
            if job >= SLOTS or not isinstance(i, int):
                eng.wait_ge(freed[job % SLOTS], i * USES + job // SLOTS)

        def all_batches(eng, run, count=None, per=0):
            run(FIRST, JOBS_FIRST, 0)
            start = count[0] if count else 0
            with eng.Fori(0, TURNS) as i:
                run(TURN, JOBS_TURN, i)
            if count:
                assert count[0] - start == per, count[0] - start
                count[0] = start
            run(LAST, JOBS_LAST, TURNS)
            if count:
                count[0] += TURNS * per

        def batch_no(i, u, per, off):
            return i * (2 * per) + (u * per + off)

        def load_counts(eng):
            eng.wait_ge(table_ready, 1)
            return [eng.value_load(n_i[0:1, kind:kind + 1], min_val=0, max_val=TILES) for kind in range(2)]

        LEAD, LEAD_DMA = 1, 16

        TILE_LEAD = 4

        def tile_no(k, per=1, part=None, back=0):
            return k * per + ((TILE_LEAD - back) * per + (per if part is None else part))

        def tile_lead(eng, *sems):
            for s_, per in sems:
                eng.sem_inc(s_, TILE_LEAD * per)

        def use_no(buffers, i, u, per):
            return i * (RECS // buffers * per) + (u // buffers + 1) * per

        W_DMAS = 6
        PAD_DMAS = 16 * 8
        blk = ctx.enter_context(nc.Block())

        @blk.sync
        def _(sp):
            sp.sem_inc(mrow_loaded, LEAD_DMA)
            sp.sem_inc(rows_stored, LEAD_DMA)
            sp.dma_start(xb[:], x_rows[0]).then_inc(x_loaded, 16)
            for k, w in enumerate((Wq, Wk, Wv)):
                sp.dma_start(w_raw[:, k, :], w).then_inc(w_loaded, 16)
            sp.dma_start(nw[:], norm_w.rearrange("(d a) -> d a", a=1)).then_inc(w_loaded, 16)
            with nc.allow_non_contiguous_dma(reason="two 8x16 matrices, transposed"):
                sp.dma_start(qf_in[:], Wqf.rearrange("d f -> f d")).then_inc(w_loaded, 16)
                sp.dma_start(kf_in[:], Wkf.rearrange("d f -> f d")).then_inc(w_loaded, 16)
            sp.dma_start(wout[:], Wout.rearrange("(k p) n -> p k n", p=P)).then_inc(wout_loaded, 16)
            sp.dma_start(gate[:], gate_W).then_inc(wout_loaded, 16)
            with nc.allow_non_contiguous_dma(reason="a few hundred words"):
                for k, w in enumerate((g0, b0)):
                    sp.dma_start(kp_raw[:, :, k], w.rearrange("e p -> p e")).then_inc(kp_loaded, 16)
                for k, w in enumerate((g1, b1)):
                    for f in range(2):
                        sp.dma_start(kp_raw[:, :, 2 + 2 * k + f], w[:, P * f:P * (f + 1)].rearrange("e p -> p e")
                                     ).then_inc(kp_loaded, 16)
            at = 0
            for rows in (kb0, kb1, mb2):
                n = rows.shape[0] * rows.shape[1] // P
                sp.dma_start(bias_in[:, at:at + n], rows.rearrange("e n -> (e n)").rearrange("(p x) -> p x", p=P)
                             ).then_inc(kp_loaded, 16)
                at += n
            sp.dma_start(grid_sb[:], grid.unsqueeze(0).to_broadcast([P, G])).then_inc(kp_loaded, 16)
            sp.wait_ge(const_ready, 1)
            sp.wait_ge(stacks_zeroed, 2)
            for u in range(2):
                sp.dma_start(stack[u][1][SHIFT_ROW:SHIFT_ROW + 1, :].rearrange("a (h t) -> a h t", h=H),
                             ones16[:]).then_inc(ones_loaded, 16)

            def load_stacks(bf, u):
                sp.wait_ge(lo_ready, bf * 3 + 3)
                sp.dma_start(hl_d[0], hi[:]).then_inc(hl_stored, 16)
                sp.dma_start(hl_d[1], lo[:]).then_inc(hl_stored, 16)
                sp.wait_ge(hl_stored, bf * 32 + 32)
                for s, parts in enumerate(((0, 1, 0), (0, 0, 1), (0, 1, 0))):
                    for g, part in enumerate(parts):
                        sp.dma_start(stack[u][s][DH * g:DH * (g + 1), :].rearrange("d (h t) -> d h t", h=H),
                                     hl_d[part, :, s, :].rearrange("(h d) t -> d h t", d=DH)
                                     ).then_inc(stack_loaded[u], 16)
                sp.dma_start(stack[u][0][SHIFT_ROW:SHIFT_ROW + 1, :].rearrange("a (h t) -> a h t", h=H),
                             zeros16[:]).then_inc(stack_loaded[u], 16)

            load_stacks(0, 0)
            sp.wait_ge(xres_ready, 1)
            sp.dma_start(xb[:], x_rows[1]).then_inc(x_loaded, 16)
            sp.wait_ge(pads_ready, 2)
            sp.dma_start(slot_d.rearrange("(p s) w -> p (s w)", p=P), pad_rec).then_inc(pads_stored, 16)
            for rows in (h2_d, n2_d, acc_d):
                sp.dma_start(rows[TOK:].rearrange("(p t) d -> p (t d)", p=P), zero_rows).then_inc(pads_stored, 16)
            sp.wait_ge(kp_ready, 2)
            sp.dma_start(kp_d.rearrange("e p c -> p e c"), kp_all[:]).then_inc(pads_stored, 16)
            at = 0
            for rows in (kb0_d, kb1_d, mb_d):
                n = rows.shape[1] // P
                sp.dma_start(rows.rearrange("c (p x) -> p c x", p=P), bias3[:, :, at:at + n]).then_inc(pads_stored, 16)
                at += n

            def batches(steps, jobs, i):
                for s, n, j, u in steps:
                    b = i * 2 + u
                    p = u % 2
                    if s == "xload":
                        sp.wait_ge(xres_ready, batch_no(i, u, 1, 2))
                        sp.dma_start(xb[:], x_rows[bass.ds((b + 2) % B, 1)].rearrange(
                            "a p t d -> (a p) t d")).then_inc(x_loaded, 16)
                    if s == "mT":
                        sp.wait_ge(mT_ready, batch_no(i, u, 1, 1))
                        sp.dma_start(stack[p][0][SHIFT_ROW:SHIFT_ROW + 1, :].rearrange("a (h t) -> a h t", h=H),
                                     mT16[:]).then_inc(mrow_loaded, 16)
                    if s == "stacks":
                        sp.wait_ge(pw_ready, batch_no(i, u, 16, LEAD))
                        load_stacks(b + 1, 1 - p)
                    if s == "logit":
                        rows = bass.ds(b, 1)
                        sp.wait_ge(x1_ready, batch_no(i, u, 1, 1))
                        sp.dma_start(out_rows[rows].rearrange("a p t d -> (a p) t d"), res[:, p]
                                     ).then_inc(rows_stored, 16)
                        sp.wait_ge(h2_ready, batch_no(i, u, 1, 1))
                        sp.dma_start(h2_rows[rows].rearrange("a p t d -> (a p) t d"), h2[:]
                                     ).then_inc(rows_stored, 16)
                        sp.wait_ge(n2_ready, batch_no(i, u, 1, 1))
                        sp.dma_start(n2_rows[rows].rearrange("a p t d -> (a p) t d"), n2[:]
                                     ).then_inc(rows_stored, 16)

            all_batches(sp, batches)
            sp.wait_ge(rows_stored, LEAD_DMA + 48 * B)
            sp.wait_ge(x_loaded, 16 * (B + 1))

            n_kind = load_counts(sp)

            def tile_expert(kind, k):
                e = sp.value_load(tab_i[0:1, 1, kind, bass.ds(k, 1)], min_val=kind * E2, max_val=kind * E2 + E2 - 1)
                return bass.ds(e - kind * E2, 1)

            def load_records(kind, i, u, for_gather):
                k = i * RECS + u
                per = E2 * TOK // TS
                at = sp.value_load(tab_i[0:1, 0, kind, bass.ds(k, 1)], min_val=kind * per, max_val=kind * per + per - 1)
                last_use = ((m_xT, k_xT) if for_gather else (m_added, k_added))[kind]
                done = ((m_grec, k_grec) if for_gather else (m_srec, k_srec))[kind][u % RECS]
                sp.wait_ge(last_use, tile_no(k, back=RECS))
                sp.dma_start((grec if for_gather else srec)[:, kind, u % RECS],
                             slot_d.rearrange("(n q p) w -> n p q w", p=P, q=Q4)[bass.ds(at, 1)].rearrange(
                                 "a p q w -> (a p) q w")).then_inc(done, 16)

            for kind in range(2):
                for u in range(3):
                    with sp.If(n_kind[kind] > u):
                        load_records(kind, 0, u, True)
            with sp.Fori(0, TILES // RECS) as i:
                with sp.If(i * RECS < n_kind[0]):
                    for u in range(RECS):
                        k = i * RECS + u
                        w = mw[u % 2]
                        with sp.If(k + 3 < n_kind[0]):
                            load_records(0, i, u + 3, True)
                        with sp.If(k < n_kind[0]):
                            load_records(0, i, u, False)
                            e = tile_expert(0, k)
                            sp.wait_ge(m_g, tile_no(k, F // P, back=2))
                            sp.dma_start(w[:, 0:F], mW1[e].rearrange("a p n -> (a p) n")).then_inc(m_w1[u % 2], 16)
                            with nc.allow_non_contiguous_dma(reason="512 words"):
                                sp.dma_start(mprm[:, u], mb1[e].rearrange("a (f p) -> (a p) f", p=P)
                                             ).then_inc(m_w1[u % 2], 16)
                            sp.wait_ge(m_y, tile_no(k, back=2))
                            sp.dma_start(w[:, F:2 * F].rearrange("p (f n) -> p f n", f=F // P),
                                         mW2[e].rearrange("a (f p) n -> (a p) f n", p=P)).then_inc(m_w2[u % 2], 16)
                            sp.dma_start(mbias[:, u % 2], mb_d.rearrange("c (e n) -> e c n", n=D)[e].rearrange(
                                "a c n -> (a c) n")).then_inc(m_w2[u % 2], 16)
            with sp.Fori(0, TILES // RECS) as i:
                with sp.If(i * RECS < n_kind[1]):
                    for u in range(RECS):
                        k = i * RECS + u
                        w = kw[u % 2]
                        with sp.If(k + 3 < n_kind[1]):
                            load_records(1, i, u + 3, True)
                        with sp.If(k < n_kind[1]):
                            load_records(1, i, u, False)
                            e = tile_expert(1, k)
                            sp.wait_ge(k_zn, tile_no(k, back=2))
                            sp.dma_start(w[:, 0:2048].rearrange("p (g n) -> p g n", g=G),
                                         kW0[e].rearrange("a (p g) n -> (a p) g n", g=G)).then_inc(k_w0[u % 2], 16)
                            sp.dma_start(kprm[:, u], kp_d[e].rearrange("a p c -> (a p) c")).then_inc(k_w0[u % 2], 16)
                            for rows, a_, n in ((kb0_d, 0, F2), (kb1_d, F2, D)):
                                sp.dma_start(kbias[u][:, a_:a_ + n],
                                             rows.rearrange("c (e n) -> e c n", n=n)[e].rearrange("a c n -> (a c) n")
                                             ).then_inc(k_w0[u % 2], 16)
                            sp.wait_ge(k_y, tile_no(k, back=2))
                            sp.dma_start(w[:, 2048:4096].rearrange("p (f x) -> p f x", f=2),
                                         kW1[e].rearrange("a (f p g) n -> (a p) f (g n)", f=2, g=G)
                                         ).then_inc(k_w1[u % 2], 16)
            sp.wait_ge(all_added, 1)
            sp.dma_start(out.rearrange("b t d -> (b t) d"), acc_d[0:TOK]).then_inc(copied, 16)
            sp.wait_ge(copied, 16)

        @blk.gpsimd
        def _(pool):
            count = [0]

            def link(ins, i=0, per=0):
                count[0] += 1
                ins.then_inc(pool_chain, 1)
                pool.wait_ge(pool_chain, i * per + count[0])

            pool.sem_inc(slots_done, LEAD)
            pool.memset(ones16[:], 1.0)
            pool.memset(zeros16[:], 0.0).then_inc(const_ready, 1)
            for k, value in enumerate((-0.5, LN_EPS, RMS_EPS, -1.0, 1.0)):
                pool.memset(consts[:, k, :], value)
            link(pool.memset(identf[:], 0.0))
            link(pool.affine_select(identf[:], identf[:], [[-1, P]], ALU.not_equal, 1.0, base=0,
                                    channel_multiplier=1))
            pool.tensor_copy(identb[:], identf[:])
            link(pool.memset(block[:], 0.5))
            link(pool.affine_select(block[:], block[:], [[-DH, H], [0, DH]], ALU.is_ge, 0.0, base=0,
                                    channel_multiplier=1))
            pool.affine_select(block[:], block[:], [[DH, H], [0, DH]], ALU.is_ge, 0.0, base=DH - 1,
                               channel_multiplier=-1).then_inc(const_ready, 1)
            half, ln_eps, rms_eps, minus, one = (consts[:, k, :] for k in range(5))

            def coefficients(mvt, c, eps2, i, per):
                m, v = mvt[:, :, 0], mvt[:, :, 1]
                link(pool.tensor_tensor(c[:, 4, :], v, ln_eps, ALU.add), i, per)
                link(pool.tensor_tensor(c[:, 0, :], c[:, 4, :], half, ALU.pow), i, per)
                pool.tensor_tensor(c[:, 8, :], c[:, 0, :], one, ALU.add)
                link(pool.tensor_tensor(c[:, 5, :], v, c[:, 0, :], ALU.mult), i, per)
                link(pool.tensor_tensor(c[:, 6, :], c[:, 5, :], c[:, 0, :], ALU.mult), i, per)
                link(pool.tensor_tensor(c[:, 7, :], c[:, 6, :], eps2, ALU.add), i, per)
                link(pool.tensor_tensor(c[:, 4, :], c[:, 7, :], half, ALU.pow), i, per)
                link(pool.tensor_tensor(c[:, 2, :], c[:, 4, :], c[:, 0, :], ALU.mult), i, per)
                link(pool.tensor_tensor(c[:, 5, :], m, c[:, 0, :], ALU.mult), i, per)
                link(pool.tensor_tensor(c[:, 1, :], c[:, 5, :], minus, ALU.mult), i, per)
                return pool.tensor_tensor(c[:, 3, :], c[:, 1, :], c[:, 4, :], ALU.mult)

            def front_coefficients(bf, i, per):
                pool.wait_ge(stats_ready, bf + 1)
                coefficients(mv, c1, rms_eps, i, per).then_inc(coef_ready, 1)

            front_coefficients(0, 0, 0)
            link(pool.memset(mask_max[:], 0.0))
            link(pool.affine_select(mask_max[:], mask_max[:], [[0, 2], [1, WQ]], ALU.is_ge, NEG, base=0,
                                    channel_multiplier=-1))
            link(pool.affine_select(mask_max[:], mask_max[:], [[0, 2], [-1, WQ]], ALU.is_ge, NEG, base=WIN,
                                    channel_multiplier=1))
            link(pool.memset(mask_win[:], 0.0))
            link(pool.affine_select(mask_win[:], mask_win[:], [[0, 2], [1, WQ]], ALU.is_ge, NEG, base=0,
                                    channel_multiplier=-1))
            link(pool.affine_select(mask_win[:], mask_win[:], [[0, 2], [-1, WQ]], ALU.is_ge, NEG, base=WIN,
                                    channel_multiplier=1))
            link(pool.memset(mask_lin[:], 1.0))
            pool.affine_select(mask_lin[:], mask_lin[:], [[1, P]], ALU.is_ge, 0.0, base=0,
                               channel_multiplier=-1).then_inc(const_ready, 1)

            pool.memset(zero_rows, 0.0)
            pool.memset(ones_bf[:], 1.0)
            for k, value in enumerate((16.0, -4.0, LN_EPS)):
                pool.memset(kconst[:, k, :], value)
            pool.iota(pad_rec.rearrange("p (s w) -> p s w", w=2)[:, :, 0], [[1, E * TOK // P]], base=0,
                      channel_multiplier=E * TOK // P)
            pool.iota(rec[:, :, 0, 0], [[P, NT]], base=0, channel_multiplier=1)
            for row in range(2):
                pool.iota(tab_i[:, row], [[row * E2 * TOK // TS, 2], [1, ENTRIES]], base=0, channel_multiplier=0)
            link(pool.memset(upper[:], 1.0))
            pool.affine_select(upper[:], upper[:], [[1, P]], ALU.is_gt, 0.0, base=0, channel_multiplier=-1)
            for e in range(E):
                pool.memset(prefer[:, :, e:e + 1], float(E - e))
                pool.memset(first_slot[:, e:e + 1], float(e * TOK))
            last = pool.memset(carry[:, 0:1], 0.0)
            last.then_inc(pads_ready, 1)
            POOL_PER = 36

            def batches(steps, jobs, i):
                for s, n, j, u in steps:
                    b = i * 2 + u
                    if s == "lin" and j < 2:
                        pool.wait_ge(dm_ready, batch_no(i, u, 8, 2 * n + j + 1))
                        pd = Pb[:, n % 2, 1024 * j:1024 * (j + 1)]
                        pool.tensor_tensor(pd, pd, pd, ALU.mult).then_inc(pd_ready, 1)
                    if s == "coef":
                        front_coefficients(b + 1, i, POOL_PER)
                    if s == "coef2":
                        pool.wait_ge(stats2_ready, batch_no(i, u, 1, 1))
                        coefficients(mv2, c2, ln_eps, i, POOL_PER).then_inc(coef2_ready, 1)
                    if s == "scatter":
                        pool.wait_ge(rec_ready, batch_no(i, u, 1, 1))
                        pool.sem_inc(pool_at, 1)
                        for t in range(NT):
                            for c in range(2):
                                pool.indirect_dma_start(
                                    slot_d, bass.IndirectOffsetOnAxis(ap=pos[:, t, c:c + 1], axis=0),
                                    rec[:, t, c, :], None).then_inc(slots_stored, 16)
                        pool.wait_ge(slots_stored, batch_no(i, u, 128, 128))
                        pool.sem_inc(slots_done, 1)

            all_batches(pool, batches, count, POOL_PER)

            n_kind = load_counts(pool)
            pool.wait_ge(rows_stored, LEAD_DMA + 48 * B)
            pool.wait_ge(pads_stored, PAD_DMAS)
            tile_lead(pool, (m_added, 1), (k_added, 1), (k_cf, 6))

            def gather(kind, i, u):
                source, rec_sem, xT_sem, x_sem, dst = ((h2_d, m_grec, m_xT, m_x, m_rows),
                                                       (n2_d, k_grec, k_xT, k_x, k_rows))[kind]
                pool.wait_ge(rec_sem[u % RECS], use_no(RECS, i, u, 16))
                pool.wait_ge(xT_sem, tile_no(i * RECS + u, back=2))
                pool.sem_inc(pool_at, 1)
                for q in range(Q4):
                    pool.indirect_dma_start(dst[:, u % 2, q, :], None, source, bass.IndirectOffsetOnAxis(
                        ap=grec[:, kind, u % RECS, q, 0:1], axis=0)).then_inc(x_sem[u % 2], 16)

            def scatter_add(kind, i, u):
                y_sem, add_sem, added, src = ((m_y, m_add, m_added, m_res), (k_y, k_add, k_added, k_res))[kind]
                k = i * RECS + u
                pool.wait_ge(y_sem, tile_no(k))
                pool.sem_inc(pool_at, 1)
                for q in range(Q4):
                    pool.indirect_dma_start(acc_d, bass.IndirectOffsetOnAxis(ap=srec[:, kind, u, q, 0:1], axis=0),
                                            src[:, u % 2, q, :], None, compute_op=ALU.add).then_inc(add_sem, 16)
                pool.wait_ge(add_sem, k * 64 + 64)
                pool.sem_inc(added, 1)

            def hidden_coefficients(i, u):
                k = i * RECS + u
                pool.wait_ge(k_st, tile_no(k))
                for c, (a, b_, op) in enumerate((
                        (zmv[:, :, 1], kconst[:, 0, :], ALU.mult), (zc[:, 0, :], kconst[:, 2, :], ALU.add),
                        (zc[:, 1, :], half, ALU.pow), (zc[:, 2, :], kconst[:, 1, :], ALU.mult),
                        (zmv[:, :, 0], zc[:, 3, :], ALU.mult), (zc[:, 4, :], minus, ALU.mult))):
                    pool.tensor_tensor(zc[:, c, :], a, b_, op).then_inc(k_cf, 1)
                    if c < 5:
                        pool.wait_ge(k_cf, tile_no(k, 6, c + 1))

            for u in range(2):
                with pool.If(n_kind[0] > u):
                    gather(0, 0, u)
            with pool.If(n_kind[0] > 2):
                gather(0, 0, 2)
            for u in range(2):
                with pool.If(n_kind[1] > u):
                    gather(1, 0, u)
            with pool.Fori(0, TILES // RECS) as i:
                with pool.If(i * RECS < n_kind[0]):
                    for u in range(RECS):
                        k = i * RECS + u
                        with pool.If(k + 3 < n_kind[0]):
                            gather(0, i, u + 3)
                        with pool.If(k < n_kind[0]):
                            scatter_add(0, i, u)
            with pool.If(n_kind[1] > 0):
                hidden_coefficients(0, 0)
            with pool.If(n_kind[1] > 2):
                gather(1, 0, 2)
            with pool.Fori(0, TILES // RECS) as i:
                with pool.If(i * RECS < n_kind[1]):
                    for u in range(RECS):
                        k = i * RECS + u
                        with pool.If(k + 1 < n_kind[1]):
                            hidden_coefficients(i, u + 1)
                        with pool.If(k + 3 < n_kind[1]):
                            gather(1, i, u + 3)
                        with pool.If(k < n_kind[1]):
                            scatter_add(1, i, u)
            pool.sem_inc(all_added, 1)

        @blk.scalar
        def _(act):
            act.sem_inc(pw_ready, LEAD)
            act.sem_inc(y_out[1], LEAD)
            act.wait_ge(zeroed, 1)
            for m in range(3):
                last = act.activation(stack[1][m][:].bitcast(F32), stack[0][0][:].bitcast(F32), ACT.Copy)
            last.then_inc(stacks_zeroed, 1)
            act.wait_ge(prep_mm, 1)
            act.activation(w_T[:], slot(0)[:, 0, 0:D], ACT.Copy).then_inc(act_prep, 1)
            act.wait_ge(prep_mm, 2)
            act.activation(w_u[:], slot(1)[:, 0, 0:D], ACT.Copy).then_inc(act_prep, 1)

            def front(s, bf, u, job, i):
                wait_filled(act, job, i)
                src = slot(job)
                if s == "hT":
                    act.activation(hT[:], src[:, 0, :], ACT.Copy).then_inc(freed[job % SLOTS], 1)
                if s in SPLIT:
                    if s == "q" and not (isinstance(bf, int) and bf == 0):
                        act.wait_ge(hl_stored, bf * 32)
                    act.activation(hi[:, SPLIT.index(s), :], src[:, 0, :], ACT.Copy).then_inc(hi_ready, 1)
                if s == "v":
                    act.wait_ge(ones_column, 1)
                    act.activation(vaug[:, u, :, :, 0:DH], src[:, 0, :].rearrange(
                        "p (t h d) -> p t h d", t=NT, h=H), ACT.Copy).then_inc(freed[job % SLOTS], 1)

            for s in FRONT:
                front(s, 0, 0, FRONT.index(s), 0)
            act.wait_ge(pads_stored, PAD_DMAS)
            def batches(steps, jobs, i):
                for s, n, j, u in steps:
                    b = i * 2 + u
                    p = u % 2
                    if s in FRONT:
                        front(s, b + 1, 1 - p, jobs[(s, n, 0, u)], i)
                    if s == "mT":
                        job = jobs[(s, n, 0, u)]
                        wait_filled(act, job, i)
                        act.wait_ge(mrow_loaded, batch_no(i, u, 16, LEAD_DMA))
                        act.activation(mT16[:], slot(job)[0:H, 0, :], ACT.Copy).then_inc(mT_ready, 1)
                        act.wait_ge(mT_ready, batch_no(i, u, 1, 1))
                        act.sem_inc(freed[job % SLOTS], 1)
                    if s == "lin" and j >= 2:
                        for hd in (j - 2,):
                            job = jobs[(s, n, j, u)]
                            wait_filled(act, job, i)
                            if hd == 0 and n >= 2:
                                act.wait_ge(pv_done, batch_no(i, u, 8, LEAD + n - 1))
                            act.activation(Pb[:, n % 2, 2048 + 768 * hd:2048 + 768 * (hd + 1)].rearrange(
                                "p (k q) -> p k q", k=2), slot(job)[:, :, 0:384], ACT.Square,
                                bias=1.0).then_inc(freed[job % SLOTS], 1)
                    if s == "win":
                        for c in (j,):
                            job = jobs[(s, n, c, u)]
                            wq = WQ if c < NT - 1 else P
                            wait_filled(act, job, i)
                            if c == 0:
                                act.wait_ge(pv_done, batch_no(i, u, 8, LEAD + n - 1))
                            act.activation(
                                Pb[:, n % 2, 768 * c:768 * (c + 1)].rearrange(
                                    "p (k j q) -> p k j q", k=2, j=2)[:, :, :, 0:wq],
                                slot(job)[:, :, 0:384].rearrange("p k (j q) -> p k j q", j=2)[:, :, :, 0:wq],
                                ACT.Exp).then_inc(pw_ready, 1)
                            act.wait_ge(pw_ready, batch_no(i, u, 16, LEAD + 4 * (n - 4) + c + 1))
                            act.sem_inc(freed[job % SLOTS], 1)
                    if s == "pv" and n % 2 == 1:
                        act.wait_ge(pv_done, batch_no(i, u, 8, LEAD + n + 1))
                        act.activation(y_sb[:, (n // 2) % 2, 1, :], pv[:, 1, :], ACT.Copy
                                       ).then_inc(y_out[1], 1)
                    if s in ("ycT", "h2T"):
                        job = jobs[(s, n, 0, u)]
                        wait_filled(act, job, i)
                        if s == "ycT":
                            act.activation(ycT[:], slot(job)[:], ACT.Copy).then_inc(freed[job % SLOTS], 1)
                        else:
                            act.activation(h2T[:], slot(job)[:, 0, :], ACT.Copy).then_inc(freed[job % SLOTS], 1)
                    if s == "gapexp":
                        act.wait_ge(gap_ready, batch_no(i, u, 1, 1))
                        act.activation(sc[:, 7, :], sc[:, 6, :], ACT.Exp).then_inc(exp_ready, 1)

            all_batches(act, batches)

            n_kind = load_counts(act)
            tile_lead(act, (m_g, F // P), (k_sig[0], G), (k_sig[1], 2 * G))

            def hidden(i, u):
                k = i * RECS + u
                act.wait_ge(m_w1[u % 2], use_no(2, i, u, 32))
                act.wait_ge(m_mm, tile_no(k, back=2))
                for f in range(F // P):
                    act.wait_ge(m_h, tile_no(k, F // P, f + 1))
                    act.activation(gelu[:, 4 * (u % 2) + f, :], ring[:, f // 2, f % 2, :], ACT.Gelu,
                                   bias=mprm[:, u % RECS, f:f + 1]).then_inc(m_g, 1)

            with act.If(n_kind[0] > 0):
                hidden(0, 0)
            with act.Fori(0, TILES // RECS) as i:
                with act.If(i * RECS < n_kind[0]):
                    for u in range(RECS):
                        k = i * RECS + u
                        with act.If(k + 1 < n_kind[0]):
                            hidden(i, u + 1)

            def sigmoids(z, i, u):
                k = i * RECS + u
                if z == 0:
                    act.wait_ge(k_w0[u % 2], use_no(2, i, u, 64))
                    act.wait_ge(k_xT, tile_no(k))
                else:
                    act.wait_ge(k_hT, tile_no(k))
                for g in range(STEPS[z]):
                    f = g // G
                    act.wait_ge(k_bas[z], tile_no(k, STEPS[z], g + 1 - SIGS))
                    prm = kprm[:, u % RECS]
                    if z == 0:
                        src, scale, bias = pv[:, 0, :], prm[:, 0:1], prm[:, 1 + g:2 + g]
                    else:
                        src, scale, bias = ring[:, 1, f, :], prm[:, 9 + f:10 + f], prm[:, 11 + g:12 + g]
                    act.activation(sig[z][:, g % SIGS, :], src, ACT.Sigmoid, bias=bias, scale=scale
                                   ).then_inc(k_sig[z], 1)

            for u in range(2):
                with act.If(n_kind[1] > u):
                    sigmoids(0, 0, u)
            with act.Fori(0, TILES // RECS) as i:
                with act.If(i * RECS < n_kind[1]):
                    for u in range(RECS):
                        k = i * RECS + u
                        with act.If(k < n_kind[1]):
                            sigmoids(1, i, u)
                        with act.If(k + 2 < n_kind[1]):
                            sigmoids(0, i, u + 2)

        @blk.vector
        def _(dve):
            count = [0]

            def link(ins, i=0, per=0):
                count[0] += 1
                ins.then_inc(dve_chain, 1)
                dve.wait_ge(dve_chain, i * per + count[0])

            def norm_stats(bf, u):
                dve.wait_ge(x_loaded, bf * 16 + 16)
                return [dve.bn_stats(stats[:, t, :], xb[:, t, :]) for t in range(NT)][-1]

            def aggregate(st, m):
                return [dve.bn_aggr(m[:, t, :], st[:, t, :]) for t in range(NT)][-1]

            dve.sem_inc(y_out[0], LEAD)
            dve.memset(stack[0][0][:].bitcast(F32), 0.0).then_inc(zeroed, 1)
            link(norm_stats(0, 0))
            aggregate(stats, mv).then_inc(stats_ready, 1)
            dve.wait_ge(zeroed, 1)
            for m in range(1, 3):
                last = dve.tensor_copy(stack[0][m][:], stack[0][0][:])
            last.then_inc(stacks_zeroed, 1)

            dve.wait_ge(w_loaded, 16 * W_DMAS)
            dve.wait_ge(const_ready, 2)
            dve.tensor_copy(qf_rep[:], qf_in[:].unsqueeze(1).to_broadcast([FEAT, H, DH]))
            dve.tensor_copy(kf_rep[:], kf_in[:].unsqueeze(1).to_broadcast([FEAT, H, DH]))
            dve.tensor_scalar(w_n[:, 0, :], w_raw[:, 0, :], nw[:], DH ** -0.5, ALU.mult, ALU.mult)
            dve.tensor_scalar(w_n[:, 1, :], w_raw[:, 1, :], nw[:], None, ALU.mult)
            dve.tensor_scalar(w_n[:, 2, :], w_raw[:, 2, :], nw[:], None, ALU.mult)
            dve.tensor_scalar(w_n[:, 3, :], w_raw[:, 0, :], nw[:], None, ALU.mult).then_inc(prep_dve, 1)
            dve.wait_ge(prep_mm, 1)
            dve.tensor_tensor(m_blk[:], slot(0)[:, 1, 0:P], block[:], ALU.mult).then_inc(prep_dve, 1)

            def front(s, bf, u, job, i):
                wait_filled(dve, job, i)
                m = SPLIT.index(s)
                dve.wait_ge(hi_ready, bf * 3 + m + 1)
                dve.tensor_tensor(lo[:, m, :], slot(job)[:, 0, :], hi[:, m, :], ALU.subtract
                                  ).then_inc(lo_ready, 1)
                dve.wait_ge(lo_ready, bf * 3 + m + 1)
                dve.sem_inc(freed[job % SLOTS], 1)

            def normed(bf, u):
                dve.wait_ge(coef_ready, bf + 1)
                for t in range(NT):
                    last = dve.tensor_scalar(hn[:, t, :], xb[:, t, :], c1[:, 2, t:t + 1],
                                             c1[:, 3, t:t + 1], ALU.mult, ALU.add)
                last.then_inc(hn_ready, 1)

            def residual(bf, u):
                for t in range(NT):
                    last = dve.tensor_scalar(res[:, u, t, :], xb[:, t, :], c1[:, 8, t:t + 1],
                                             c1[:, 1, t:t + 1], ALU.mult, ALU.add)
                last.then_inc(xres_ready, 1)

            normed(0, 0)
            for s in FRONT:
                if s in SPLIT:
                    front(s, 0, 0, FRONT.index(s), 0)
            residual(0, 0)
            link(dve.memset(vaug[:], 0.0))
            dve.memset(vaug[:, :, :, :, DH:DH + 1], 1.0).then_inc(ones_column, 1)
            dve.memset(pv[:], 0.0).then_inc(pv_zeroed, 1)
            dve.wait_ge(pads_ready, 1)
            pads = pad_rec.rearrange("p (s w) -> p s w", w=2)
            link(dve.tensor_scalar(pads[:, :, 0], pads[:, :, 0], TS - 1, None, ALU.bitwise_and))
            dve.tensor_scalar(pads[:, :, 1], pads[:, :, 0], 0.0, None, ALU.mult)
            dve.tensor_copy(ids_f[:], rec[:, :, 0, 0])
            dve.tensor_copy(carry[:], first_slot[:])
            dve.tensor_copy(tile_idx[:], tab_i[:, 0:2])
            link(dve.tensor_scalar(tile_idx4[:], tab_i[:, 0], -float(Q4), None, ALU.mult))
            dve.tensor_scalar(pads[:, :, 0], pads[:, :, 0], float(TOK), None, ALU.add).then_inc(pads_ready, 1)
            dve.wait_ge(kp_loaded, 16 * 10)
            for e in range(E2):
                dve.tensor_copy(kp_all[:, e, 0:1], kp_raw[:, e, 0:1])
                dve.tensor_copy(kp_all[:, e, 9:11], kp_raw[:, e, 2:4])
                for dst, src in ((1, 1), (11, 4), (19, 5)):
                    last = dve.scalar_tensor_tensor(kp_all[:, e, dst:dst + G], grid_sb[:], -1.0,
                                                    kp_raw[:, e, src:src + 1].to_broadcast([P, G]),
                                                    ALU.mult, ALU.add)
            last.then_inc(kp_ready, 1)
            link(dve.tensor_scalar(bias_in[:, 0:KB], bias_in[:, 0:KB], -0.25, None, ALU.mult))
            link(dve.tensor_copy(bias3[:, 0], bias_in))
            link(dve.tensor_tensor(bias_rest[:, 0], bias_in, bias3[:, 0], ALU.subtract))
            link(dve.tensor_copy(bias3[:, 1], bias_rest[:, 0]))
            link(dve.tensor_tensor(bias_rest[:, 1], bias_rest[:, 0], bias3[:, 1], ALU.subtract))
            dve.tensor_copy(bias3[:, 2], bias_rest[:, 1]).then_inc(kp_ready, 1)
            dve.wait_ge(const_ready, 3)
            dve.wait_ge(pads_stored, PAD_DMAS)
            DVE_PER = 16
            ROUTE = 20

            def batches(steps, jobs, i):
                for s, n, j, u in steps:
                    b = i * 2 + u
                    p = u % 2
                    if s in SPLIT:
                        front(s, b + 1, 1 - p, jobs[(s, n, 0, u)], i)
                    if s == "max":
                        for c in (j,):
                            job = jobs[(s, n, c, u)]
                            wait_filled(dve, job, i)
                            k0 = WIN if c == 0 else 0
                            red = dve.tensor_reduce(
                                negm[:, c, HG * n:HG * (n + 1)].rearrange("p (k j) -> p k j", k=2),
                                slot(job)[:, :, 0:384].rearrange("p k (j q) -> p k j q", j=2)[:, :, :, k0:WQ],
                                AX.X, ALU.max, negate=True)
                            red.then_inc(freed[job % SLOTS], 1)
                    if s == "stats":
                        link(norm_stats(b + 1, 1 - p), i, DVE_PER)
                    if s == "aggr":
                        aggregate(stats, mv).then_inc(stats_ready, 1)
                    if s == "normed":
                        normed(b + 1, 1 - p)
                    if s == "residual":
                        dve.wait_ge(rows_stored, batch_no(i, u, 48, LEAD_DMA))
                        residual(b + 1, 1 - p)
                    if s == "lin" and j < 2:
                        for cp in (j,):
                            job = jobs[(s, n, cp, u)]
                            wait_filled(dve, job, i)
                            if cp == 0 and n < 2:
                                dve.wait_ge(pv_done, batch_no(i, u, 8, LEAD))
                            if cp == 0 and n >= 2:
                                dve.wait_ge(pv_done, batch_no(i, u, 8, LEAD + n - 1))
                            dve.scalar_tensor_tensor(
                                Pb[:, n % 2, 1024 * cp:1024 * (cp + 1)].rearrange("p (a q) -> p a q", q=P),
                                slot(job)[:].rearrange("p k (j q) -> p (k j) q", q=P), 1.0,
                                mask_lin[:].unsqueeze(1).to_broadcast([P, 8, P]), ALU.add, ALU.mult
                            ).then_inc(dm_ready, 1)
                            dve.wait_ge(dm_ready, batch_no(i, u, 8, 2 * n + cp + 1))
                            dve.sem_inc(freed[job % SLOTS], 1)
                    if s == "pv" and n % 2 == 0:
                        dve.wait_ge(pv_done, batch_no(i, u, 8, LEAD + n + 1))
                        dve.tensor_copy(y_sb[:, (n // 2) % 2, 0, :], pv[:, 0, :]).then_inc(y_out[0], 1)
                    if s == "ytr":
                        job = jobs[(s, n, 0, u)]
                        wait_filled(dve, job, i)
                        z = slot(job)[:].rearrange("p k (a c) -> p (k a) c", c=32)[:, :, DH]
                        kind, rz = n // 2, rz4[:, n]
                        if kind == 0:
                            link(dve.tensor_scalar(rz, z, LIN_EPS, None, ALU.add), i, DVE_PER)
                            link(dve.reciprocal(rz, rz), i, DVE_PER)
                        else:
                            link(dve.reciprocal(rz, z), i, DVE_PER)
                        for bk in range(2):
                            hg = (2 * n + bk) % 4
                            last = dve.tensor_tensor(
                                ycat[:, :, kind, 32 * hg:32 * (hg + 1)].rearrange("p t (j d) -> p t j d", j=HG),
                                slot(job)[:, bk, :].rearrange("p (t j c) -> p t j c", t=NT, j=HG)[:, :, :, 0:DH],
                                rz[:, 16 * bk:16 * (bk + 1)].rearrange("p (t j) -> p t j", t=NT).unsqueeze(3)
                                .to_broadcast([P, NT, HG, DH]), ALU.mult)
                        last.then_inc(freed[job % SLOTS], 1)
                    if s == "out":
                        job = jobs[(s, n, 0, u)]
                        wait_filled(dve, job, i)
                        dve.wait_ge(xres_ready, batch_no(i, u, 1, 1))
                        dve.tensor_tensor(res[:, p].rearrange("p t d -> p (t d)"), slot(job)[:, 0, :],
                                          res[:, p].rearrange("p t d -> p (t d)"), ALU.add).then_inc(x1_ready, 1)
                        dve.wait_ge(x1_ready, batch_no(i, u, 1, 1))
                        dve.sem_inc(freed[job % SLOTS], 1)
                        link([dve.bn_stats(stats2[:, t, :], res[:, p, t, :]) for t in range(NT)][-1], i, DVE_PER)
                        dve.tensor_copy(stats2c[:], stats2[:, 0, 0:1])
                        aggregate(stats2, mv2).then_inc(stats2_ready, 1)
                    if s == "h2norm":
                        dve.wait_ge(coef2_ready, batch_no(i, u, 1, 1))
                        dve.wait_ge(rows_stored, batch_no(i, u, 48, LEAD_DMA))
                        for t in range(NT):
                            last = dve.tensor_scalar(h2[:, t, :], res[:, p, t, :], c2[:, 0, t:t + 1],
                                                     c2[:, 1, t:t + 1], ALU.mult, ALU.add)
                        last.then_inc(h2_ready, 1)
                        for t in range(NT):
                            last = dve.tensor_scalar(n2[:, t, :], res[:, p, t, :], c2[:, 2, t:t + 1],
                                                     c2[:, 3, t:t + 1], ALU.mult, ALU.add)
                        last.then_inc(n2_ready, 1)
                    if s == "logit":
                        job = jobs[(s, n, 0, u)]
                        wait_filled(dve, job, i)
                        step = [0]

                        def chain(ins, wait=True):
                            step[0] += 1
                            ins.then_inc(route_chain, 1)
                            if wait:
                                dve.wait_ge(route_chain, batch_no(i, u, ROUTE, step[0]))

                        logit = slot(job)[:, 0, 0:NT * E].rearrange("p (t e) -> p t e", e=E)
                        dve.wait_ge(slots_done, batch_no(i, u, 1, LEAD))
                        dve.tensor_copy(lg[:, 0], logit).then_inc(freed[job % SLOTS], 1)
                        dve.wait_ge(freed[job % SLOTS], fill_no(job, i))

                        def over_e(row):
                            return sc[:, row, :].unsqueeze(2).to_broadcast([P, NT, E])

                        for c in range(2):
                            chain(dve.tensor_reduce(sc[:, c, :], lg[:, c], AX.X, ALU.max))
                            chain(dve.tensor_tensor(lg[:, 2], lg[:, c], over_e(c), ALU.is_equal))
                            chain(dve.tensor_tensor(lg[:, 5], lg[:, 2], prefer[:], ALU.mult))
                            chain(dve.tensor_reduce(sc[:, 2 + c, :], lg[:, 5], AX.X, ALU.max))
                            chain(dve.tensor_tensor(lg[:, 3 + c], prefer[:], over_e(2 + c), ALU.is_equal))
                            if c == 0:
                                chain(dve.scalar_tensor_tensor(lg[:, 1], lg[:, 3], NEG, lg[:, 0], ALU.mult, ALU.add))
                        dve.tensor_tensor(sel[:], lg[:, 3], lg[:, 4], ALU.add).then_inc(sel_ready, 1)
                        dve.tensor_tensor(sc[:, 6, :], sc[:, 1, :], sc[:, 0, :], ALU.subtract).then_inc(gap_ready, 1)
                    if s == "rank":
                        dve.wait_ge(exp_ready, batch_no(i, u, 1, 1))
                        w = rec[:].bitcast(F32)
                        chain(dve.tensor_scalar(sc[:, 8, :], sc[:, 7, :], 1.0, None, ALU.add))
                        chain(dve.reciprocal(w[:, :, 0, 1], sc[:, 8, :]))
                        chain(dve.tensor_tensor(w[:, :, 1, 1], w[:, :, 0, 1], sc[:, 7, :], ALU.mult), False)
                        for c in range(2):
                            dve.tensor_copy(rec[:, :, c, 0], ids_f[:])
                        chain(dve.tensor_scalar(sc[:, 9, :], ids_f[:], float(T), None, ALU.add))
                        chain(dve.tensor_copy(ids_f[:], sc[:, 9, :]), False)
                        job = jobs[(s, n, 0, u)]
                        wait_filled(dve, job, i)
                        dve.tensor_tensor(lg[:, 6], slot(job)[:, 0, 0:NT * E].rearrange("p (t e) -> p t e", e=E),
                                          carry[:].unsqueeze(1).to_broadcast([P, NT, E]), ALU.add
                                          ).then_inc(freed[job % SLOTS], 1)
                        dve.wait_ge(freed[job % SLOTS], fill_no(job, i))
                        for c in range(2):
                            chain(dve.tensor_tensor(lg[:, 5 + 2 * c], lg[:, 6], lg[:, 3 + c], ALU.mult))
                            chain(dve.tensor_reduce(sc[:, 10 + c, :], lg[:, 5 + 2 * c], AX.X, ALU.add))
                        dve.tensor_copy(pos[:].rearrange("p t c -> p c t"), sc[:, 10:12, :]).then_inc(rec_ready, 1)
                        assert step[0] == ROUTE, step[0]
                    if s == "total":
                        job = jobs[(s, n, 0, u)]
                        wait_filled(dve, job, i)
                        dve.tensor_tensor(carry[:], slot(job)[:, 0, 0:E], carry[:], ALU.add
                                          ).then_inc(freed[job % SLOTS], 1)

            all_batches(dve, batches, count, DVE_PER)

            total_job = JOBS_LAST[("total", 0, 0, 1)]
            dve.wait_ge(freed[total_job % SLOTS], fill_no(total_job, TURNS))
            link(dve.tensor_tensor(tab_e[:, 0].rearrange("a k e -> a (k e)"), carry[0:1, :], first_slot[0:1, :],
                                   ALU.subtract))
            dve.tensor_scalar(tab_e[:, 1], tab_e[:, 0], float(P - 1), None, ALU.add)
            link(dve.tensor_scalar(tab_e[:, 2], tab_e[:, 0], float(TS - 1), None, ALU.add))
            link(dve.tensor_copy(cnt_i[:], tab_e[:, 1:3]))
            dve.tensor_scalar(cnt_i[:, 0], cnt_i[:, 0], P.bit_length() - 1, None, ALU.logical_shift_right)
            link(dve.tensor_scalar(cnt_i[:, 1], cnt_i[:, 1], TS.bit_length() - 1, None, ALU.logical_shift_right))
            link(dve.tensor_copy(tab_e[:, 3:5], cnt_i[:]))
            dve.tensor_scalar(tab_e[:, 6], tab_e[:, 4], -1.0, float(TOK // TS), ALU.mult, ALU.add)
            dve.scalar_tensor_tensor(tab_e[:, 7, :, 0:E2 - 1], tab_e[:, 4, :, 0:E2 - 1], float(Q4),
                                     tab_e[:, 3, :, 0:E2 - 1], ALU.mult, ALU.subtract)
            link(dve.tensor_copy(tab_e[:, 5, :, 0:1], tab_e[:, 4, :, 0:1]))
            for e in range(1, E2):
                link(dve.tensor_tensor(tab_e[:, 5, :, e:e + 1], tab_e[:, 5, :, e - 1:e], tab_e[:, 4, :, e:e + 1],
                                       ALU.add))
            link(dve.tensor_tensor(tab_e[:, 7, :, 0:E2 - 1], tab_e[:, 7, :, 0:E2 - 1], tab_e[:, 3, :, 1:E2], ALU.add))
            grid3 = space[4][0:1, 0:3 * 2 * (E2 - 1) * ENTRIES].rearrange(
                "a (r k j t) -> a r k j t", r=3, k=2, j=E2 - 1)
            sums = space[4][0:1, 2048:2048 + 4 * 2 * ENTRIES].rearrange("a (r k t) -> a r k t", r=4, k=2)
            shape = [1, E2 - 1, ENTRIES]
            for kind in range(2):
                last = dve.tensor_tensor(grid3[:, 0, kind], tile_idx[:, 0, kind].unsqueeze(1).to_broadcast(shape),
                                         tab_e[:, 5, kind, 0:E2 - 1].unsqueeze(2).to_broadcast(shape), ALU.is_ge)
            link(last)
            for row in range(2):
                for kind in range(2):
                    last = dve.tensor_tensor(grid3[:, 1 + row, kind], grid3[:, 0, kind],
                                             tab_e[:, 6 + row, kind, 0:E2 - 1].unsqueeze(2).to_broadcast(shape),
                                             ALU.mult)
            link(last)
            for row in range(2):
                for kind in range(2):
                    last = dve.tensor_reduce(sums[:, row, kind], grid3[:, 1 + row, kind].rearrange("a j t -> a t j"),
                                             AX.X, ALU.add)
            link(last)
            dve.tensor_tensor(sums[:, 2], sums[:, 0], tile_idx[:, 1], ALU.add)
            link(dve.tensor_tensor(sums[:, 3], sums[:, 1], tile_idx4[:], ALU.add))
            for kind in range(2):
                dve.tensor_scalar(sums[:, 0, kind], sums[:, 2, kind], float((kind + 1) * E2 * TOK // TS - 1), None, ALU.min)
            link(dve.tensor_tensor(sums[:, 1], sums[:, 3], tab_e[:, 3, :, 0:1].to_broadcast([1, 2, ENTRIES]), ALU.add))
            dve.tensor_copy(tab_i[:, 0], sums[:, 0])
            link(dve.tensor_scalar(sums[:, 2], sums[:, 1], float(Q4), 0.0, ALU.min, ALU.max))
            dve.tensor_scalar(tab_i[:, 1], tab_i[:, 0], (TOK // TS).bit_length() - 1, None, ALU.logical_shift_right)
            dve.tensor_copy(tab_i[:, 2], sums[:, 2])
            link(dve.tensor_copy(n_i[:].unsqueeze(2), tab_e[:, 5, :, E2 - 1:E2]))
            dve.wait_ge(slots_done, LEAD + B)
            dve.sem_inc(table_ready, 1)

            n_kind = load_counts(dve)
            tile_lead(dve, (m_xs, 1), (m_y, 1), (k_y, 1), (k_st2, 1), (k_st, 1), (k_zn, 1), (k_bas[0], G), (k_bas[1], 2 * G))
            weight = srec[:].bitcast(F32)

            def copy_rows(i, u):
                k = i * RECS + u
                dve.wait_ge(m_xT, tile_no(k))
                dve.wait_ge(m_h, tile_no(k, F // P, back=1))
                dve.tensor_copy(mxs, pv[:, 0, :]).then_inc(m_xs, 1)

            def weighted(kind, i, u):
                k = i * RECS + u
                rec_sem, added, mm_sem, per, dst, y_sem = (
                    (m_srec, m_added, m_mm, 1, m_res, m_y), (k_srec, k_added, k_mm[1], 2 * G, k_res, k_y))[kind]
                dve.wait_ge(rec_sem[u], use_no(RECS, i, u, 16))
                dve.wait_ge(added, tile_no(k, back=2))
                dve.wait_ge(mm_sem, tile_no(k, per))
                for q in range(Q4):
                    last = dve.tensor_scalar(dst[:, u % 2, q, :], pv[:, 1, P * q:P * (q + 1)],
                                             weight[:, kind, u, q, 1:2], (1.0, -4.0)[kind], ALU.mult, ALU.mult)
                last.then_inc(y_sem, 1)

            def basis_functions(z, i, u, steps):
                k = i * RECS + u
                for g in steps:
                    dve.wait_ge(k_sig[z], tile_no(k, STEPS[z], g + 1))
                    dve.wait_ge(k_mm[z], tile_no(k, STEPS[z], g + 1 - G))
                    s_ = sig[z][:, g % SIGS, :]
                    dve.scalar_tensor_tensor(basis[z][:, g % G, :], s_, -1.0, s_, ALU.add, ALU.mult
                                             ).then_inc(k_bas[z], 1)

            def z_rows(q):
                return ring[:, 0, q // 2, F2 * (q % 2):F2 * (q % 2 + 1)]

            def hidden_stats(i, u):
                k = i * RECS + u
                dve.wait_ge(k_mm[0], tile_no(k, G))
                for q in range(Q4):
                    last = dve.bn_stats(zst[:, q, :], z_rows(q))
                last.then_inc(k_st2, 1)
                dve.wait_ge(k_st2, tile_no(k))
                dve.tensor_copy(stats2c[:], zst[:, 0, 0:1])
                for q in range(Q4):
                    last = dve.bn_aggr(zmv[:, q, :], zst[:, q, :])
                last.then_inc(k_st, 1)

            def hidden_norm(i, u):
                k = i * RECS + u
                dve.wait_ge(k_cf, tile_no(k, 6))
                dve.wait_ge(k_hT, tile_no(k, back=1))
                for q in range(Q4):
                    last = dve.tensor_scalar(zn[:, q, :], z_rows(q), zc[:, 3, q:q + 1], zc[:, 5, q:q + 1],
                                             ALU.mult, ALU.add)
                last.then_inc(k_zn, 1)

            for u in range(2):
                with dve.If(n_kind[0] > u):
                    copy_rows(0, u)
            with dve.Fori(0, TILES // RECS) as i:
                with dve.If(i * RECS < n_kind[0]):
                    for u in range(RECS):
                        k = i * RECS + u
                        with dve.If(k + 2 < n_kind[0]):
                            copy_rows(i, u + 2)
                        with dve.If(k < n_kind[0]):
                            weighted(0, i, u)
            with dve.If(n_kind[1] > 0):
                basis_functions(0, 0, 0, range(G))
                hidden_stats(0, 0)
                hidden_norm(0, 0)
            with dve.If(n_kind[1] > 1):
                basis_functions(0, 0, 1, range(G))
            with dve.Fori(0, TILES // RECS) as i:
                with dve.If(i * RECS < n_kind[1]):
                    for u in range(RECS):
                        k = i * RECS + u
                        with dve.If(k < n_kind[1]):
                            basis_functions(1, i, u, range(0, G))
                        with dve.If(k + 1 < n_kind[1]):
                            hidden_stats(i, u + 1)
                        with dve.If(k < n_kind[1]):
                            basis_functions(1, i, u, range(G, G + 2))
                        with dve.If(k + 1 < n_kind[1]):
                            hidden_norm(i, u + 1)
                        with dve.If(k < n_kind[1]):
                            basis_functions(1, i, u, range(G + 2, 2 * G))
                        with dve.If(k + 2 < n_kind[1]):
                            basis_functions(0, i, u + 2, range(G))
                        with dve.If(k < n_kind[1]):
                            weighted(1, i, u)

        @blk.tensor
        def _(pe):
            pe.sem_inc(pv_done, LEAD)
            pe.wait_ge(const_ready, 2)
            pe.wait_ge(prep_dve, 1)
            pe.transpose(slot(0)[:, 0, 0:P], w_n[:, 3, :], identf[:])
            pe.matmul(slot(0)[:, 1, 0:P], qf_rep[:].rearrange("f h d -> f (h d)"),
                      kf_rep[:].rearrange("f h d -> f (h d)"), start=True, stop=True).then_inc(prep_mm, 1)
            pe.wait_ge(act_prep, 1)
            pe.wait_ge(prep_dve, 2)
            pe.matmul(slot(1)[:, 0, 0:D], w_T[:], m_blk[:], start=True, stop=True).then_inc(prep_mm, 1)
            pe.wait_ge(act_prep, 2)

            def front(s, bf, u, job, i, jobs):
                if s == "hT":
                    pe.wait_ge(hn_ready, bf + 1)
                if s == "q":
                    hT_job = FRONT.index("hT") if jobs is None else jobs[("hT", 0, 0, u)]
                    pe.wait_ge(freed[hT_job % SLOTS], fill_no(hT_job, i))
                wait_freed(pe, job, i)
                dst = slot(job)
                if s == "hT":
                    for t in range(NT):
                        mm = pe.transpose(dst[:, 0, P * t:P * (t + 1)], hn[:, t, :], identf[:])
                if s in SPLIT:
                    w = {"q": w_n[:, 0, :], "k": w_n[:, 1, :], "u": w_u[:]}[s]
                    mm = pe.matmul(dst[:, 0, :], w, hT[:], start=True, stop=True)
                if s == "v":
                    for t in range(NT):
                        mm = pe.matmul(dst[:, 0, P * t:P * (t + 1)], hT[:, P * t:P * (t + 1)], w_n[:, 2, :],
                                       start=True, stop=True)
                mm.then_inc(filled[job % SLOTS], 1)

            for s in FRONT:
                front(s, 0, 0, FRONT.index(s), 0, None)
            pe.wait_ge(ones_loaded, 32)
            pe.wait_ge(const_ready, 3)
            pe.wait_ge(pv_zeroed, 1)
            pe.wait_ge(wout_loaded, 32)
            def batches(steps, jobs, i):
                for s, n, j, u in steps:
                    b = i * 2 + u
                    p = u % 2
                    sq, sk, su = (stack[p][m][:].rearrange("r (h t) -> r h t", h=H) for m in range(3))
                    if s in FRONT:
                        front(s, b + 1, u, jobs[(s, n, 0, u)], i, jobs)
                    if s == "begin":
                        pe.wait_ge(stack_loaded[p], i * 160 + (u // 2 * 160 + 160))
                    if s == "max":
                        for c in (j,):
                            job = jobs[(s, n, c, u)]
                            wait_freed(pe, job, i)
                            k0 = WIN if c == 0 else 0
                            for bk in range(2):
                                pe.matmul(slot(job)[:, bk, 0:2 * WQ], identb[:],
                                          mask_max[:].rearrange("p a q -> p (a q)"), start=True, stop=True)
                                for jj in range(2):
                                    h = HG * n + 2 * bk + jj
                                    mm = pe.matmul(slot(job)[:, bk, WQ * jj + k0:WQ * (jj + 1)],
                                                   sq[:, h, P * c:P * (c + 1)],
                                                   sk[:, h, P * c - WIN + k0:P * (c + 1)],
                                                   start=False, stop=True, skip_group_check=True)
                            mm.then_inc(filled[job % SLOTS], 1)
                    if s == "mT":
                        job = jobs[(s, n, 0, u)]
                        wait_freed(pe, job, i)
                        last_max = jobs[("max", NHG - 1, NT - 1, u)]
                        pe.wait_ge(freed[last_max % SLOTS], fill_no(last_max, i))
                        for c in range(NT):
                            mm = pe.transpose(slot(job)[0:H, 0, P * c:P * (c + 1)], negm[:, c, :], identf[:])
                        mm.then_inc(filled[job % SLOTS], 1)
                    if s == "lin" and j < 2:
                        job = jobs[(s, n, j, u)]
                        wait_freed(pe, job, i)
                        for bk in range(2):
                            c = 2 * j + bk
                            for hd in range(HG):
                                mm = pe.matmul(slot(job)[:, bk, P * hd:P * (hd + 1)],
                                               sk[:, HG * n + hd, P * c:P * (c + 1)],
                                               su[:, HG * n + hd, P * c:P * (c + 1)], start=True, stop=True)
                        mm.then_inc(filled[job % SLOTS], 1)
                    if s == "lin" and j >= 2:
                        job = jobs[(s, n, j, u)]
                        wait_freed(pe, job, i)
                        for bk, o, c in ((0, 0, 0), (1, 0, 1), (1, 256, 2)):
                            w = T - P * (c + 1)
                            mm = pe.matmul(slot(job)[:, bk, o:o + w],
                                           sk[:, HG * n + j - 2, P * c:P * (c + 1)],
                                           su[:, HG * n + j - 2, P * (c + 1):T], start=True, stop=True)
                        mm.then_inc(filled[job % SLOTS], 1)
                    if s == "win":
                        if n == NHG and j == 0:
                            pe.wait_ge(mrow_loaded, batch_no(i, u, 16, LEAD_DMA + 16))
                        for c in (j,):
                            job = jobs[(s, n, c, u)]
                            wq = WQ if c < NT - 1 else P
                            wait_freed(pe, job, i)
                            for bk in range(2):
                                pe.matmul(slot(job)[:, bk, 0:2 * WQ], identb[:],
                                          mask_win[:].rearrange("p a q -> p (a q)"), start=True, stop=True)
                                for jj in range(2):
                                    h = HG * (n - NHG) + 2 * bk + jj
                                    mm = pe.matmul(slot(job)[:, bk, WQ * jj:WQ * jj + wq],
                                                   sk[:, h, P * c:P * (c + 1)],
                                                   sq[:, h, P * c:P * c + wq],
                                                   start=False, stop=True, skip_group_check=True)
                            mm.then_inc(filled[job % SLOTS], 1)
                    if s == "pv":
                        if n < NHG:
                            pe.wait_ge(pd_ready, batch_no(i, u, 8, 2 * n + 2))
                            po_job = jobs[("lin", n, 5, u)]
                            pe.wait_ge(freed[po_job % SLOTS], fill_no(po_job, i))
                        else:
                            pe.wait_ge(pw_ready, batch_no(i, u, 16, LEAD + 4 * (n - NHG) + 4))
                        pe.wait_ge(y_out[n % 2], batch_no(i, u, 4, LEAD + n // 2))
                        for c in range(NT):
                            parts = []
                            if n < NHG:
                                pd = Pb[:, n % 2, 512 * c:512 * (c + 1)].rearrange("p (j q) -> p j q", j=HG)
                                po = Pb[:, n % 2, 2048:5120].rearrange("p (j q) -> p j q", j=HG)
                                parts.append((P * c, P, pd))
                                if c < NT - 1:
                                    o = (0, 384, 640)[c]
                                    w = T - P * (c + 1)
                                    parts.append((P * (c + 1), w, po[:, :, o:o + w]))
                            else:
                                wq = WQ if c < NT - 1 else P
                                pw = Pb[:, n % 2, 768 * c:768 * (c + 1)].rearrange("p (j q) -> p j q", j=HG)
                                parts.append((P * c, wq, pw[:, :, 0:wq]))
                            for x_, (q0, w, src) in enumerate(parts):
                                for j in range(HG):
                                    mm = pe.matmul(pv[32 * j:32 * j + 16, n % 2, q0:q0 + w],
                                                   vaug[:, p, c, HG * (n % NHG) + j, :], src[:, j, :],
                                                   start=(c == 0 and x_ == 0), stop=(c == NT - 1),
                                                   skip_group_check=True)
                        mm.then_inc(pv_done, 1)
                    if s == "ytr":
                        job = jobs[(s, n, 0, u)]
                        wait_freed(pe, job, i)
                        for bk in range(2):
                            pe.wait_ge(y_out[bk], batch_no(i, u, 4, LEAD + n + 1))
                            for t in range(NT):
                                mm = pe.transpose(slot(job)[:, bk, P * t:P * (t + 1)],
                                                  y_sb[:, n % 2, bk, P * t:P * (t + 1)], identf[:])
                        mm.then_inc(filled[job % SLOTS], 1)
                    if s == "ycT":
                        job = jobs[(s, n, 0, u)]
                        wait_freed(pe, job, i)
                        y_job = jobs[("ytr", 3, 0, u)]
                        pe.wait_ge(freed[y_job % SLOTS], fill_no(y_job, i))
                        for kind in range(2):
                            for t in range(NT):
                                mm = pe.transpose(slot(job)[:, kind, P * t:P * (t + 1)], ycat[:, t, kind, :],
                                                  identf[:])
                        mm.then_inc(filled[job % SLOTS], 1)
                    if s == "out":
                        job = jobs[(s, n, 0, u)]
                        wait_freed(pe, job, i)
                        c_job = jobs[("ycT", 0, 0, u)]
                        pe.wait_ge(freed[c_job % SLOTS], fill_no(c_job, i))
                        for t in range(NT):
                            for kind in range(2):
                                mm = pe.matmul(slot(job)[:, 0, P * t:P * (t + 1)], ycT[:, kind, P * t:P * (t + 1)],
                                               wout[:, kind, :], start=(kind == 0), stop=(kind == 1))
                        mm.then_inc(filled[job % SLOTS], 1)
                    if s == "h2T":
                        job = jobs[(s, n, 0, u)]
                        wait_freed(pe, job, i)
                        pe.wait_ge(h2_ready, batch_no(i, u, 1, 1))
                        for t in range(NT):
                            mm = pe.transpose(slot(job)[:, 0, P * t:P * (t + 1)], h2[:, t, :], identf[:])
                        mm.then_inc(filled[job % SLOTS], 1)
                    if s == "logit":
                        job = jobs[(s, n, 0, u)]
                        wait_freed(pe, job, i)
                        t_job = jobs[("h2T", 0, 0, u)]
                        pe.wait_ge(freed[t_job % SLOTS], fill_no(t_job, i))
                        for t in range(NT):
                            mm = pe.matmul(slot(job)[:, 0, 8 * t:8 * (t + 1)], h2T[:, P * t:P * (t + 1)], gate[:],
                                           start=True, stop=True)
                        mm.then_inc(filled[job % SLOTS], 1)
                    if s == "rank":
                        job = jobs[(s, n, 0, u)]
                        wait_freed(pe, job, i)
                        pe.wait_ge(sel_ready, batch_no(i, u, 1, 1))
                        for t in range(NT):
                            for t2 in range(t + 1):
                                mm = pe.matmul(slot(job)[:, 0, E * t:E * (t + 1)], upper[:] if t2 == t else ones_bf[:],
                                               sel[:, t2, :], start=(t2 == 0), stop=(t2 == t))
                        mm.then_inc(filled[job % SLOTS], 1)
                    if s == "total":
                        job = jobs[(s, n, 0, u)]
                        wait_freed(pe, job, i)
                        for t in range(NT):
                            mm = pe.matmul(slot(job)[:, 0, 0:E], ones_bf[:], sel[:, t, :], start=(t == 0),
                                           stop=(t == NT - 1))
                        mm.then_inc(filled[job % SLOTS], 1)

            all_batches(pe, batches)

            n_kind = load_counts(pe)
            tile_lead(pe, (m_xT, 1), (m_h, F // P), (m_mm, 1), (k_xT, 1), (k_hT, 1), (k_mm[0], G), (k_mm[1], 2 * G))

            def rows_transposed(kind, i, u):
                k = i * RECS + u
                x_sem, rows, xT_sem = ((m_x, m_rows, m_xT), (k_x, k_rows, k_xT))[kind]
                pe.wait_ge(x_sem[u % 2], use_no(2, i, u, 64))
                pe.wait_ge(*((m_xs, tile_no(k, back=1)) if kind == 0 else (k_sig[0], tile_no(k, G, back=1))))
                for q in range(Q4):
                    mm = pe.transpose(pv[:, 0, P * q:P * (q + 1)], rows[:, u % 2, q, :], identf[:])
                mm.then_inc(xT_sem, 1)

            def load_blocks(kind, k):
                return pe.value_load(tab_i[0:1, 2, kind, bass.ds(k, 1)], min_val=0, max_val=Q4)

            def for_blocks(blocks, products):
                with pe.If(blocks < 3):
                    products(2)
                with pe.If(blocks > 2):
                    with pe.If(blocks < 4):
                        products(3)
                    with pe.If(blocks > 3):
                        products(4)

            def bias_row(dst, copies, row, n):
                pe.matmul(dst.rearrange("p (q d) -> p q d", q=copies), ones_bf[0:3, :],
                          row.unsqueeze(1).to_broadcast([3, copies, n]), start=True, stop=True)

            def mlp_first(i, u):
                k = i * RECS + u
                pe.wait_ge(m_w1[u % 2], use_no(2, i, u, 32))
                pe.wait_ge(m_xs, tile_no(k))
                pe.wait_ge(m_g, tile_no(k, F // P, back=1))
                for f in range(F // P):
                    pe.matmul(ring[:, f // 2, f % 2, :], mw[u % 2][:, P * f:P * (f + 1)], mxs,
                              start=True, stop=True).then_inc(m_h, 1)

            def mlp_second(i, u):
                k = i * RECS + u
                blocks = load_blocks(0, k)
                pe.wait_ge(m_w2[u % 2], use_no(2, i, u, 32))
                pe.wait_ge(m_y, tile_no(k, back=1))
                bias_row(pv[:, 1, :], Q4, mbias[:, u % 2], D)

                def products(n):
                    for f in range(F // P):
                        pe.wait_ge(m_g, tile_no(k, F // P, f + 1))
                        for q in range(n):
                            mm = pe.matmul(pv[:, 1, P * q:P * (q + 1)], gelu[:, 4 * (u % 2) + f, P * q:P * (q + 1)],
                                           mw[u % 2][:, F + D * f:F + D * (f + 1)], start=False, stop=True,
                                           skip_group_check=True)
                    mm.then_inc(m_mm, 1)

                for_blocks(blocks, products)

            with pe.If(n_kind[0] > 0):
                rows_transposed(0, 0, 0)
                mlp_first(0, 0)
            with pe.If(n_kind[0] > 1):
                rows_transposed(0, 0, 1)
            with pe.Fori(0, TILES // RECS) as i:
                with pe.If(i * RECS < n_kind[0]):
                    for u in range(RECS):
                        k = i * RECS + u
                        with pe.If(k + 1 < n_kind[0]):
                            mlp_first(i, u + 1)
                        with pe.If(k + 2 < n_kind[0]):
                            rows_transposed(0, i, u + 2)
                        with pe.If(k < n_kind[0]):
                            mlp_second(i, u)
            pe.wait_ge(m_y, n_kind[0] + TILE_LEAD)
            pe.sem_inc(mlps_done, 1)

            def kan_first(i, u):
                k = i * RECS + u
                blocks = load_blocks(1, k)
                pe.wait_ge(k_w0[u % 2], use_no(2, i, u, 64))
                pe.wait_ge(k_zn, tile_no(k, back=1))
                for bk in range(2):
                    bias_row(ring[:, 0, bk, :], 2, kbias[u % RECS][:, 0:F2], F2)

                def products(n):
                    for g in range(G):
                        pe.wait_ge(k_bas[0], tile_no(k, G, g + 1))
                        for q in range(n):
                            mm = pe.matmul(ring[:, 0, q // 2, F2 * (q % 2):F2 * (q % 2 + 1)],
                                           basis[0][:, g, P * q:P * (q + 1)], kw[u % 2][:, F2 * g:F2 * (g + 1)],
                                           start=False, stop=True, skip_group_check=True)
                        mm.then_inc(k_mm[0], 1)

                for_blocks(blocks, products)

            def hidden_transposed(i, u):
                k = i * RECS + u
                pe.wait_ge(k_zn, tile_no(k))
                pe.wait_ge(k_sig[1], tile_no(k, 2 * G, back=1))
                for f in range(2):
                    for q in range(Q4):
                        mm = pe.transpose(ring[:, 1, f, P * q:P * (q + 1)], zn[:, q, P * f:P * (f + 1)], identf[:])
                mm.then_inc(k_hT, 1)

            def kan_second(i, u):
                k = i * RECS + u
                blocks = load_blocks(1, k)
                pe.wait_ge(k_w1[u % 2], use_no(2, i, u, 16))
                pe.wait_ge(k_y, tile_no(k, back=1))
                bias_row(pv[:, 1, :], Q4, kbias[u % RECS][:, F2:], D)

                def products(n):
                    for g in range(2 * G):
                        pe.wait_ge(k_bas[1], tile_no(k, 2 * G, g + 1))
                        for q in range(n):
                            mm = pe.matmul(pv[:, 1, P * q:P * (q + 1)], basis[1][:, g % G, P * q:P * (q + 1)],
                                           kw[u % 2][:, 2048 + D * g:2048 + D * (g + 1)], start=False, stop=True,
                                           skip_group_check=True)
                        mm.then_inc(k_mm[1], 1)

                for_blocks(blocks, products)

            with pe.If(n_kind[1] > 0):
                rows_transposed(1, 0, 0)
                kan_first(0, 0)
            with pe.If(n_kind[1] > 1):
                rows_transposed(1, 0, 1)
            with pe.Fori(0, TILES // RECS) as i:
                with pe.If(i * RECS < n_kind[1]):
                    for u in range(RECS):
                        k = i * RECS + u
                        with pe.If(k < n_kind[1]):
                            hidden_transposed(i, u)
                        with pe.If(k + 1 < n_kind[1]):
                            kan_first(i, u + 1)
                        with pe.If(k + 2 < n_kind[1]):
                            rows_transposed(1, i, u + 2)
                        with pe.If(k < n_kind[1]):
                            kan_second(i, u)


def kernel(**inputs):
    import numpy as np
    import concourse.bacc as bacc
    from concourse.bass_utils import run_bass_kernel_spmd as run

    nc = bacc.Bacc("TRN2", target_bir_lowering=False, num_devices=1)
    names = ["L0_attn_x", "L0_attn_norm_w", "L0_attn_Wq", "L0_attn_Wk", "L0_attn_Wv", "L0_attn_Wqf",
             "L0_attn_Wkf", "L0_attn_Wout", "L0_ffn_gate_W", "L0_ffn_mlp_W1", "L0_ffn_mlp_b1", "L0_ffn_mlp_W2",
             "L0_ffn_mlp_b2", "L0_ffn_kan_ln_g0", "L0_ffn_kan_ln_b0", "L0_ffn_kan_sl_W0", "L0_ffn_kan_sl_b0",
             "L0_ffn_kan_ln_g1", "L0_ffn_kan_ln_b1", "L0_ffn_kan_sl_W1", "L0_ffn_kan_sl_b1"]
    arrays, args = {}, []
    for name in names:
        a = np.ascontiguousarray(inputs[name])
        arrays[name] = a
        args.append(nc.dram_tensor(name, a.shape, mybir.dt.from_np(a.dtype), kind="ExternalInput").ap())
    arrays["grid"] = np.linspace(GRID_LO, GRID_HI, G).astype(np.float32)
    args.append(nc.dram_tensor("grid", (G,), F32, kind="ExternalInput").ap())
    args.append(nc.dram_tensor("result", (B, T, D), F32, kind="ExternalOutput").ap())
    transformer_kernel(nc, *args)
    return run(nc, [arrays], core_ids=[0]).results[0]["result"]
```

```python
from contextlib import ExitStack

import concourse.bass as bass
from concourse import mybir

ALU = mybir.AluOpType
ACT = mybir.ActivationFunctionType
AX = mybir.AxisListType
F32 = mybir.dt.float32
F16 = mybir.dt.float16
BF16 = mybir.dt.bfloat16
I32 = mybir.dt.int32

P = 128
B, T, D = 8, 512, 128
H, DH, FEAT = 16, 8, 16
NT = T // P
WIN = 64
WQ = P + WIN
HG = 4
NHG = H // HG
LN_EPS, RMS_EPS, LIN_EPS = 1e-5, 1e-6, 1e-6
NEG = -1e30

E, E2 = 8, 4
F, F2, G = 512, 256, 8
TS = 512
Q4 = TS // P
SIGS = 4
STEPS = (G, 2 * G)
MROWS = 4
RECS = 4
TOK = B * T
TILES = 20
ENTRIES = TILES + 4
GRID_LO, GRID_HI = -1.2, 0.2

KR = 3 * DH
SHIFT_ROW = KR


FRONT = ["hT", "q", "k", "u", "v"]
RING_STEPS = FRONT + ["max", "lin", "win", "mT", "ytr", "ycT", "out", "h2T", "logit", "rank", "total"]
SPLIT = ["q", "k", "u"]
SLOTS = 3

ORDER = """
M L M L M -ytr L M L M L -ycT M L M M -out L L L M -coef2 L M L +stats M +aggr P +coef L L M L L M L
M M L -h2norm P L +hT -h2T M L -logit L +q L +k mT Y L L -store P L -choose W W W +u +v -rank P
-total W +stacks +residual W -gapexp W W P W Y W W -weights +xload P W W W W Y W W P -scatter P
""".split()


def batch_steps(u, tail, front):
    series = {"L": iter([("lin", n, j, u) for n in range(NHG) for j in range(6)]),
              "M": iter([("max", n, j, u) for n in range(NHG) for j in range(NT)]),
              "W": iter([("win", n, j, u) for n in range(NHG, 2 * NHG) for j in range(NT)]),
              "P": iter([("pv", n, 0, u) for n in range(2 * NHG)]),
              "Y": iter([("ytr", n, 0, u) for n in range(3)])}
    steps = [("begin", 0, 0, u)]
    for word in ORDER:
        if word in series:
            steps.append(next(series[word]))
        elif word == "mT":
            steps.append(("mT", 0, 0, u))
        elif word[0] == "-" and tail:
            steps.append(("ytr", 3, 0, u - 1) if word == "-ytr" else (word[1:], 0, 0, u - 1))
        elif word[0] == "+" and front:
            steps.append((word[1:], 0, 0, u))
    return steps


TAIL = [("ytr", 3)] + [(step, 0) for step in (
    "ycT", "out", "coef2", "h2norm", "store", "h2T", "logit", "choose", "gapexp", "rank", "total", "weights",
    "scatter")]
FIRST = batch_steps(0, False, True)
TURN = batch_steps(1, True, True) + batch_steps(2, True, True)
LAST = batch_steps(1, True, False) + [(step, n, 0, 1) for step, n in TAIL]
TURNS = B // 2 - 1


def numbered(steps, job):
    jobs = {}
    for entry in steps:
        if entry[0] in RING_STEPS:
            jobs[entry] = job
            job += 1
    return jobs, job


JOBS_FIRST, LOOP_JOB = numbered(FIRST, len(FRONT))
JOBS_TURN, _end = numbered(TURN, LOOP_JOB)
JOBS_LAST, _ = numbered(LAST, LOOP_JOB)
PER_TURN = _end - LOOP_JOB
assert PER_TURN % SLOTS == 0
USES = PER_TURN // SLOTS


def transformer_kernel(nc, x, norm_w, Wq, Wk, Wv, Wqf, Wkf, Wout, gate_W, mW1, mb1, mW2, mb2,
                       g0, b0, kW0, kb0, g1, b1, kW1, kb1, grid, out):
    with ExitStack() as ctx:
        def sb(name, shape, dt=F32):
            return ctx.enter_context(nc.sbuf_tensor(name, shape, dt))

        def sem(name):
            return ctx.enter_context(nc.semaphore(name))

        identf = sb("identf", [P, P])
        identb = sb("identb", [P, P], BF16)
        mask_max = sb("mask_max", [P, WQ], BF16)
        mask_win = sb("mask_win", [P, 2, WQ], BF16)
        block = sb("block", [P, P])
        consts = sb("consts", [P, 5, NT])
        w_raw = sb("w_raw", [P, 3, D])
        w_n = sb("w_n", [P, 4, D])
        w_T = sb("w_T", [P, D])
        w_u = sb("w_u", [P, D])
        qf_rep = sb("qf_rep", [FEAT, H, DH])
        kf_rep = sb("kf_rep", [FEAT, H, DH])
        qf_in = sb("qf_in", [FEAT, DH])
        kf_in = sb("kf_in", [FEAT, DH])
        m_blk = sb("m_blk", [P, P])
        nw = sb("nw", [P, 1])
        wout = sb("wout", [P, 2, D])
        gate = sb("gate", [P, 8])
        ones16 = sb("ones16", [H, T], F16)
        zeros16 = sb("zeros16", [H, T], F16)
        xb = sb("xb", [P, NT, D])
        res = sb("res", [P, 2, NT, D])
        stack = [[sb(f"stack{s}{u}", [P, H * T], F16) for s in range(3)] for u in range(2)]
        vaug = sb("vaug", [P, 2, NT, H, 16])
        stats = sb("stats", [P, NT, 6])
        stats2 = sb("stats2", [P, NT, 6])
        spacer = sb("spacer", [P, 1])
        mv = sb("mv", [P, NT, 2])
        mv2 = sb("mv2", [P, NT, 2])
        c1 = sb("c1", [P, 9, NT])
        c2 = sb("c2", [P, 9, NT])
        hn = sb("hn", [P, NT, D])
        hT = sb("hT", [P, T])
        hi = sb("hi", [P, 3, T], F16)
        lo = sb("lo", [P, 3, T], F16)
        maxima = sb("maxima", [P, NT, H])
        masked = sb("masked", [P, SLOTS, HG, WQ], BF16)
        mT16 = sb("mT16", [H, T], F16)
        Pb = sb("Pb", [P, 2, 5120])
        y_sb = sb("y_sb", [P, 2, 2, T])
        rz4 = sb("rz", [P, 4, 32])
        ycat = sb("ycat", [P, NT, 2, D])
        ycT = sb("ycT", [P, 2, T])
        h2 = sb("h2", [P, NT, D])
        n2 = sb("n2", [P, NT, D])
        h2T = sb("h2T", [P, T])
        upper = sb("upper", [P, P], BF16)
        ones_bf = sb("ones_bf", [P, P], BF16)
        prefer = sb("prefer", [P, NT, E])
        first_slot = sb("first_slot", [P, E])
        lg = sb("lg", [P, 8, NT, E])
        sc = sb("sc", [P, 12, NT])
        sel = sb("sel", [P, NT, E], BF16)
        carry = sb("carry", [P, E])
        pos = sb("pos", [P, NT, 2], I32)
        ids_f = sb("ids_f", [P, NT])
        rec = sb("rec", [P, NT, 2, 2], I32)
        tile_idx = sb("tile_idx", [1, 2, 2, ENTRIES])
        tile_idx4 = sb("tile_idx4", [1, 2, ENTRIES])
        tab_e = sb("tab_e", [1, 8, 2, E2])
        tab_i = sb("tab_i", [1, 3, 2, ENTRIES], I32)
        cnt_i = sb("cnt_i", [1, 2, 2, E2], I32)
        n_i = sb("n_i", [1, 2], I32)
        kp_raw = sb("kp_raw", [P, E2, 6])
        kp_all = sb("kp_all", [P, E2, 27])
        grid_sb = sb("grid_sb", [P, G])
        pad_rec = Pb[:, 0, 0:2 * E * TOK // P].bitcast(I32)
        zero_rows = Pb[:, 0, 512:512 + TS * D // P]
        KB, BIASES = E2 * (F2 + D) // P, E2 * (F2 + 2 * D) // P
        bias_in = Pb[:, 0, 1024:1024 + BIASES]
        bias_rest = Pb[:, 0, 1088:1088 + 2 * BIASES].rearrange("p (r n) -> p r n", r=2)
        bias3 = Pb[:, 0, 1152:1152 + 3 * BIASES // 2].bitcast(BF16).rearrange("p (c n) -> p c n", c=3)
        kprm = sb("kprm", [P, RECS, 27])
        mprm = sb("mprm", [P, RECS, F // P])
        mbias = sb("mbias", [3, 2, D], BF16)
        grec = sb("grec", [P, 2, RECS, Q4, 2], I32)
        srec = sb("srec", [P, 2, RECS, Q4, 2], I32)
        zst = sb("zst", [P, Q4, 6])
        zmv = sb("zmv", [P, Q4, 2])
        zc = sb("zc", [P, 6, Q4])
        kconst = sb("kconst", [P, 3, Q4])
        space = [stack[u][m][:].bitcast(F32) for u in range(2) for m in range(3)]
        space += [Pb[:, 0, 0:4096], Pb[:, 1, 0:4096]]
        kbias = [Pb[0:3, 0, 4096 + (F2 + D) // 2 * r:4096 + (F2 + D) // 2 * (r + 1)].bitcast(BF16) for r in range(RECS)]
        kw = [space[0], space[1]]
        basis = [space[2 + z].rearrange("p (r n) -> p r n", r=G) for z in range(2)]
        sig = [space[4][:, 2048 * z:2048 * (z + 1)].rearrange("p (r n) -> p r n", r=SIGS) for z in range(2)]
        k_rows = space[5][:, 0:1024].rearrange("p (a q d) -> p a q d", a=2, q=Q4)
        m_rows = space[3][:, 0:2048].rearrange("p (a q d) -> p a q d", a=MROWS, q=Q4)
        k_res, m_res = (space[5][:, 2048 * z + 1024:2048 * (z + 1)].rearrange("p (a q d) -> p a q d", a=2, q=Q4)
                        for z in range(2))
        zn = space[6][:, 0:Q4 * F2].rearrange("p (q f) -> p q f", q=Q4)
        mw = [space[6][:, 1024 * (1 + z):1024 * (2 + z)] for z in range(2)]
        mxs = space[6][:, 3072:3072 + TS]
        gelu = space[7].rearrange("p (r n) -> p r n", r=2 * (F // P))

        ring = ctx.enter_context(nc.psum_tensor("ring", [P, SLOTS, 2, 512], F32))
        pv = ctx.enter_context(nc.psum_tensor("pv", [P, 2, 512], F32))

        hl_d = nc.dram_tensor("hl_d", [2, P, 3, T], F16, kind="Internal").ap()
        h2_d = nc.dram_tensor("h2_d", [TOK + TS, D], F32, kind="Internal").ap()
        n2_d = nc.dram_tensor("n2_d", [TOK + TS, D], F32, kind="Internal").ap()
        acc_d = nc.dram_tensor("acc_d", [TOK + TS, D], F32, kind="Internal").ap()
        slot_d = nc.dram_tensor("slot_d", [E * TOK, 2], I32, kind="Internal").ap()
        kp_d = nc.dram_tensor("kp_d", [E2, P, 27], F32, kind="Internal").ap()
        kb0_d = nc.dram_tensor("kb0_d", [3, E2 * F2], BF16, kind="Internal").ap()
        kb1_d = nc.dram_tensor("kb1_d", [3, E2 * D], BF16, kind="Internal").ap()
        mb_d = nc.dram_tensor("mb_d", [3, E2 * D], BF16, kind="Internal").ap()

        filled = [sem(f"filled{s}") for s in range(SLOTS)]
        freed = [sem(f"freed{s}") for s in range(SLOTS)]
        w_loaded = sem("w_loaded")
        x_loaded = sem("x_loaded")
        const_ready = sem("const_ready")
        wout_loaded = sem("wout_loaded")
        zeroed = sem("zeroed")
        stack0_zeroed, stack1_zeroed = sem("stack0_zeroed"), sem("stack1_zeroed")
        ones_column = sem("ones_column")
        pv_zeroed = sem("pv_zeroed")
        act_prep = sem("act_prep")
        prep_mm = sem("prep_mm")
        prep_dve = sem("prep_dve")
        pool_chain = sem("pool_chain")
        dve_chain = sem("dve_chain")
        stats_ready = sem("stats_ready")
        hn_ready = sem("hn_ready")
        xres_ready = sem("xres_ready")
        hT_ready = sem("hT_ready")
        hi_ready = sem("hi_ready")
        lo_ready = sem("lo_ready")
        v_ready = sem("v_ready")
        hl_stored = sem("hl_stored")
        first_stored = [sem(f"first_stored{s}") for s in range(3)]
        stack_loaded = [sem(f"stack_loaded{u}") for u in range(2)]
        ones_loaded = [sem(f"ones_loaded{u}") for u in range(2)]
        mT_ready = sem("mT_ready")
        mrow_loaded = sem("mrow_loaded")
        pd_ready = sem("pd_ready")
        pv_done = sem("pv_done")
        y_out = [sem("y_out_dve"), sem("y_out_act")]
        ycat_ready = sem("ycat_ready")
        ycT_ready = sem("ycT_ready")
        x1_ready = sem("x1_ready")
        stats2_ready = sem("stats2_ready")
        coef2_ready = sem("coef2_ready")
        h2_ready = sem("h2_ready")
        n2_ready = sem("n2_ready")
        x1_stored = [sem(f"x1_stored{u}") for u in range(2)]
        rows_stored = sem("rows_stored")
        h2T_ready = sem("h2T_ready")
        sel_ready = sem("sel_ready")
        gap_ready = sem("gap_ready")
        exp_ready = sem("exp_ready")
        route_chain = sem("route_chain")
        rec_ready = sem("rec_ready")
        slots_stored = sem("slots_stored")
        slots_done = sem("slots_done")
        pads_ready = sem("pads_ready")
        pads_stored = sem("pads_stored")
        kp_loaded = sem("kp_loaded")
        kp_ready = sem("kp_ready")
        table_ready = sem("table_ready")
        k_w0, k_w1, k_x, m_w1, m_w2 = ([sem(f"{name}_{u}") for u in range(2)] for name in (
            "k_w0", "k_w1", "k_x", "m_w1", "m_w2"))
        m_x = [sem(f"m_x_{u}") for u in range(MROWS)]
        k_grec, k_srec, m_grec, m_srec = ([sem(f"{name}_{u}") for u in range(RECS)] for name in (
            "k_grec", "k_srec", "m_grec", "m_srec"))
        k_xT, k_hT, k_st2, k_st, k_cf, k_zn, k_y, k_add, k_added = (
            sem(name) for name in ("k_xT", "k_hT", "k_st2", "k_st", "k_cf", "k_zn", "k_y", "k_add", "k_added"))
        k_sig, k_bas, k_mm = ([sem(f"{name}{z}") for z in range(2)] for name in ("k_sig", "k_bas", "k_mm"))
        m_xT, m_xs, m_h, m_g, m_mm, m_y, m_add, m_added = (
            sem(name) for name in ("m_xT", "m_xs", "m_h", "m_g", "m_mm", "m_y", "m_add", "m_added"))
        pool_at = sem("pool_at")
        dve_at = sem("dve_at")
        mlps_done = sem("mlps_done")
        all_added = sem("all_added")
        copied = sem("copied")

        x_rows = x.rearrange("b (t p) d -> b p t d", p=P)
        out_rows, h2_rows, n2_rows = (a[0:TOK].rearrange("(b t p) d -> b p t d", b=B, p=P)
                                      for a in (acc_d, h2_d, n2_d))

        def slot(job):
            return ring[:, job % SLOTS]

        def fill_no(job, i):
            return i * USES + (job // SLOTS + 1)

        def wait_filled(eng, job, i):
            eng.wait_ge(filled[job % SLOTS], fill_no(job, i))

        def wait_freed(eng, job, i):
            if job >= SLOTS or not isinstance(i, int):
                eng.wait_ge(freed[job % SLOTS], i * USES + job // SLOTS)

        def all_batches(eng, run, count=None, per=0):
            run(FIRST, JOBS_FIRST, 0)
            start = count[0] if count else 0
            with eng.Fori(0, TURNS) as i:
                run(TURN, JOBS_TURN, i)
            if count:
                assert count[0] - start == per, count[0] - start
                count[0] = start
            run(LAST, JOBS_LAST, TURNS)
            if count:
                count[0] += TURNS * per

        def batch_no(i, u, per, off):
            return i * (2 * per) + (u * per + off)

        def load_counts(eng):
            eng.wait_ge(table_ready, 1)
            return [eng.value_load(n_i[0:1, kind:kind + 1], min_val=0, max_val=TILES) for kind in range(2)]

        LEAD, LEAD_DMA = 1, 16

        TILE_LEAD = 4

        def tile_no(k, per=1, part=None, back=0):
            return k * per + ((TILE_LEAD - back) * per + (per if part is None else part))

        def tile_lead(eng, *sems):
            for s_, per in sems:
                eng.sem_inc(s_, TILE_LEAD * per)

        def use_no(buffers, i, u, per):
            return i * (RECS // buffers * per) + (u // buffers + 1) * per

        W_DMAS = 6
        PAD_DMAS = 16 * 8
        blk = ctx.enter_context(nc.Block())

        @blk.sync
        def _(sp):
            sp.sem_inc(mrow_loaded, LEAD_DMA)
            sp.sem_inc(rows_stored, LEAD_DMA)
            for u in range(2):
                sp.sem_inc(x1_stored[u], LEAD_DMA)
            sp.dma_start(xb[:], x_rows[0]).then_inc(x_loaded, 16)
            for k, w in enumerate((Wq, Wk, Wv)):
                sp.dma_start(w_raw[:, k, :], w).then_inc(w_loaded, 16)
            sp.dma_start(nw[:], norm_w.rearrange("(d a) -> d a", a=1)).then_inc(w_loaded, 16)
            with nc.allow_non_contiguous_dma(reason="two 8x16 matrices, transposed"):
                sp.dma_start(qf_in[:], Wqf.rearrange("d f -> f d")).then_inc(w_loaded, 16)
                sp.dma_start(kf_in[:], Wkf.rearrange("d f -> f d")).then_inc(w_loaded, 16)
            sp.dma_start(wout[:], Wout.rearrange("(k p) n -> p k n", p=P)).then_inc(wout_loaded, 16)
            sp.dma_start(gate[:], gate_W).then_inc(wout_loaded, 16)
            with nc.allow_non_contiguous_dma(reason="a few hundred words"):
                for k, w in enumerate((g0, b0)):
                    sp.dma_start(kp_raw[:, :, k], w.rearrange("e p -> p e")).then_inc(kp_loaded, 16)
                for k, w in enumerate((g1, b1)):
                    for f in range(2):
                        sp.dma_start(kp_raw[:, :, 2 + 2 * k + f], w[:, P * f:P * (f + 1)].rearrange("e p -> p e")
                                     ).then_inc(kp_loaded, 16)
            at = 0
            for rows in (kb0, kb1, mb2):
                n = rows.shape[0] * rows.shape[1] // P
                sp.dma_start(bias_in[:, at:at + n], rows.rearrange("e n -> (e n)").rearrange("(p x) -> p x", p=P)
                             ).then_inc(kp_loaded, 16)
                at += n
            sp.dma_start(grid_sb[:], grid.unsqueeze(0).to_broadcast([P, G])).then_inc(kp_loaded, 16)
            sp.wait_ge(const_ready, 1)
            sp.wait_ge(stack0_zeroed, 1)

            def load_ones(u):
                sp.dma_start(stack[u][1][SHIFT_ROW:SHIFT_ROW + 1, :].rearrange("a (h t) -> a h t", h=H),
                             ones16[:]).then_inc(ones_loaded[u], 16)

            load_ones(0)

            def load_stack(u, s):
                for g, part in enumerate(((0, 1, 0), (0, 0, 1), (0, 1, 0))[s]):
                    sp.dma_start(stack[u][s][DH * g:DH * (g + 1), :].rearrange("d (h t) -> d h t", h=H),
                                 hl_d[part, :, s, :].rearrange("(h d) t -> d h t", d=DH)
                                 ).then_inc(stack_loaded[u], 16)

            def clear_shift(u):
                sp.dma_start(stack[u][0][SHIFT_ROW:SHIFT_ROW + 1, :].rearrange("a (h t) -> a h t", h=H),
                             zeros16[:]).then_inc(stack_loaded[u], 16)

            def load_stacks(bf, u):
                sp.wait_ge(lo_ready, bf * 3 + 3)
                sp.dma_start(hl_d[0], hi[:]).then_inc(hl_stored, 16)
                sp.dma_start(hl_d[1], lo[:]).then_inc(hl_stored, 16)
                sp.wait_ge(hl_stored, bf * 32 + 32)
                for s in range(3):
                    load_stack(u, s)
                clear_shift(u)

            clear_shift(0)
            for s in range(3):
                sp.wait_ge(lo_ready, s + 1)
                for part, half in enumerate((hi, lo)):
                    sp.dma_start(hl_d[part, :, s, :], half[:, s, :]).then_inc(first_stored[s], 16)
            for s in range(3):
                sp.wait_ge(first_stored[s], 32)
                load_stack(0, s)
            sp.sem_inc(hl_stored, 32)
            sp.wait_ge(xres_ready, 1)
            sp.dma_start(xb[:], x_rows[1]).then_inc(x_loaded, 16)
            sp.wait_ge(pads_ready, 2)
            sp.dma_start(slot_d.rearrange("(p s) w -> p (s w)", p=P), pad_rec).then_inc(pads_stored, 16)
            for rows in (h2_d, n2_d, acc_d):
                sp.dma_start(rows[TOK:].rearrange("(p t) d -> p (t d)", p=P), zero_rows).then_inc(pads_stored, 16)
            sp.wait_ge(kp_ready, 2)
            sp.dma_start(kp_d.rearrange("e p c -> p e c"), kp_all[:]).then_inc(pads_stored, 16)
            at = 0
            for rows in (kb0_d, kb1_d, mb_d):
                n = rows.shape[1] // P
                sp.dma_start(rows.rearrange("c (p x) -> p c x", p=P), bias3[:, :, at:at + n]).then_inc(pads_stored, 16)
                at += n

            sp.wait_ge(stack1_zeroed, 1)
            load_ones(1)

            def batches(steps, jobs, i):
                for s, n, j, u in steps:
                    b = i * 2 + u
                    p = u % 2
                    if s == "xload":
                        sp.wait_ge(xres_ready, batch_no(i, u, 1, 2))
                        sp.dma_start(xb[:], x_rows[bass.ds((b + 2) % B, 1)].rearrange(
                            "a p t d -> (a p) t d")).then_inc(x_loaded, 16)
                    if s == "mT":
                        sp.wait_ge(mT_ready, batch_no(i, u, 1, 1))
                        sp.dma_start(stack[p][0][SHIFT_ROW:SHIFT_ROW + 1, :].rearrange("a (h t) -> a h t", h=H),
                                     mT16[:]).then_inc(mrow_loaded, 16)
                    if s == "stacks":
                        sp.wait_ge(pv_done, batch_no(i, u, 8, LEAD))
                        load_stacks(b + 1, 1 - p)
                    if s == "store":
                        rows = bass.ds(b, 1)
                        sp.wait_ge(x1_ready, batch_no(i, u, 1, 1))
                        sp.dma_start(out_rows[rows].rearrange("a p t d -> (a p) t d"), res[:, p]
                                     ).then_inc(x1_stored[p], 16)
                        sp.wait_ge(h2_ready, batch_no(i, u, 1, 1))
                        sp.dma_start(h2_rows[rows].rearrange("a p t d -> (a p) t d"), h2[:]
                                     ).then_inc(rows_stored, 16)
                        sp.wait_ge(n2_ready, batch_no(i, u, 1, 1))
                        sp.dma_start(n2_rows[rows].rearrange("a p t d -> (a p) t d"), n2[:]
                                     ).then_inc(rows_stored, 16)

            all_batches(sp, batches)
            sp.wait_ge(rows_stored, LEAD_DMA + 32 * B)
            for u in range(2):
                sp.wait_ge(x1_stored[u], LEAD_DMA + 16 * (B // 2))
            sp.wait_ge(x_loaded, 16 * (B + 1))

            n_kind = load_counts(sp)

            def tile_expert(kind, k):
                e = sp.value_load(tab_i[0:1, 1, kind, bass.ds(k, 1)], min_val=kind * E2, max_val=kind * E2 + E2 - 1)
                return bass.ds(e - kind * E2, 1)

            def load_records(kind, i, u, for_gather):
                k = i * RECS + u
                per = E2 * TOK // TS
                at = sp.value_load(tab_i[0:1, 0, kind, bass.ds(k, 1)], min_val=kind * per, max_val=kind * per + per - 1)
                last_use = ((m_xT, k_xT) if for_gather else (m_added, k_added))[kind]
                done = ((m_grec, k_grec) if for_gather else (m_srec, k_srec))[kind][u % RECS]
                sp.wait_ge(last_use, tile_no(k, back=RECS))
                sp.dma_start((grec if for_gather else srec)[:, kind, u % RECS],
                             slot_d.rearrange("(n q p) w -> n p q w", p=P, q=Q4)[bass.ds(at, 1)].rearrange(
                                 "a p q w -> (a p) q w")).then_inc(done, 16)

            def load_mlp(i, u):
                k = i * RECS + u
                w = mw[u % 2]
                e = tile_expert(0, k)
                sp.wait_ge(m_g, tile_no(k, F // P, back=2))
                sp.dma_start(w[:, 0:F], mW1[e].rearrange("a p n -> (a p) n")).then_inc(m_w1[u % 2], 16)
                with nc.allow_non_contiguous_dma(reason="512 words"):
                    sp.dma_start(mprm[:, u % RECS], mb1[e].rearrange("a (f p) -> (a p) f", p=P)
                                 ).then_inc(m_w1[u % 2], 16)
                sp.wait_ge(m_y, tile_no(k, back=2))
                sp.dma_start(w[:, F:2 * F].rearrange("p (f n) -> p f n", f=F // P),
                             mW2[e].rearrange("a (f p) n -> (a p) f n", p=P)).then_inc(m_w2[u % 2], 16)
                sp.dma_start(mbias[:, u % 2], mb_d.rearrange("c (e n) -> e c n", n=D)[e].rearrange(
                    "a c n -> (a c) n")).then_inc(m_w2[u % 2], 16)

            for u in range(2):
                with sp.If(n_kind[0] > u):
                    load_records(0, 0, u, True)
            with sp.If(n_kind[0] > 0):
                load_mlp(0, 0)
            for kind, u in ((1, 0), (0, 2), (1, 1), (0, 3), (1, 2)):
                with sp.If(n_kind[kind] > u):
                    load_records(kind, 0, u, True)
            with sp.Fori(0, TILES // RECS) as i:
                with sp.If(i * RECS < n_kind[0]):
                    for u in range(RECS):
                        k = i * RECS + u
                        with sp.If(k < n_kind[0]):
                            load_records(0, i, u, False)
                        with sp.If(k + 1 < n_kind[0]):
                            load_mlp(i, u + 1)
                        with sp.If(k + 4 < n_kind[0]):
                            load_records(0, i, u + 4, True)
            with sp.Fori(0, TILES // RECS) as i:
                with sp.If(i * RECS < n_kind[1]):
                    for u in range(RECS):
                        k = i * RECS + u
                        w = kw[u % 2]
                        with sp.If(k + 3 < n_kind[1]):
                            load_records(1, i, u + 3, True)
                        with sp.If(k < n_kind[1]):
                            load_records(1, i, u, False)
                            e = tile_expert(1, k)
                            sp.wait_ge(k_zn, tile_no(k, back=2))
                            sp.dma_start(w[:, 0:2048].rearrange("p (g n) -> p g n", g=G),
                                         kW0[e].rearrange("a (p g) n -> (a p) g n", g=G)).then_inc(k_w0[u % 2], 16)
                            sp.dma_start(kprm[:, u], kp_d[e].rearrange("a p c -> (a p) c")).then_inc(k_w0[u % 2], 16)
                            for rows, a_, n in ((kb0_d, 0, F2), (kb1_d, F2, D)):
                                sp.dma_start(kbias[u][:, a_:a_ + n],
                                             rows.rearrange("c (e n) -> e c n", n=n)[e].rearrange("a c n -> (a c) n")
                                             ).then_inc(k_w0[u % 2], 16)
                            sp.wait_ge(k_y, tile_no(k, back=2))
                            sp.dma_start(w[:, 2048:4096].rearrange("p (f x) -> p f x", f=2),
                                         kW1[e].rearrange("a (f p g) n -> (a p) f (g n)", f=2, g=G)
                                         ).then_inc(k_w1[u % 2], 16)
            sp.wait_ge(all_added, 1)
            sp.dma_start(out.rearrange("b t d -> (b t) d"), acc_d[0:TOK]).then_inc(copied, 16)
            sp.wait_ge(copied, 16)

        @blk.gpsimd
        def _(pool):
            count = [0]

            def link(ins, i=0, per=0):
                count[0] += 1
                ins.then_inc(pool_chain, 1)
                pool.wait_ge(pool_chain, i * per + count[0])

            pool.sem_inc(slots_done, LEAD)
            pool.memset(ones16[:], 1.0)
            pool.memset(zeros16[:], 0.0).then_inc(const_ready, 1)
            for k, value in enumerate((-0.5, LN_EPS, RMS_EPS, -1.0, 1.0)):
                pool.memset(consts[:, k, :], value)
            link(pool.memset(identf[:], 0.0))
            link(pool.affine_select(identf[:], identf[:], [[-1, P]], ALU.not_equal, 1.0, base=0,
                                    channel_multiplier=1))
            pool.tensor_copy(identb[:], identf[:])
            link(pool.memset(block[:], 0.5))
            link(pool.affine_select(block[:], block[:], [[-DH, H], [0, DH]], ALU.is_ge, 0.0, base=0,
                                    channel_multiplier=1))
            pool.affine_select(block[:], block[:], [[DH, H], [0, DH]], ALU.is_ge, 0.0, base=DH - 1,
                               channel_multiplier=-1).then_inc(const_ready, 1)
            half, ln_eps, rms_eps, minus, one = (consts[:, k, :] for k in range(5))

            def coefficients(mvt, c, eps2, i, per, s_ready=None):
                m, v = mvt[:, :, 0], mvt[:, :, 1]
                pool.tensor_tensor(c[:, 7, :], m, minus, ALU.mult)
                link(pool.tensor_tensor(c[:, 4, :], v, ln_eps, ALU.add), i, per)
                pool.tensor_tensor(c[:, 0, :], c[:, 4, :], half, ALU.pow)
                link(pool.tensor_tensor(c[:, 5, :], c[:, 4, :], eps2, ALU.mult), i, per)
                minus_ms = pool.tensor_tensor(c[:, 1, :], c[:, 7, :], c[:, 0, :], ALU.mult)
                if s_ready:
                    minus_ms.then_inc(s_ready, 1)
                pool.tensor_tensor(c[:, 8, :], c[:, 0, :], one, ALU.add)
                link(pool.tensor_tensor(c[:, 6, :], c[:, 5, :], v, ALU.add), i, per)
                link(pool.tensor_tensor(c[:, 2, :], c[:, 6, :], half, ALU.pow), i, per)
                link(pool.tensor_tensor(c[:, 3, :], c[:, 7, :], c[:, 2, :], ALU.mult), i, per)

            def front_coefficients(bf, i, per):
                pool.wait_ge(stats_ready, bf + 1)
                coefficients(mv, c1, rms_eps, i, per)

            def normed():
                pool.sem_inc(pool_at, 1)
                for t in range(NT):
                    last = pool.tensor_scalar(hn[:, t, :], xb[:, t, :], c1[:, 2, t:t + 1], c1[:, 3, t:t + 1],
                                              ALU.mult, ALU.add)
                last.then_inc(hn_ready, 1)

            def residual(u):
                for t in range(NT):
                    last = pool.tensor_scalar(res[:, u, t, :], xb[:, t, :], c1[:, 8, t:t + 1], c1[:, 1, t:t + 1],
                                              ALU.mult, ALU.add)
                last.then_inc(xres_ready, 1)

            front_coefficients(0, 0, 0)
            normed()
            residual(0)
            link(pool.memset(mask_max[:], 0.0))
            link(pool.affine_select(mask_max[:], mask_max[:], [[1, WQ]], ALU.is_ge, NEG, base=0,
                                    channel_multiplier=-1))
            link(pool.affine_select(mask_max[:], mask_max[:], [[-1, WQ]], ALU.is_ge, NEG, base=WIN,
                                    channel_multiplier=1))
            link(pool.memset(mask_win[:], 0.0))
            link(pool.affine_select(mask_win[:], mask_win[:], [[0, 2], [1, WQ]], ALU.is_ge, NEG, base=0,
                                    channel_multiplier=-1))
            pool.affine_select(mask_win[:], mask_win[:], [[0, 2], [-1, WQ]], ALU.is_ge, NEG, base=WIN,
                               channel_multiplier=1).then_inc(const_ready, 1)

            pool.memset(zero_rows, 0.0)
            pool.memset(ones_bf[:], 1.0)
            for k, value in enumerate((16.0, -4.0, LN_EPS)):
                pool.memset(kconst[:, k, :], value)
            pool.iota(pad_rec.rearrange("p (s w) -> p s w", w=2)[:, :, 0], [[1, E * TOK // P]], base=0,
                      channel_multiplier=E * TOK // P)
            pool.iota(rec[:, :, 0, 0], [[P, NT]], base=0, channel_multiplier=1)
            for row in range(2):
                pool.iota(tab_i[:, row], [[row * E2 * TOK // TS, 2], [1, ENTRIES]], base=0, channel_multiplier=0)
            link(pool.memset(upper[:], 1.0))
            pool.affine_select(upper[:], upper[:], [[1, P]], ALU.is_gt, 0.0, base=0, channel_multiplier=-1)
            for e in range(E):
                pool.memset(prefer[:, :, e:e + 1], float(E - e))
                pool.memset(first_slot[:, e:e + 1], float(e * TOK))
            pool.memset(carry[:, 0:1], 0.0).then_inc(pads_ready, 1)
            POOL_PER = 20

            def batches(steps, jobs, i):
                for s, n, j, u in steps:
                    b = i * 2 + u
                    if s == "lin" and j < 2:
                        job = jobs[(s, n, j, u)]
                        pool.wait_ge(freed[job % SLOTS], fill_no(job, i))
                        pool.sem_inc(pool_at, 1)
                        pd = Pb[:, n % 2, 1024 * j:1024 * (j + 1)].rearrange("p (a q) -> p a q", q=P)
                        pool.affine_select(pd, pd, [[0, 8], [1, P]], ALU.is_ge, 0.0, base=0,
                                           channel_multiplier=-1).then_inc(pd_ready, 1)
                    if s == "coef":
                        front_coefficients(b + 1, i, POOL_PER)
                        normed()
                    if s == "residual":
                        pool.wait_ge(x1_stored[1 - u % 2], i * 16 + ((u + 1) // 2 * 16 + LEAD_DMA))
                        pool.sem_inc(pool_at, 1)
                        residual(1 - u % 2)
                    if s == "coef2":
                        pool.wait_ge(stats2_ready, batch_no(i, u, 1, 1))
                        coefficients(mv2, c2, ln_eps, i, POOL_PER, coef2_ready)
                        pool.wait_ge(rows_stored, batch_no(i, u, 32, LEAD_DMA))
                        pool.sem_inc(pool_at, 1)
                        for t in range(NT):
                            last = pool.tensor_scalar(n2[:, t, :], res[:, u % 2, t, :], c2[:, 2, t:t + 1],
                                                      c2[:, 3, t:t + 1], ALU.mult, ALU.add)
                        last.then_inc(n2_ready, 1)
                    if s == "scatter":
                        pool.wait_ge(rec_ready, batch_no(i, u, 1, 1))
                        pool.sem_inc(pool_at, 1)
                        for t in range(NT):
                            for c in range(2):
                                pool.indirect_dma_start(
                                    slot_d, bass.IndirectOffsetOnAxis(ap=pos[:, t, c:c + 1], axis=0),
                                    rec[:, t, c, :], None).then_inc(slots_stored, 16)
                        pool.wait_ge(slots_stored, batch_no(i, u, 128, 128))
                        pool.sem_inc(slots_done, 1)

            all_batches(pool, batches, count, POOL_PER)

            n_kind = load_counts(pool)
            pool.wait_ge(rows_stored, LEAD_DMA + 32 * B)
            for u in range(2):
                pool.wait_ge(x1_stored[u], LEAD_DMA + 16 * (B // 2))
            pool.wait_ge(pads_stored, PAD_DMAS)
            tile_lead(pool, (m_added, 1), (k_added, 1), (k_cf, 6))

            def gather(kind, i, u):
                source, rec_sem, xT_sem, x_sem, dst = ((h2_d, m_grec, m_xT, m_x, m_rows),
                                                       (n2_d, k_grec, k_xT, k_x, k_rows))[kind]
                n = len(x_sem)
                pool.wait_ge(rec_sem[u % RECS], use_no(RECS, i, u, 16))
                pool.wait_ge(xT_sem, tile_no(i * RECS + u, back=n))
                pool.sem_inc(pool_at, 1)
                for q in range(Q4):
                    pool.indirect_dma_start(dst[:, u % n, q, :], None, source, bass.IndirectOffsetOnAxis(
                        ap=grec[:, kind, u % RECS, q, 0:1], axis=0)).then_inc(x_sem[u % n], 16)

            def scatter_add(kind, i, u):
                y_sem, add_sem, added, src = ((m_y, m_add, m_added, m_res), (k_y, k_add, k_added, k_res))[kind]
                k = i * RECS + u
                pool.wait_ge(y_sem, tile_no(k))
                pool.sem_inc(pool_at, 1)
                for q in range(Q4):
                    pool.indirect_dma_start(acc_d, bass.IndirectOffsetOnAxis(ap=srec[:, kind, u, q, 0:1], axis=0),
                                            src[:, u % 2, q, :], None, compute_op=ALU.add).then_inc(add_sem, 16)

            def end_of_add(kind, i, u):
                add_sem, added = ((m_add, m_added), (k_add, k_added))[kind]
                pool.wait_ge(add_sem, (i * RECS + u) * 64 + 64)
                pool.sem_inc(added, 1)

            def hidden_coefficients(i, u):
                k = i * RECS + u
                pool.wait_ge(k_st, tile_no(k))
                for c, (a, b_, op) in enumerate((
                        (zmv[:, :, 1], kconst[:, 0, :], ALU.mult), (zc[:, 0, :], kconst[:, 2, :], ALU.add),
                        (zc[:, 1, :], half, ALU.pow), (zc[:, 2, :], kconst[:, 1, :], ALU.mult),
                        (zmv[:, :, 0], zc[:, 3, :], ALU.mult), (zc[:, 4, :], minus, ALU.mult))):
                    pool.tensor_tensor(zc[:, c, :], a, b_, op).then_inc(k_cf, 1)
                    if c < 5:
                        pool.wait_ge(k_cf, tile_no(k, 6, c + 1))

            for kind, u in ((0, 0), (0, 1), (1, 0), (0, 2), (1, 1), (0, 3)):
                with pool.If(n_kind[kind] > u):
                    gather(kind, 0, u)
            with pool.Fori(0, TILES // RECS) as i:
                with pool.If(i * RECS < n_kind[0]):
                    for u in range(RECS):
                        k = i * RECS + u
                        with pool.If(k < n_kind[0]):
                            scatter_add(0, i, u)
                        with pool.If(k + 4 < n_kind[0]):
                            gather(0, i, u + 4)
                        with pool.If(k < n_kind[0]):
                            end_of_add(0, i, u)
            with pool.If(n_kind[1] > 0):
                hidden_coefficients(0, 0)
            with pool.If(n_kind[1] > 2):
                gather(1, 0, 2)
            with pool.Fori(0, TILES // RECS) as i:
                with pool.If(i * RECS < n_kind[1]):
                    for u in range(RECS):
                        k = i * RECS + u
                        with pool.If(k + 1 < n_kind[1]):
                            hidden_coefficients(i, u + 1)
                        with pool.If(k + 3 < n_kind[1]):
                            gather(1, i, u + 3)
                        with pool.If(k < n_kind[1]):
                            scatter_add(1, i, u)
                            end_of_add(1, i, u)
            pool.sem_inc(all_added, 1)

        @blk.scalar
        def _(act):
            act.sem_inc(y_out[1], LEAD)
            act.wait_ge(prep_mm, 1)
            act.activation(w_T[:], slot(0)[:, 0, 0:D], ACT.Copy).then_inc(act_prep, 1)
            act.wait_ge(prep_mm, 2)
            act.activation(w_u[:], slot(1)[:, 0, 0:D], ACT.Copy).then_inc(act_prep, 1)

            def front(s, bf, u, job, i):
                wait_filled(act, job, i)
                src = slot(job)
                if s == "hT":
                    act.activation(hT[:], src[:, 0, :], ACT.Copy).then_inc(freed[job % SLOTS], 1)
                if s in SPLIT:
                    if s == "q" and not (isinstance(bf, int) and bf == 0):
                        act.wait_ge(hl_stored, bf * 32)
                    act.activation(hi[:, SPLIT.index(s), :], src[:, 0, :], ACT.Copy).then_inc(hi_ready, 1)
                if s == "v":
                    act.wait_ge(ones_column, 1)
                    act.activation(vaug[:, u, :, :, 0:DH], src[:, 0, :].rearrange(
                        "p (t h d) -> p t h d", t=NT, h=H), ACT.Copy).then_inc(freed[job % SLOTS], 1)

            for s in FRONT:
                front(s, 0, 0, FRONT.index(s), 0)
            act.wait_ge(zeroed, 1)
            for m in range(1, 3):
                last = act.activation(stack[1][m][:].bitcast(F32), stack[1][0][:].bitcast(F32), ACT.Copy)
            last.then_inc(stack1_zeroed, 1)
            act.wait_ge(pads_stored, PAD_DMAS)

            def batches(steps, jobs, i):
                for s, n, j, u in steps:
                    b = i * 2 + u
                    p = u % 2
                    if s in FRONT:
                        front(s, b + 1, 1 - p, jobs[(s, n, 0, u)], i)
                    if s == "mT":
                        job = jobs[(s, n, 0, u)]
                        wait_filled(act, job, i)
                        act.wait_ge(mrow_loaded, batch_no(i, u, 16, LEAD_DMA))
                        act.activation(mT16[:], slot(job)[0:H, 0, :], ACT.Copy, scale=-1.0).then_inc(mT_ready, 1)
                        act.wait_ge(mT_ready, batch_no(i, u, 1, 1))
                        act.sem_inc(freed[job % SLOTS], 1)
                    if s == "lin" and j < 2:
                        job = jobs[(s, n, j, u)]
                        wait_filled(act, job, i)
                        if j == 0:
                            act.wait_ge(pv_done, batch_no(i, u, 8, LEAD + max(n - 1, 0)))
                        act.activation(Pb[:, n % 2, 1024 * j:1024 * (j + 1)].rearrange("p (k q) -> p k q", k=2),
                                       slot(job), ACT.Square, bias=1.0).then_inc(freed[job % SLOTS], 1)
                    if s == "lin" and j >= 2:
                        hd = j - 2
                        job = jobs[(s, n, j, u)]
                        wait_filled(act, job, i)
                        act.activation(Pb[:, n % 2, 2048 + 768 * hd:2048 + 768 * (hd + 1)].rearrange(
                            "p (k q) -> p k q", k=2), slot(job)[:, :, 0:384], ACT.Square,
                            bias=1.0).then_inc(freed[job % SLOTS], 1)
                    if s == "win":
                        c = j
                        job = jobs[(s, n, c, u)]
                        wq = WQ if c < NT - 1 else P
                        wait_filled(act, job, i)
                        if c == 0:
                            act.wait_ge(pv_done, batch_no(i, u, 8, LEAD + n - 1))
                        act.activation(
                            Pb[:, n % 2, 768 * c:768 * (c + 1)].rearrange(
                                "p (k j q) -> p k j q", k=2, j=2)[:, :, :, 0:wq],
                            slot(job)[:, :, 0:384].rearrange("p k (j q) -> p k j q", j=2)[:, :, :, 0:wq],
                            ACT.Exp).then_inc(freed[job % SLOTS], 1)
                    if s == "pv" and n % 2 == 1:
                        act.wait_ge(pv_done, batch_no(i, u, 8, LEAD + n + 1))
                        act.activation(y_sb[:, (n // 2) % 2, 1, :], pv[:, 1, :], ACT.Copy
                                       ).then_inc(y_out[1], 1)
                    if s in ("ycT", "h2T"):
                        job = jobs[(s, n, 0, u)]
                        wait_filled(act, job, i)
                        if s == "ycT":
                            act.activation(ycT[:], slot(job)[:], ACT.Copy).then_inc(freed[job % SLOTS], 1)
                        else:
                            act.activation(h2T[:], slot(job)[:, 0, :], ACT.Copy).then_inc(freed[job % SLOTS], 1)
                    if s == "gapexp":
                        act.wait_ge(gap_ready, batch_no(i, u, 1, 1))
                        act.activation(sc[:, 7, :], sc[:, 6, :], ACT.Exp).then_inc(exp_ready, 1)

            all_batches(act, batches)

            n_kind = load_counts(act)
            tile_lead(act, (m_g, F // P), (k_sig[0], G), (k_sig[1], 2 * G))

            def hidden(i, u):
                k = i * RECS + u
                act.wait_ge(m_w1[u % 2], use_no(2, i, u, 32))
                act.wait_ge(m_mm, tile_no(k, back=2))
                for f in range(F // P):
                    act.wait_ge(m_h, tile_no(k, F // P, f + 1))
                    act.activation(gelu[:, 4 * (u % 2) + f, :], ring[:, f // 2, f % 2, :], ACT.Gelu,
                                   bias=mprm[:, u % RECS, f:f + 1]).then_inc(m_g, 1)

            with act.If(n_kind[0] > 0):
                hidden(0, 0)
            with act.Fori(0, TILES // RECS) as i:
                with act.If(i * RECS < n_kind[0]):
                    for u in range(RECS):
                        k = i * RECS + u
                        with act.If(k + 1 < n_kind[0]):
                            hidden(i, u + 1)

            def sigmoids(z, i, u):
                k = i * RECS + u
                if z == 0:
                    act.wait_ge(k_w0[u % 2], use_no(2, i, u, 64))
                    act.wait_ge(k_xT, tile_no(k))
                else:
                    act.wait_ge(k_hT, tile_no(k))
                for g in range(STEPS[z]):
                    f = g // G
                    act.wait_ge(k_bas[z], tile_no(k, STEPS[z], g + 1 - SIGS))
                    prm = kprm[:, u % RECS]
                    if z == 0:
                        src, scale, bias = pv[:, 0, :], prm[:, 0:1], prm[:, 1 + g:2 + g]
                    else:
                        src, scale, bias = ring[:, 1, f, :], prm[:, 9 + f:10 + f], prm[:, 11 + g:12 + g]
                    act.activation(sig[z][:, g % SIGS, :], src, ACT.Sigmoid, bias=bias, scale=scale
                                   ).then_inc(k_sig[z], 1)

            for u in range(2):
                with act.If(n_kind[1] > u):
                    sigmoids(0, 0, u)
            with act.Fori(0, TILES // RECS) as i:
                with act.If(i * RECS < n_kind[1]):
                    for u in range(RECS):
                        k = i * RECS + u
                        with act.If(k < n_kind[1]):
                            sigmoids(1, i, u)
                        with act.If(k + 2 < n_kind[1]):
                            sigmoids(0, i, u + 2)

        @blk.vector
        def _(dve):
            count = [0]

            def link(ins, i=0, per=0):
                count[0] += 1
                ins.then_inc(dve_chain, 1)
                dve.wait_ge(dve_chain, i * per + count[0])

            def norm_stats(bf):
                dve.wait_ge(x_loaded, bf * 16 + 16)
                return [dve.bn_stats(stats[:, t, :], xb[:, t, :]) for t in range(NT)][-1]

            def aggregate(st, m):
                return [dve.bn_aggr(m[:, t, :], st[:, t, :]) for t in range(NT)][-1]

            dve.sem_inc(y_out[0], LEAD)
            dve.memset(stack[1][0][:].bitcast(F32), 0.0).then_inc(zeroed, 1)
            link(norm_stats(0))
            aggregate(stats, mv).then_inc(stats_ready, 1)
            dve.wait_ge(w_loaded, 16 * W_DMAS)
            dve.wait_ge(const_ready, 2)
            dve.tensor_copy(qf_rep[:], qf_in[:].unsqueeze(1).to_broadcast([FEAT, H, DH]))
            dve.tensor_copy(kf_rep[:], kf_in[:].unsqueeze(1).to_broadcast([FEAT, H, DH]))
            dve.tensor_scalar(w_n[:, 0, :], w_raw[:, 0, :], nw[:], DH ** -0.5, ALU.mult, ALU.mult)
            dve.tensor_scalar(w_n[:, 1, :], w_raw[:, 1, :], nw[:], None, ALU.mult)
            dve.tensor_scalar(w_n[:, 2, :], w_raw[:, 2, :], nw[:], None, ALU.mult)
            dve.tensor_scalar(w_n[:, 3, :], w_raw[:, 0, :], nw[:], None, ALU.mult).then_inc(prep_dve, 1)
            dve.wait_ge(prep_mm, 1)
            dve.tensor_tensor(m_blk[:], slot(0)[:, 1, 0:P], block[:], ALU.mult).then_inc(prep_dve, 1)
            dve.wait_ge(zeroed, 1)
            for m in range(3):
                last = dve.tensor_copy(stack[0][m][:], stack[1][0][:])
            last.then_inc(stack0_zeroed, 1)

            def front(s, bf, u, job, i):
                wait_filled(dve, job, i)
                m = SPLIT.index(s)
                dve.wait_ge(hi_ready, bf * 3 + m + 1)
                dve.tensor_tensor(lo[:, m, :], slot(job)[:, 0, :], hi[:, m, :], ALU.subtract
                                  ).then_inc(lo_ready, 1)
                dve.wait_ge(lo_ready, bf * 3 + m + 1)
                dve.sem_inc(freed[job % SLOTS], 1)

            for s in FRONT:
                if s in SPLIT:
                    front(s, 0, 0, FRONT.index(s), 0)
            link(dve.memset(vaug[:], 0.0))
            dve.memset(vaug[:, :, :, :, DH:DH + 1], 1.0).then_inc(ones_column, 1)
            dve.memset(pv[:], 0.0).then_inc(pv_zeroed, 1)
            dve.wait_ge(pads_ready, 1)
            pads = pad_rec.rearrange("p (s w) -> p s w", w=2)
            link(dve.tensor_scalar(pads[:, :, 0], pads[:, :, 0], TS - 1, None, ALU.bitwise_and))
            dve.tensor_scalar(pads[:, :, 1], pads[:, :, 0], 0.0, None, ALU.mult)
            dve.tensor_copy(ids_f[:], rec[:, :, 0, 0])
            dve.tensor_copy(carry[:], first_slot[:])
            dve.tensor_copy(tile_idx[:], tab_i[:, 0:2])
            link(dve.tensor_scalar(tile_idx4[:], tab_i[:, 0], -float(Q4), None, ALU.mult))
            dve.tensor_scalar(pads[:, :, 0], pads[:, :, 0], float(TOK), None, ALU.add).then_inc(pads_ready, 1)
            dve.wait_ge(kp_loaded, 16 * 10)
            for e in range(E2):
                dve.tensor_copy(kp_all[:, e, 0:1], kp_raw[:, e, 0:1])
                dve.tensor_copy(kp_all[:, e, 9:11], kp_raw[:, e, 2:4])
                for dst, src in ((1, 1), (11, 4), (19, 5)):
                    last = dve.scalar_tensor_tensor(kp_all[:, e, dst:dst + G], grid_sb[:], -1.0,
                                                    kp_raw[:, e, src:src + 1].to_broadcast([P, G]),
                                                    ALU.mult, ALU.add)
            last.then_inc(kp_ready, 1)
            link(dve.tensor_scalar(bias_in[:, 0:KB], bias_in[:, 0:KB], -0.25, None, ALU.mult))
            link(dve.tensor_copy(bias3[:, 0], bias_in))
            link(dve.tensor_tensor(bias_rest[:, 0], bias_in, bias3[:, 0], ALU.subtract))
            link(dve.tensor_copy(bias3[:, 1], bias_rest[:, 0]))
            link(dve.tensor_tensor(bias_rest[:, 1], bias_rest[:, 0], bias3[:, 1], ALU.subtract))
            dve.tensor_copy(bias3[:, 2], bias_rest[:, 1]).then_inc(kp_ready, 1)
            dve.wait_ge(const_ready, 3)
            dve.wait_ge(pads_stored, PAD_DMAS)
            DVE_PER = 16
            ROUTE = 16
            step = [0]

            def chain(ins, i, u, wait=True):
                step[0] += 1
                ins.then_inc(route_chain, 1)
                if wait:
                    dve.wait_ge(route_chain, batch_no(i, u, ROUTE, step[0]))

            def batches(steps, jobs, i):
                for s, n, j, u in steps:
                    b = i * 2 + u
                    p = u % 2
                    if s in SPLIT:
                        front(s, b + 1, 1 - p, jobs[(s, n, 0, u)], i)
                    if s == "max":
                        c = j
                        job = jobs[(s, n, c, u)]
                        wait_filled(dve, job, i)
                        k0 = WIN if c == 0 else 0
                        dve.sem_inc(dve_at, 1)
                        for hh in range(HG):
                            red = dve.tensor_tensor_reduce(
                                masked[:, (NT * n + c) % SLOTS, hh, k0:WQ],
                                slot(job)[:, hh // 2, WQ * (hh % 2) + k0:WQ * (hh % 2 + 1)], mask_max[:, k0:WQ],
                                1.0, NEG, ALU.add, ALU.max, maxima[:, c, HG * n + hh:HG * n + hh + 1])
                        red.then_inc(freed[job % SLOTS], 1)
                    if s == "stats":
                        link(norm_stats(b + 1), i, DVE_PER)
                    if s == "aggr":
                        aggregate(stats, mv).then_inc(stats_ready, 1)
                    if s == "pv" and n % 2 == 0:
                        dve.wait_ge(pv_done, batch_no(i, u, 8, LEAD + n + 1))
                        dve.tensor_copy(y_sb[:, (n // 2) % 2, 0, :], pv[:, 0, :]).then_inc(y_out[0], 1)
                    if s == "ytr":
                        job = jobs[(s, n, 0, u)]
                        wait_filled(dve, job, i)
                        y = slot(job).rearrange("p k (a c) -> p k a c", c=32)
                        z = y[:, :, :, DH]
                        kind, rz = n // 2, rz4[:, n].rearrange("p (k a) -> p k a", k=2)
                        if kind == 0:
                            link(dve.tensor_scalar(rz, z, LIN_EPS, None, ALU.add), i, DVE_PER)
                            link(dve.reciprocal(rz, rz), i, DVE_PER)
                        else:
                            link(dve.reciprocal(rz, z), i, DVE_PER)
                        for bk in range(2):
                            hg = (2 * n + bk) % 4
                            last = dve.tensor_tensor(
                                ycat[:, :, kind, 32 * hg:32 * (hg + 1)].rearrange("p t (j d) -> p t j d", j=HG),
                                y[:, bk].rearrange("p (t j) c -> p t j c", t=NT)[:, :, :, 0:DH],
                                rz[:, bk].rearrange("p (t j) -> p t j", t=NT).unsqueeze(3)
                                .to_broadcast([P, NT, HG, DH]), ALU.mult)
                        last.then_inc(freed[job % SLOTS], 1)
                    if s == "out":
                        job = jobs[(s, n, 0, u)]
                        wait_filled(dve, job, i)
                        dve.wait_ge(xres_ready, batch_no(i, u, 1, 1))
                        dve.tensor_tensor(res[:, p].rearrange("p t d -> p (t d)"), slot(job)[:, 0, :],
                                          res[:, p].rearrange("p t d -> p (t d)"), ALU.add).then_inc(x1_ready, 1)
                        dve.wait_ge(x1_ready, batch_no(i, u, 1, 1))
                        dve.sem_inc(freed[job % SLOTS], 1)
                        link([dve.bn_stats(stats2[:, t, :], res[:, p, t, :]) for t in range(NT)][-1], i, DVE_PER)
                        dve.tensor_copy(spacer[:], stats2[:, 0, 0:1])
                        aggregate(stats2, mv2).then_inc(stats2_ready, 1)
                    if s == "h2norm":
                        dve.wait_ge(coef2_ready, batch_no(i, u, 1, 1))
                        dve.wait_ge(rows_stored, batch_no(i, u, 32, LEAD_DMA))
                        for t in range(NT):
                            last = dve.tensor_scalar(h2[:, t, :], res[:, p, t, :], c2[:, 0, t:t + 1],
                                                     c2[:, 1, t:t + 1], ALU.mult, ALU.add)
                        last.then_inc(h2_ready, 1)
                    if s == "logit":
                        job = jobs[(s, n, 0, u)]
                        wait_filled(dve, job, i)
                        logit = slot(job)[:, 0, 0:NT * E].rearrange("p (t e) -> p t e", e=E)
                        dve.wait_ge(slots_done, batch_no(i, u, 1, LEAD))
                        dve.tensor_copy(lg[:, 0], logit).then_inc(freed[job % SLOTS], 1)
                        dve.wait_ge(freed[job % SLOTS], fill_no(job, i))

                    if s == "choose":
                        def over_e(row):
                            return sc[:, row, :].unsqueeze(2).to_broadcast([P, NT, E])

                        step[0] = 0
                        for c in range(2):
                            chain(dve.tensor_reduce(sc[:, c, :], lg[:, c], AX.X, ALU.max), i, u)
                            chain(dve.tensor_tensor(lg[:, 2], lg[:, c], over_e(c), ALU.is_equal), i, u)
                            chain(dve.tensor_tensor(lg[:, 5], lg[:, 2], prefer[:], ALU.mult), i, u)
                            chain(dve.tensor_reduce(sc[:, 2 + c, :], lg[:, 5], AX.X, ALU.max), i, u)
                            chain(dve.tensor_tensor(lg[:, 3 + c], prefer[:], over_e(2 + c), ALU.is_equal), i, u)
                            if c == 0:
                                chain(dve.scalar_tensor_tensor(lg[:, 1], lg[:, 3], NEG, lg[:, 0], ALU.mult,
                                                               ALU.add), i, u)
                        dve.tensor_tensor(sel[:], lg[:, 3], lg[:, 4], ALU.add).then_inc(sel_ready, 1)
                        dve.tensor_tensor(sc[:, 6, :], sc[:, 1, :], sc[:, 0, :], ALU.subtract).then_inc(gap_ready, 1)
                    if s == "rank":
                        job = jobs[(s, n, 0, u)]
                        wait_filled(dve, job, i)
                        dve.tensor_tensor(lg[:, 6], slot(job)[:, 0, 0:NT * E].rearrange("p (t e) -> p t e", e=E),
                                          carry[:].unsqueeze(1).to_broadcast([P, NT, E]), ALU.add
                                          ).then_inc(freed[job % SLOTS], 1)
                        dve.wait_ge(freed[job % SLOTS], fill_no(job, i))
                    if s == "weights":
                        dve.wait_ge(exp_ready, batch_no(i, u, 1, 1))
                        w = rec[:].bitcast(F32)
                        chain(dve.tensor_scalar(sc[:, 8, :], sc[:, 7, :], 1.0, None, ALU.add), i, u, False)
                        chain(dve.tensor_tensor(lg[:, 1:3], lg[:, 6].unsqueeze(1).to_broadcast([P, 2, NT, E]),
                                                lg[:, 3:5], ALU.mult), i, u)
                        chain(dve.reciprocal(w[:, :, 0, 1], sc[:, 8, :]), i, u, False)
                        chain(dve.tensor_reduce(sc[:, 10:12, :], lg[:, 1:3], AX.X, ALU.add), i, u)
                        dve.tensor_tensor(w[:, :, 1, 1], w[:, :, 0, 1], sc[:, 7, :], ALU.mult)
                        for c in range(2):
                            dve.tensor_copy(rec[:, :, c, 0], ids_f[:])
                        dve.tensor_copy(pos[:].rearrange("p t c -> p c t"), sc[:, 10:12, :]).then_inc(rec_ready, 1)
                        chain(dve.tensor_scalar(ids_f[:], ids_f[:], float(T), None, ALU.add), i, u, False)
                        assert step[0] == ROUTE, step[0]
                    if s == "total":
                        job = jobs[(s, n, 0, u)]
                        wait_filled(dve, job, i)
                        dve.tensor_tensor(carry[:], slot(job)[:, 0, 0:E], carry[:], ALU.add
                                          ).then_inc(freed[job % SLOTS], 1)

            all_batches(dve, batches, count, DVE_PER)

            total_job = JOBS_LAST[("total", 0, 0, 1)]
            dve.wait_ge(freed[total_job % SLOTS], fill_no(total_job, TURNS))
            link(dve.tensor_tensor(tab_e[:, 0].rearrange("a k e -> a (k e)"), carry[0:1, :], first_slot[0:1, :],
                                   ALU.subtract))
            dve.tensor_scalar(tab_e[:, 1], tab_e[:, 0], float(P - 1), None, ALU.add)
            link(dve.tensor_scalar(tab_e[:, 2], tab_e[:, 0], float(TS - 1), None, ALU.add))
            link(dve.tensor_copy(cnt_i[:], tab_e[:, 1:3]))
            dve.tensor_scalar(cnt_i[:, 0], cnt_i[:, 0], P.bit_length() - 1, None, ALU.logical_shift_right)
            link(dve.tensor_scalar(cnt_i[:, 1], cnt_i[:, 1], TS.bit_length() - 1, None, ALU.logical_shift_right))
            link(dve.tensor_copy(tab_e[:, 3:5], cnt_i[:]))
            dve.tensor_scalar(tab_e[:, 6], tab_e[:, 4], -1.0, float(TOK // TS), ALU.mult, ALU.add)
            dve.scalar_tensor_tensor(tab_e[:, 7, :, 0:E2 - 1], tab_e[:, 4, :, 0:E2 - 1], float(Q4),
                                     tab_e[:, 3, :, 0:E2 - 1], ALU.mult, ALU.subtract)
            link(dve.tensor_copy(tab_e[:, 5, :, 0:1], tab_e[:, 4, :, 0:1]))
            for e in range(1, E2):
                link(dve.tensor_tensor(tab_e[:, 5, :, e:e + 1], tab_e[:, 5, :, e - 1:e], tab_e[:, 4, :, e:e + 1],
                                       ALU.add))
            link(dve.tensor_tensor(tab_e[:, 7, :, 0:E2 - 1], tab_e[:, 7, :, 0:E2 - 1], tab_e[:, 3, :, 1:E2], ALU.add))
            grid3 = space[4][0:1, 0:3 * 2 * (E2 - 1) * ENTRIES].rearrange(
                "a (r k j t) -> a r k j t", r=3, k=2, j=E2 - 1)
            sums = space[4][0:1, 2048:2048 + 4 * 2 * ENTRIES].rearrange("a (r k t) -> a r k t", r=4, k=2)
            shape = [1, E2 - 1, ENTRIES]
            for kind in range(2):
                last = dve.tensor_tensor(grid3[:, 0, kind], tile_idx[:, 0, kind].unsqueeze(1).to_broadcast(shape),
                                         tab_e[:, 5, kind, 0:E2 - 1].unsqueeze(2).to_broadcast(shape), ALU.is_ge)
            link(last)
            for row in range(2):
                for kind in range(2):
                    last = dve.tensor_tensor(grid3[:, 1 + row, kind], grid3[:, 0, kind],
                                             tab_e[:, 6 + row, kind, 0:E2 - 1].unsqueeze(2).to_broadcast(shape),
                                             ALU.mult)
            link(last)
            for row in range(2):
                for kind in range(2):
                    last = dve.tensor_reduce(sums[:, row, kind], grid3[:, 1 + row, kind].rearrange("a j t -> a t j"),
                                             AX.X, ALU.add)
            link(last)
            dve.tensor_tensor(sums[:, 2], sums[:, 0], tile_idx[:, 1], ALU.add)
            link(dve.tensor_tensor(sums[:, 3], sums[:, 1], tile_idx4[:], ALU.add))
            for kind in range(2):
                dve.tensor_scalar(sums[:, 0, kind], sums[:, 2, kind], float((kind + 1) * E2 * TOK // TS - 1), None,
                                  ALU.min)
            link(dve.tensor_tensor(sums[:, 1], sums[:, 3], tab_e[:, 3, :, 0:1].to_broadcast([1, 2, ENTRIES]), ALU.add))
            dve.tensor_copy(tab_i[:, 0], sums[:, 0])
            link(dve.tensor_scalar(sums[:, 2], sums[:, 1], float(Q4), 0.0, ALU.min, ALU.max))
            dve.tensor_scalar(tab_i[:, 1], tab_i[:, 0], (TOK // TS).bit_length() - 1, None, ALU.logical_shift_right)
            dve.tensor_copy(tab_i[:, 2], sums[:, 2])
            link(dve.tensor_copy(n_i[:].unsqueeze(2), tab_e[:, 5, :, E2 - 1:E2]))
            dve.wait_ge(slots_done, LEAD + B)
            dve.sem_inc(table_ready, 1)

            n_kind = load_counts(dve)
            tile_lead(dve, (m_xs, 1), (m_y, 1), (k_y, 1), (k_st2, 1), (k_st, 1), (k_zn, 1), (k_bas[0], G),
                      (k_bas[1], 2 * G))
            weight = srec[:].bitcast(F32)

            def copy_rows(i, u):
                k = i * RECS + u
                dve.wait_ge(m_xT, tile_no(k))
                dve.wait_ge(m_h, tile_no(k, F // P, back=1))
                dve.tensor_copy(mxs, pv[:, 0, :]).then_inc(m_xs, 1)

            def weighted(kind, i, u):
                k = i * RECS + u
                rec_sem, added, mm_sem, per, dst, y_sem = (
                    (m_srec, m_added, m_mm, 1, m_res, m_y), (k_srec, k_added, k_mm[1], 2 * G, k_res, k_y))[kind]
                dve.wait_ge(rec_sem[u], use_no(RECS, i, u, 16))
                dve.wait_ge(added, tile_no(k, back=2))
                dve.wait_ge(mm_sem, tile_no(k, per))
                for q in range(Q4):
                    last = dve.tensor_scalar(dst[:, u % 2, q, :], pv[:, 1, P * q:P * (q + 1)],
                                             weight[:, kind, u, q, 1:2], (1.0, -4.0)[kind], ALU.mult, ALU.mult)
                last.then_inc(y_sem, 1)

            def basis_functions(z, i, u, steps):
                k = i * RECS + u
                for g in steps:
                    dve.wait_ge(k_sig[z], tile_no(k, STEPS[z], g + 1))
                    dve.wait_ge(k_mm[z], tile_no(k, STEPS[z], g + 1 - G))
                    s_ = sig[z][:, g % SIGS, :]
                    dve.scalar_tensor_tensor(basis[z][:, g % G, :], s_, -1.0, s_, ALU.add, ALU.mult
                                             ).then_inc(k_bas[z], 1)

            def z_rows(q):
                return ring[:, 0, q // 2, F2 * (q % 2):F2 * (q % 2 + 1)]

            def hidden_stats(i, u):
                k = i * RECS + u
                dve.wait_ge(k_mm[0], tile_no(k, G))
                for q in range(Q4):
                    last = dve.bn_stats(zst[:, q, :], z_rows(q))
                last.then_inc(k_st2, 1)
                dve.wait_ge(k_st2, tile_no(k))
                dve.tensor_copy(spacer[:], zst[:, 0, 0:1])
                for q in range(Q4):
                    last = dve.bn_aggr(zmv[:, q, :], zst[:, q, :])
                last.then_inc(k_st, 1)

            def hidden_norm(i, u):
                k = i * RECS + u
                dve.wait_ge(k_cf, tile_no(k, 6))
                dve.wait_ge(k_hT, tile_no(k, back=1))
                for q in range(Q4):
                    last = dve.tensor_scalar(zn[:, q, :], z_rows(q), zc[:, 3, q:q + 1], zc[:, 5, q:q + 1],
                                             ALU.mult, ALU.add)
                last.then_inc(k_zn, 1)

            for u in range(2):
                with dve.If(n_kind[0] > u):
                    copy_rows(0, u)
            with dve.Fori(0, TILES // RECS) as i:
                with dve.If(i * RECS < n_kind[0]):
                    for u in range(RECS):
                        k = i * RECS + u
                        with dve.If(k + 2 < n_kind[0]):
                            copy_rows(i, u + 2)
                        with dve.If(k < n_kind[0]):
                            weighted(0, i, u)
            with dve.If(n_kind[1] > 0):
                basis_functions(0, 0, 0, range(G))
                hidden_stats(0, 0)
                hidden_norm(0, 0)
            with dve.If(n_kind[1] > 1):
                basis_functions(0, 0, 1, range(G))
            with dve.Fori(0, TILES // RECS) as i:
                with dve.If(i * RECS < n_kind[1]):
                    for u in range(RECS):
                        k = i * RECS + u
                        with dve.If(k < n_kind[1]):
                            basis_functions(1, i, u, range(0, G))
                        with dve.If(k + 1 < n_kind[1]):
                            hidden_stats(i, u + 1)
                        with dve.If(k < n_kind[1]):
                            basis_functions(1, i, u, range(G, G + 2))
                        with dve.If(k + 1 < n_kind[1]):
                            hidden_norm(i, u + 1)
                        with dve.If(k < n_kind[1]):
                            basis_functions(1, i, u, range(G + 2, 2 * G))
                        with dve.If(k + 2 < n_kind[1]):
                            basis_functions(0, i, u + 2, range(G))
                        with dve.If(k < n_kind[1]):
                            weighted(1, i, u)

        @blk.tensor
        def _(pe):
            pe.sem_inc(pv_done, LEAD)
            pe.wait_ge(const_ready, 2)
            pe.wait_ge(prep_dve, 1)
            pe.transpose(slot(0)[:, 0, 0:P], w_n[:, 3, :], identf[:])
            pe.matmul(slot(0)[:, 1, 0:P], qf_rep[:].rearrange("f h d -> f (h d)"),
                      kf_rep[:].rearrange("f h d -> f (h d)"), start=True, stop=True).then_inc(prep_mm, 1)
            pe.wait_ge(act_prep, 1)
            pe.wait_ge(prep_dve, 2)
            pe.matmul(slot(1)[:, 0, 0:D], w_T[:], m_blk[:], start=True, stop=True).then_inc(prep_mm, 1)
            pe.wait_ge(act_prep, 2)

            def front(s, bf, u, job, i, jobs):
                if s == "hT":
                    pe.wait_ge(hn_ready, bf + 1)
                if s == "q":
                    hT_job = FRONT.index("hT") if jobs is None else jobs[("hT", 0, 0, u)]
                    pe.wait_ge(freed[hT_job % SLOTS], fill_no(hT_job, i))
                wait_freed(pe, job, i)
                dst = slot(job)
                if s == "hT":
                    for t in range(NT):
                        mm = pe.transpose(dst[:, 0, P * t:P * (t + 1)], hn[:, t, :], identf[:])
                if s in SPLIT:
                    w = {"q": w_n[:, 0, :], "k": w_n[:, 1, :], "u": w_u[:]}[s]
                    mm = pe.matmul(dst[:, 0, :], w, hT[:], start=True, stop=True)
                if s == "v":
                    for t in range(NT):
                        mm = pe.matmul(dst[:, 0, P * t:P * (t + 1)], hT[:, P * t:P * (t + 1)], w_n[:, 2, :],
                                       start=True, stop=True)
                mm.then_inc(filled[job % SLOTS], 1)

            for s in FRONT:
                front(s, 0, 0, FRONT.index(s), 0, None)
            for u in range(2):
                pe.wait_ge(ones_loaded[u], 16)
            pe.wait_ge(const_ready, 3)
            pe.wait_ge(pv_zeroed, 1)
            pe.wait_ge(wout_loaded, 32)

            def batches(steps, jobs, i):
                for s, n, j, u in steps:
                    b = i * 2 + u
                    p = u % 2
                    sq, sk, su = (stack[p][m][:].rearrange("r (h t) -> r h t", h=H) for m in range(3))
                    if s in FRONT:
                        front(s, b + 1, u, jobs[(s, n, 0, u)], i, jobs)
                    if s == "begin":
                        pe.wait_ge(stack_loaded[p], i * 160 + (u // 2 * 160 + 160))
                    if s == "max":
                        c = j
                        job = jobs[(s, n, c, u)]
                        wait_freed(pe, job, i)
                        k0 = WIN if c == 0 else 0
                        for bk in range(2):
                            for jj in range(2):
                                h = HG * n + 2 * bk + jj
                                mm = pe.matmul(slot(job)[:, bk, WQ * jj + k0:WQ * (jj + 1)],
                                               sq[:, h, P * c:P * (c + 1)],
                                               sk[:, h, P * c - WIN + k0:P * (c + 1)],
                                               start=True, stop=True)
                        mm.then_inc(filled[job % SLOTS], 1)
                    if s == "mT":
                        job = jobs[(s, n, 0, u)]
                        wait_freed(pe, job, i)
                        last_max = jobs[("max", NHG - 1, NT - 1, u)]
                        pe.wait_ge(freed[last_max % SLOTS], fill_no(last_max, i))
                        for c in range(NT):
                            mm = pe.transpose(slot(job)[0:H, 0, P * c:P * (c + 1)], maxima[:, c, :], identf[:])
                        mm.then_inc(filled[job % SLOTS], 1)
                    if s == "lin" and j < 2:
                        job = jobs[(s, n, j, u)]
                        wait_freed(pe, job, i)
                        for bk in range(2):
                            c = 2 * j + bk
                            for hd in range(HG):
                                mm = pe.matmul(slot(job)[:, bk, P * hd:P * (hd + 1)],
                                               sk[:, HG * n + hd, P * c:P * (c + 1)],
                                               su[:, HG * n + hd, P * c:P * (c + 1)], start=True, stop=True)
                        mm.then_inc(filled[job % SLOTS], 1)
                    if s == "lin" and j >= 2:
                        job = jobs[(s, n, j, u)]
                        wait_freed(pe, job, i)
                        for bk, o, c in ((0, 0, 0), (1, 0, 1), (1, 256, 2)):
                            w = T - P * (c + 1)
                            mm = pe.matmul(slot(job)[:, bk, o:o + w],
                                           sk[:, HG * n + j - 2, P * c:P * (c + 1)],
                                           su[:, HG * n + j - 2, P * (c + 1):T], start=True, stop=True)
                        mm.then_inc(filled[job % SLOTS], 1)
                    if s == "win":
                        if n == NHG and j == 0:
                            pe.wait_ge(mrow_loaded, batch_no(i, u, 16, LEAD_DMA + 16))
                        c = j
                        job = jobs[(s, n, c, u)]
                        wq = WQ if c < NT - 1 else P
                        wait_freed(pe, job, i)
                        for bk in range(2):
                            pe.matmul(slot(job)[:, bk, 0:2 * WQ], identb[:],
                                      mask_win[:].rearrange("p a q -> p (a q)"), start=True, stop=True)
                            for jj in range(2):
                                h = HG * (n - NHG) + 2 * bk + jj
                                mm = pe.matmul(slot(job)[:, bk, WQ * jj:WQ * jj + wq],
                                               sk[:, h, P * c:P * (c + 1)],
                                               sq[:, h, P * c:P * c + wq],
                                               start=False, stop=True, skip_group_check=True)
                        mm.then_inc(filled[job % SLOTS], 1)
                    if s == "pv":
                        if n < NHG:
                            pe.wait_ge(pd_ready, batch_no(i, u, 8, 2 * n + 2))
                            po_job = jobs[("lin", n, 5, u)]
                            pe.wait_ge(freed[po_job % SLOTS], fill_no(po_job, i))
                        else:
                            pw_job = jobs[("win", n, NT - 1, u)]
                            pe.wait_ge(freed[pw_job % SLOTS], fill_no(pw_job, i))
                        pe.wait_ge(y_out[n % 2], batch_no(i, u, 4, LEAD + n // 2))
                        for c in range(NT):
                            parts = []
                            if n < NHG:
                                pd = Pb[:, n % 2, 512 * c:512 * (c + 1)].rearrange("p (j q) -> p j q", j=HG)
                                po = Pb[:, n % 2, 2048:5120].rearrange("p (j q) -> p j q", j=HG)
                                parts.append((P * c, P, pd))
                                if c < NT - 1:
                                    o = (0, 384, 640)[c]
                                    w = T - P * (c + 1)
                                    parts.append((P * (c + 1), w, po[:, :, o:o + w]))
                            else:
                                wq = WQ if c < NT - 1 else P
                                pw = Pb[:, n % 2, 768 * c:768 * (c + 1)].rearrange("p (j q) -> p j q", j=HG)
                                parts.append((P * c, wq, pw[:, :, 0:wq]))
                            for x_, (q0, w, src) in enumerate(parts):
                                for j in range(HG):
                                    mm = pe.matmul(pv[32 * j:32 * j + 16, n % 2, q0:q0 + w],
                                                   vaug[:, p, c, HG * (n % NHG) + j, :], src[:, j, :],
                                                   start=(c == 0 and x_ == 0), stop=(c == NT - 1),
                                                   skip_group_check=True)
                        mm.then_inc(pv_done, 1)
                    if s == "ytr":
                        job = jobs[(s, n, 0, u)]
                        wait_freed(pe, job, i)
                        for bk in range(2):
                            pe.wait_ge(y_out[bk], batch_no(i, u, 4, LEAD + n + 1))
                            for t in range(NT):
                                mm = pe.transpose(slot(job)[:, bk, P * t:P * (t + 1)],
                                                  y_sb[:, n % 2, bk, P * t:P * (t + 1)], identf[:])
                        mm.then_inc(filled[job % SLOTS], 1)
                    if s == "ycT":
                        job = jobs[(s, n, 0, u)]
                        wait_freed(pe, job, i)
                        y_job = jobs[("ytr", 3, 0, u)]
                        pe.wait_ge(freed[y_job % SLOTS], fill_no(y_job, i))
                        for kind in range(2):
                            for t in range(NT):
                                mm = pe.transpose(slot(job)[:, kind, P * t:P * (t + 1)], ycat[:, t, kind, :],
                                                  identf[:])
                        mm.then_inc(filled[job % SLOTS], 1)
                    if s == "out":
                        job = jobs[(s, n, 0, u)]
                        wait_freed(pe, job, i)
                        c_job = jobs[("ycT", 0, 0, u)]
                        pe.wait_ge(freed[c_job % SLOTS], fill_no(c_job, i))
                        for t in range(NT):
                            for kind in range(2):
                                mm = pe.matmul(slot(job)[:, 0, P * t:P * (t + 1)], ycT[:, kind, P * t:P * (t + 1)],
                                               wout[:, kind, :], start=(kind == 0), stop=(kind == 1))
                        mm.then_inc(filled[job % SLOTS], 1)
                    if s == "h2T":
                        job = jobs[(s, n, 0, u)]
                        wait_freed(pe, job, i)
                        pe.wait_ge(h2_ready, batch_no(i, u, 1, 1))
                        for t in range(NT):
                            mm = pe.transpose(slot(job)[:, 0, P * t:P * (t + 1)], h2[:, t, :], identf[:])
                        mm.then_inc(filled[job % SLOTS], 1)
                    if s == "logit":
                        job = jobs[(s, n, 0, u)]
                        wait_freed(pe, job, i)
                        t_job = jobs[("h2T", 0, 0, u)]
                        pe.wait_ge(freed[t_job % SLOTS], fill_no(t_job, i))
                        for t in range(NT):
                            mm = pe.matmul(slot(job)[:, 0, 8 * t:8 * (t + 1)], h2T[:, P * t:P * (t + 1)], gate[:],
                                           start=True, stop=True)
                        mm.then_inc(filled[job % SLOTS], 1)
                    if s == "rank":
                        job = jobs[(s, n, 0, u)]
                        wait_freed(pe, job, i)
                        pe.wait_ge(sel_ready, batch_no(i, u, 1, 1))
                        for t in range(NT):
                            for t2 in range(t + 1):
                                mm = pe.matmul(slot(job)[:, 0, E * t:E * (t + 1)], upper[:] if t2 == t else ones_bf[:],
                                               sel[:, t2, :], start=(t2 == 0), stop=(t2 == t))
                        mm.then_inc(filled[job % SLOTS], 1)
                    if s == "total":
                        job = jobs[(s, n, 0, u)]
                        wait_freed(pe, job, i)
                        for t in range(NT):
                            mm = pe.matmul(slot(job)[:, 0, 0:E], ones_bf[:], sel[:, t, :], start=(t == 0),
                                           stop=(t == NT - 1))
                        mm.then_inc(filled[job % SLOTS], 1)

            all_batches(pe, batches)

            n_kind = load_counts(pe)
            tile_lead(pe, (m_xT, 1), (m_h, F // P), (m_mm, 1), (k_xT, 1), (k_hT, 1), (k_mm[0], G), (k_mm[1], 2 * G))

            def rows_transposed(kind, i, u):
                k = i * RECS + u
                x_sem, rows, xT_sem = ((m_x, m_rows, m_xT), (k_x, k_rows, k_xT))[kind]
                n = len(x_sem)
                pe.wait_ge(x_sem[u % n], use_no(n, i, u, 64))
                pe.wait_ge(*((m_xs, tile_no(k, back=1)) if kind == 0 else (k_sig[0], tile_no(k, G, back=1))))
                for q in range(Q4):
                    mm = pe.transpose(pv[:, 0, P * q:P * (q + 1)], rows[:, u % n, q, :], identf[:])
                mm.then_inc(xT_sem, 1)

            def load_blocks(kind, k):
                return pe.value_load(tab_i[0:1, 2, kind, bass.ds(k, 1)], min_val=0, max_val=Q4)

            def for_blocks(blocks, products):
                with pe.If(blocks < 3):
                    products(2)
                with pe.If(blocks > 2):
                    with pe.If(blocks < 4):
                        products(3)
                    with pe.If(blocks > 3):
                        products(4)

            def bias_row(dst, copies, row, n):
                pe.matmul(dst.rearrange("p (q d) -> p q d", q=copies), ones_bf[0:3, :],
                          row.unsqueeze(1).to_broadcast([3, copies, n]), start=True, stop=True)

            def mlp_first(i, u):
                k = i * RECS + u
                pe.wait_ge(m_w1[u % 2], use_no(2, i, u, 32))
                pe.wait_ge(m_xs, tile_no(k))
                pe.wait_ge(m_g, tile_no(k, F // P, back=1))
                for f in range(F // P):
                    pe.matmul(ring[:, f // 2, f % 2, :], mw[u % 2][:, P * f:P * (f + 1)], mxs,
                              start=True, stop=True).then_inc(m_h, 1)

            def mlp_second(i, u):
                k = i * RECS + u
                blocks = load_blocks(0, k)
                pe.wait_ge(m_w2[u % 2], use_no(2, i, u, 32))
                pe.wait_ge(m_y, tile_no(k, back=1))
                bias_row(pv[:, 1, :], Q4, mbias[:, u % 2], D)

                def products(n):
                    for f in range(F // P):
                        pe.wait_ge(m_g, tile_no(k, F // P, f + 1))
                        for q in range(n):
                            mm = pe.matmul(pv[:, 1, P * q:P * (q + 1)], gelu[:, 4 * (u % 2) + f, P * q:P * (q + 1)],
                                           mw[u % 2][:, F + D * f:F + D * (f + 1)], start=False, stop=True,
                                           skip_group_check=True)
                    mm.then_inc(m_mm, 1)

                for_blocks(blocks, products)

            with pe.If(n_kind[0] > 0):
                rows_transposed(0, 0, 0)
                mlp_first(0, 0)
            with pe.If(n_kind[0] > 1):
                rows_transposed(0, 0, 1)
            with pe.Fori(0, TILES // RECS) as i:
                with pe.If(i * RECS < n_kind[0]):
                    for u in range(RECS):
                        k = i * RECS + u
                        with pe.If(k + 1 < n_kind[0]):
                            mlp_first(i, u + 1)
                        with pe.If(k + 2 < n_kind[0]):
                            rows_transposed(0, i, u + 2)
                        with pe.If(k < n_kind[0]):
                            mlp_second(i, u)
            pe.wait_ge(m_y, n_kind[0] + TILE_LEAD)
            pe.sem_inc(mlps_done, 1)

            def kan_first(i, u):
                k = i * RECS + u
                blocks = load_blocks(1, k)
                pe.wait_ge(k_w0[u % 2], use_no(2, i, u, 64))
                pe.wait_ge(k_zn, tile_no(k, back=1))
                for bk in range(2):
                    bias_row(ring[:, 0, bk, :], 2, kbias[u % RECS][:, 0:F2], F2)

                def products(n):
                    for g in range(G):
                        pe.wait_ge(k_bas[0], tile_no(k, G, g + 1))
                        for q in range(n):
                            mm = pe.matmul(ring[:, 0, q // 2, F2 * (q % 2):F2 * (q % 2 + 1)],
                                           basis[0][:, g, P * q:P * (q + 1)], kw[u % 2][:, F2 * g:F2 * (g + 1)],
                                           start=False, stop=True, skip_group_check=True)
                        mm.then_inc(k_mm[0], 1)

                for_blocks(blocks, products)

            def hidden_transposed(i, u):
                k = i * RECS + u
                pe.wait_ge(k_zn, tile_no(k))
                pe.wait_ge(k_sig[1], tile_no(k, 2 * G, back=1))
                for f in range(2):
                    for q in range(Q4):
                        mm = pe.transpose(ring[:, 1, f, P * q:P * (q + 1)], zn[:, q, P * f:P * (f + 1)], identf[:])
                mm.then_inc(k_hT, 1)

            def kan_second(i, u):
                k = i * RECS + u
                blocks = load_blocks(1, k)
                pe.wait_ge(k_w1[u % 2], use_no(2, i, u, 16))
                pe.wait_ge(k_y, tile_no(k, back=1))
                bias_row(pv[:, 1, :], Q4, kbias[u % RECS][:, F2:], D)

                def products(n):
                    for g in range(2 * G):
                        pe.wait_ge(k_bas[1], tile_no(k, 2 * G, g + 1))
                        for q in range(n):
                            mm = pe.matmul(pv[:, 1, P * q:P * (q + 1)], basis[1][:, g % G, P * q:P * (q + 1)],
                                           kw[u % 2][:, 2048 + D * g:2048 + D * (g + 1)], start=False, stop=True,
                                           skip_group_check=True)
                        mm.then_inc(k_mm[1], 1)

                for_blocks(blocks, products)

            with pe.If(n_kind[1] > 0):
                rows_transposed(1, 0, 0)
                kan_first(0, 0)
            with pe.If(n_kind[1] > 1):
                rows_transposed(1, 0, 1)
            with pe.Fori(0, TILES // RECS) as i:
                with pe.If(i * RECS < n_kind[1]):
                    for u in range(RECS):
                        k = i * RECS + u
                        with pe.If(k < n_kind[1]):
                            hidden_transposed(i, u)
                        with pe.If(k + 1 < n_kind[1]):
                            kan_first(i, u + 1)
                        with pe.If(k + 2 < n_kind[1]):
                            rows_transposed(1, i, u + 2)
                        with pe.If(k < n_kind[1]):
                            kan_second(i, u)


def kernel(**inputs):
    import numpy as np
    import concourse.bacc as bacc
    from concourse.bass_utils import run_bass_kernel_spmd as run

    nc = bacc.Bacc("TRN2", target_bir_lowering=False, num_devices=1)
    names = ["L0_attn_x", "L0_attn_norm_w", "L0_attn_Wq", "L0_attn_Wk", "L0_attn_Wv", "L0_attn_Wqf",
             "L0_attn_Wkf", "L0_attn_Wout", "L0_ffn_gate_W", "L0_ffn_mlp_W1", "L0_ffn_mlp_b1", "L0_ffn_mlp_W2",
             "L0_ffn_mlp_b2", "L0_ffn_kan_ln_g0", "L0_ffn_kan_ln_b0", "L0_ffn_kan_sl_W0", "L0_ffn_kan_sl_b0",
             "L0_ffn_kan_ln_g1", "L0_ffn_kan_ln_b1", "L0_ffn_kan_sl_W1", "L0_ffn_kan_sl_b1"]
    arrays, args = {}, []
    for name in names:
        a = np.ascontiguousarray(inputs[name])
        arrays[name] = a
        args.append(nc.dram_tensor(name, a.shape, mybir.dt.from_np(a.dtype), kind="ExternalInput").ap())
    arrays["grid"] = np.linspace(GRID_LO, GRID_HI, G).astype(np.float32)
    args.append(nc.dram_tensor("grid", (G,), F32, kind="ExternalInput").ap())
    args.append(nc.dram_tensor("result", (B, T, D), F32, kind="ExternalOutput").ap())
    transformer_kernel(nc, *args)
    return run(nc, [arrays], core_ids=[0]).results[0]["result"]
```
